# Optimizing a Trainium2 kernel written in Bass

```python
import numpy as np
import jax
import jax.numpy as jnp

def _softmax(x, axis=-1):
    return jax.nn.softmax(x, axis=axis)

def _gelu(x):
    return jax.nn.gelu(x, approximate=True)

def _silu(x):
    return jax.nn.silu(x)

def _sigmoid(x):
    return jax.nn.sigmoid(x)

def _layernorm(x, axis=-1, eps=1e-05):
    m = jnp.mean(x, axis=axis, keepdims=True)
    v = jnp.var(x, axis=axis, keepdims=True)
    return (x - m) / jnp.sqrt(v + eps)

def _scatter_add(tgt, idx, src, axis=0):
    return tgt.at[idx].add(src)

def _segment_sum(src, seg, n):
    return jax.ops.segment_sum(src, seg, n)
kernel_name = 'mk_decoder_preln_d2_seqx_r8_a07fb5'

def setup_inputs(seed: int=0):
    np.random.seed(seed)
    _w = jnp.asarray

    def _rec_inputs():
        import jax
        import jax.numpy as jnp
        _rk = jax.random.key(seed)
        x = -0.000125 + 0.9999 * jax.random.normal(jax.random.fold_in(_rk, 1), (1, 1024, 128), jnp.float32)
        _lenS = 1024 - jax.random.randint(jax.random.fold_in(_rk, 7), (1,), 0, max(1, 1024 // 4) + 1, jnp.int32)
        _lenS2 = 6404 - jax.random.randint(jax.random.fold_in(_rk, 8), (1,), 0, max(1, 6404 // 4) + 1, jnp.int32)
        _ctx_768P = jax.random.normal(jax.random.fold_in(_rk, 11), (1, 16, 96), jnp.float32)
        _ctx_768c = jax.random.dirichlet(jax.random.fold_in(_rk, 511), 0.3 * jnp.ones((16,), jnp.float32), (1, 6404))
        _ctx_768t = jnp.einsum('bsk,bkd->bsd', _ctx_768c, _ctx_768P)
        _ctx_768t = _ctx_768t * jax.lax.rsqrt(jnp.mean(jnp.square(_ctx_768t)) + 1e-12) * 0.953939
        ctx_768 = 0.00272024 + 0.999456 * (_ctx_768t + 0.3 * jax.random.normal(jax.random.fold_in(_rk, 611), (1, 6404, 96), jnp.float32))
        return (x, ctx_768)
    x, ctx_768 = _rec_inputs()

    def _L0_attn_setup():
        import jax, jax.numpy as jnp
        import numpy as np
        D_MODEL = 128
        N_HEADS = 16
        HEAD_DIM = D_MODEL // N_HEADS
        B, S = (4, 256)

        def _split_heads(t):
            b, s, _ = t.shape
            return t.reshape(b, s, N_HEADS, HEAD_DIM).transpose(0, 2, 1, 3)
        key = jax.random.key(seed)
        ks = jax.random.split(key, 5)
        scale = 1.0 / np.sqrt(D_MODEL)
        return {'x': jax.random.normal(ks[0], (B, S, D_MODEL), dtype=jnp.float32), 'w_q': jax.random.normal(ks[1], (D_MODEL, D_MODEL), dtype=jnp.float32) * scale, 'w_k': jax.random.normal(ks[2], (D_MODEL, D_MODEL), dtype=jnp.float32) * scale, 'w_v': jax.random.normal(ks[3], (D_MODEL, D_MODEL), dtype=jnp.float32) * scale, 'w_o': jax.random.normal(ks[4], (D_MODEL, D_MODEL), dtype=jnp.float32) * scale}
    _L0_attn_all = _L0_attn_setup()
    _L0_attn_in = {k: v for k, v in _L0_attn_all.items() if k in ('w_q', 'w_k', 'w_v', 'w_o')}
    del _L0_attn_all

    def _L0_xattn_setup():
        import jax, jax.numpy as jnp
        import numpy as np
        N_HEADS = 16
        DIM_EMBED = 128
        DIM_CROSS = 96
        DIM_HEAD = DIM_EMBED // N_HEADS
        key = jax.random.key(seed)
        ks = jax.random.split(key, 10)
        B, Sq, Sk = (8, 512, 77)
        s_e = 1.0 / np.sqrt(DIM_EMBED)
        s_c = 1.0 / np.sqrt(DIM_CROSS)
        return {'x': jax.random.normal(ks[0], (B, Sq, DIM_EMBED), jnp.float32), 'y': jax.random.normal(ks[1], (B, Sk, DIM_CROSS), jnp.float32), 'wq': jax.random.normal(ks[2], (DIM_EMBED, DIM_EMBED), jnp.float32) * s_e, 'bq': jax.random.normal(ks[3], (DIM_EMBED,), jnp.float32) * 0.01, 'wk': jax.random.normal(ks[4], (DIM_CROSS, DIM_EMBED), jnp.float32) * s_c, 'bk': jax.random.normal(ks[5], (DIM_EMBED,), jnp.float32) * 0.01, 'wv': jax.random.normal(ks[6], (DIM_CROSS, DIM_EMBED), jnp.float32) * s_c, 'bv': jax.random.normal(ks[7], (DIM_EMBED,), jnp.float32) * 0.01, 'wo': jax.random.normal(ks[8], (DIM_EMBED, DIM_EMBED), jnp.float32) * s_e, 'bo': jax.random.normal(ks[9], (DIM_EMBED,), jnp.float32) * 0.01}
    _L0_xattn_all = _L0_xattn_setup()
    _L0_xattn_in = {k: v for k, v in _L0_xattn_all.items() if k in ('wq', 'bq', 'wk', 'bk', 'wv', 'bv', 'wo', 'bo')}
    del _L0_xattn_all

    def _L0_ffn_setup():
        import jax, jax.numpy as jnp
        import numpy as np
        EMBED = 128
        D_FF = 4 * EMBED
        N_EXPERTS = 8
        TOP_K = 2
        B, S = (2, 128)
        key = jax.random.key(seed)
        ks = jax.random.split(key, 10)
        sc_d = 1.0 / np.sqrt(EMBED)
        sc_h = 1.0 / np.sqrt(D_FF)
        return {'inputs': jax.random.normal(ks[0], (B, S, EMBED), jnp.float32), 'rw1': jax.random.normal(ks[1], (EMBED, D_FF), jnp.float32) * sc_d, 'rb1': jnp.zeros((D_FF,), jnp.float32), 'rw2': jax.random.normal(ks[2], (D_FF, N_EXPERTS), jnp.float32) * sc_h, 'rb2': jnp.zeros((N_EXPERTS,), jnp.float32), 'W1': jax.random.normal(ks[3], (N_EXPERTS, EMBED, D_FF), jnp.float32) * sc_d, 'b1': jnp.zeros((N_EXPERTS, D_FF), jnp.float32), 'W2': jax.random.normal(ks[4], (N_EXPERTS, D_FF, EMBED), jnp.float32) * sc_h, 'b2': jnp.zeros((N_EXPERTS, EMBED), jnp.float32)}
    _L0_ffn_all = _L0_ffn_setup()
    _L0_ffn_in = {k: v for k, v in _L0_ffn_all.items() if k in ('rw1', 'rb1', 'rw2', 'rb2', 'W1', 'b1', 'W2', 'b2')}
    del _L0_ffn_all

    def _L1_attn_setup():
        import jax, jax.numpy as jnp
        import numpy as np
        D_MODEL = 128
        N_HEADS = 16
        D_LATENT = 32
        HEAD_DIM = D_MODEL // N_HEADS

        def apply_rope(x):
            B, T, H, D = x.shape
            inv_freq = 1.0 / 10000.0 ** (jnp.arange(0, D, 2, dtype=jnp.float32) / D)
            t = jnp.arange(T, dtype=jnp.float32)
            freqs = t[:, None] * inv_freq[None, :]
            sin_f = jnp.sin(freqs)[None, :, None, :]
            cos_f = jnp.cos(freqs)[None, :, None, :]
            x1, x2 = jnp.split(x, 2, axis=-1)
            return jnp.concatenate([x1 * cos_f - x2 * sin_f, x1 * sin_f + x2 * cos_f], axis=-1)
        key = jax.random.key(seed)
        ks = jax.random.split(key, 10)
        B, T = (4, 512)
        s = lambda fan_in: 1.0 / np.sqrt(fan_in)
        return {'x': jax.random.normal(ks[0], (B, T, D_MODEL), dtype=jnp.float32), 'Wq': jax.random.normal(ks[1], (D_MODEL, D_MODEL), dtype=jnp.float32) * s(D_MODEL), 'bq': jnp.zeros((D_MODEL,), jnp.float32), 'Wdown': jax.random.normal(ks[2], (D_MODEL, D_LATENT), dtype=jnp.float32) * s(D_MODEL), 'bdown': jnp.zeros((D_LATENT,), jnp.float32), 'Wup': jax.random.normal(ks[3], (D_LATENT, 2 * D_MODEL), dtype=jnp.float32) * s(D_LATENT), 'bup': jnp.zeros((2 * D_MODEL,), jnp.float32), 'Wout': jax.random.normal(ks[4], (D_MODEL, D_MODEL), dtype=jnp.float32) * s(D_MODEL), 'bout': jnp.zeros((D_MODEL,), jnp.float32)}
    _L1_attn_all = _L1_attn_setup()
    _L1_attn_in = {k: v for k, v in _L1_attn_all.items() if k in ('Wq', 'bq', 'Wdown', 'bdown', 'Wup', 'bup', 'Wout', 'bout')}
    del _L1_attn_all

    def _L1_xattn_setup():
        import jax, jax.numpy as jnp
        import numpy as np
        NUM_HEADS = 16
        HEAD_DIM = 64
        INNER = NUM_HEADS * HEAD_DIM
        QUERY_DIM = 128
        CONTEXT_DIM = 96
        SCALE = HEAD_DIM ** (-0.5)
        key = jax.random.key(seed)
        ks = jax.random.split(key, 6)
        B, NQ, NKV = (8, 128, 256)
        query = jax.random.normal(ks[0], (B, NQ, QUERY_DIM), dtype=jnp.float32)
        context = jax.random.normal(ks[1], (B, NKV, CONTEXT_DIM), dtype=jnp.float32)
        w_q = jax.random.normal(ks[2], (QUERY_DIM, INNER), dtype=jnp.float32) * QUERY_DIM ** (-0.5)
        w_kv = jax.random.normal(ks[3], (CONTEXT_DIM, 2 * INNER), dtype=jnp.float32) * CONTEXT_DIM ** (-0.5)
        w_out = jax.random.normal(ks[4], (INNER, QUERY_DIM), dtype=jnp.float32) * INNER ** (-0.5)
        b_out = jax.random.normal(ks[5], (QUERY_DIM,), dtype=jnp.float32) * 0.01
        return {'query': query, 'context': context, 'w_q': w_q, 'w_kv': w_kv, 'w_out': w_out, 'b_out': b_out}
    _L1_xattn_all = _L1_xattn_setup()
    _L1_xattn_in = {k: v for k, v in _L1_xattn_all.items() if k in ('w_q', 'w_kv', 'w_out', 'b_out')}
    del _L1_xattn_all

    def _L1_ffn_setup():
        import jax, jax.numpy as jnp
        import numpy as np
        B, T, D = (1, 128, 128)
        E, S, H = (8, 2, 512)
        key = jax.random.key(seed)
        kx, kg, k1, k2, k3 = jax.random.split(key, 5)
        X = jax.random.normal(kx, (B, T, D), jnp.float32)
        Wg = jax.random.normal(kg, (D, E), jnp.float32) * 0.02
        bg = jnp.zeros((E,), jnp.float32)
        W1 = jax.random.normal(k1, (E, D, H), jnp.float32) * 0.02
        W3 = jax.random.normal(k3, (E, D, H), jnp.float32) * 0.02
        W2 = jax.random.normal(k2, (E, H, D), jnp.float32) * 0.02
        return {'X': X, 'Wg': Wg, 'bg': bg, 'W1': W1, 'W2': W2, 'W3': W3}
    _L1_ffn_all = _L1_ffn_setup()
    _L1_ffn_in = {k: v for k, v in _L1_ffn_all.items() if k in ('Wg', 'bg', 'W1', 'W2', 'W3')}
    del _L1_ffn_all
    return {'x': x, 'ctx_768': ctx_768, 'L0_attn_w_q': _L0_attn_in['w_q'], 'L0_attn_w_k': _L0_attn_in['w_k'], 'L0_attn_w_v': _L0_attn_in['w_v'], 'L0_attn_w_o': _L0_attn_in['w_o'], 'L0_xattn_wq': _L0_xattn_in['wq'], 'L0_xattn_bq': _L0_xattn_in['bq'], 'L0_xattn_wk': _L0_xattn_in['wk'], 'L0_xattn_bk': _L0_xattn_in['bk'], 'L0_xattn_wv': _L0_xattn_in['wv'], 'L0_xattn_bv': _L0_xattn_in['bv'], 'L0_xattn_wo': _L0_xattn_in['wo'], 'L0_xattn_bo': _L0_xattn_in['bo'], 'L0_ffn_rw1': _L0_ffn_in['rw1'], 'L0_ffn_rb1': _L0_ffn_in['rb1'], 'L0_ffn_rw2': _L0_ffn_in['rw2'], 'L0_ffn_rb2': _L0_ffn_in['rb2'], 'L0_ffn_W1': _L0_ffn_in['W1'], 'L0_ffn_b1': _L0_ffn_in['b1'], 'L0_ffn_W2': _L0_ffn_in['W2'], 'L0_ffn_b2': _L0_ffn_in['b2'], 'L1_attn_Wq': _L1_attn_in['Wq'], 'L1_attn_bq': _L1_attn_in['bq'], 'L1_attn_Wdown': _L1_attn_in['Wdown'], 'L1_attn_bdown': _L1_attn_in['bdown'], 'L1_attn_Wup': _L1_attn_in['Wup'], 'L1_attn_bup': _L1_attn_in['bup'], 'L1_attn_Wout': _L1_attn_in['Wout'], 'L1_attn_bout': _L1_attn_in['bout'], 'L1_xattn_w_q': _L1_xattn_in['w_q'], 'L1_xattn_w_kv': _L1_xattn_in['w_kv'], 'L1_xattn_w_out': _L1_xattn_in['w_out'], 'L1_xattn_b_out': _L1_xattn_in['b_out'], 'L1_ffn_Wg': _L1_ffn_in['Wg'], 'L1_ffn_bg': _L1_ffn_in['bg'], 'L1_ffn_W1': _L1_ffn_in['W1'], 'L1_ffn_W2': _L1_ffn_in['W2'], 'L1_ffn_W3': _L1_ffn_in['W3']}

def reference(x, ctx_768, L0_attn_w_q, L0_attn_w_k, L0_attn_w_v, L0_attn_w_o, L0_xattn_wq, L0_xattn_bq, L0_xattn_wk, L0_xattn_bk, L0_xattn_wv, L0_xattn_bv, L0_xattn_wo, L0_xattn_bo, L0_ffn_rw1, L0_ffn_rb1, L0_ffn_rw2, L0_ffn_rb2, L0_ffn_W1, L0_ffn_b1, L0_ffn_W2, L0_ffn_b2, L1_attn_Wq, L1_attn_bq, L1_attn_Wdown, L1_attn_bdown, L1_attn_Wup, L1_attn_bup, L1_attn_Wout, L1_attn_bout, L1_xattn_w_q, L1_xattn_w_kv, L1_xattn_w_out, L1_xattn_b_out, L1_ffn_Wg, L1_ffn_bg, L1_ffn_W1, L1_ffn_W2, L1_ffn_W3):
    import jax
    import jax.numpy as jnp

    def _L0_attn_ref(x, w_q, w_k, w_v, w_o):
        import jax, jax.numpy as jnp
        import numpy as np
        D_MODEL = 128
        N_HEADS = 16
        HEAD_DIM = D_MODEL // N_HEADS
        B, S = (4, 256)

        def _split_heads(t):
            b, s, _ = t.shape
            return t.reshape(b, s, N_HEADS, HEAD_DIM).transpose(0, 2, 1, 3)
        b, s, _ = x.shape
        q = _split_heads(jnp.einsum('bsd,ed->bse', x, w_q))
        k = _split_heads(jnp.einsum('bsd,ed->bse', x, w_k))
        v = _split_heads(jnp.einsum('bsd,ed->bse', x, w_v))
        scores = jnp.einsum('bhqd,bhkd->bhqk', q, k) / jnp.sqrt(jnp.asarray(HEAD_DIM, dtype=x.dtype))
        causal = jnp.tril(jnp.ones((s, s), dtype=bool))
        scores = jnp.where(causal[None, None], scores, -jnp.inf)
        probs = jax.nn.softmax(scores, axis=-1)
        out = jnp.einsum('bhqk,bhkd->bhqd', probs, v)
        out = out.transpose(0, 2, 1, 3).reshape(b, s, D_MODEL)
        return jnp.einsum('bsd,ed->bse', out, w_o)

    def _L0_xattn_ref(x, y, wq, bq, wk, bk, wv, bv, wo, bo):
        import jax, jax.numpy as jnp
        import numpy as np
        N_HEADS = 16
        DIM_EMBED = 128
        DIM_CROSS = 96
        DIM_HEAD = DIM_EMBED // N_HEADS
        B, Sq, E = x.shape
        H, D = (N_HEADS, DIM_HEAD)
        q = (x @ wq + bq).reshape(B, Sq, H, D).transpose(0, 2, 1, 3)
        k = (y @ wk + bk).reshape(B, -1, H, D).transpose(0, 2, 1, 3)
        v = (y @ wv + bv).reshape(B, -1, H, D).transpose(0, 2, 1, 3)
        scores = jnp.einsum('bhqd,bhkd->bhqk', q, k) / jnp.sqrt(jnp.asarray(D, x.dtype))
        attn = jax.nn.softmax(scores, axis=-1)
        out = jnp.einsum('bhqk,bhkd->bhqd', attn, v)
        out = out.transpose(0, 2, 1, 3).reshape(B, Sq, E)
        return out @ wo + bo

    def _L0_ffn_ref(inputs, rw1, rb1, rw2, rb2, W1, b1, W2, b2):
        import jax, jax.numpy as jnp
        import numpy as np
        EMBED = 128
        D_FF = 4 * EMBED
        N_EXPERTS = 8
        TOP_K = 2
        B, S = (2, 128)
        Bb, Ss, D = inputs.shape
        T = Bb * Ss
        xf = inputs.reshape(T, D)
        score = jax.nn.relu(xf @ rw1 + rb1) @ rw2 + rb2
        _, topi = jax.lax.top_k(score, TOP_K)
        mask = jnp.zeros(score.shape, bool).at[jnp.arange(T)[:, None], topi].set(True)
        gate = jax.nn.softmax(jnp.where(mask, score, -jnp.inf), axis=-1)
        out = jnp.zeros_like(xf)
        for e in range(N_EXPERTS):
            h = jax.nn.relu(xf @ W1[e] + b1[e])
            y = h @ W2[e] + b2[e]
            out = out + gate[:, e:e + 1] * y
        return out.reshape(Bb, Ss, D)

    def _L1_attn_ref(x, Wq, bq, Wdown, bdown, Wup, bup, Wout, bout):
        import jax, jax.numpy as jnp
        import numpy as np
        D_MODEL = 128
        N_HEADS = 16
        D_LATENT = 32
        HEAD_DIM = D_MODEL // N_HEADS

        def apply_rope(x):
            B, T, H, D = x.shape
            inv_freq = 1.0 / 10000.0 ** (jnp.arange(0, D, 2, dtype=jnp.float32) / D)
            t = jnp.arange(T, dtype=jnp.float32)
            freqs = t[:, None] * inv_freq[None, :]
            sin_f = jnp.sin(freqs)[None, :, None, :]
            cos_f = jnp.cos(freqs)[None, :, None, :]
            x1, x2 = jnp.split(x, 2, axis=-1)
            return jnp.concatenate([x1 * cos_f - x2 * sin_f, x1 * sin_f + x2 * cos_f], axis=-1)
        B, T, D = x.shape
        H, Dh = (N_HEADS, HEAD_DIM)
        q = x @ Wq + bq
        kv_latent = x @ Wdown + bdown
        kv = kv_latent @ Wup + bup
        q = q.reshape(B, T, H, Dh)
        kv = kv.reshape(B, T, H, 2 * Dh)
        k, v = jnp.split(kv, 2, axis=-1)
        q = apply_rope(q)
        k = apply_rope(k)
        att = jnp.einsum('bthd,btgd->bthg', q, k) / jnp.sqrt(jnp.float32(Dh))
        att = jax.nn.softmax(att, axis=-1)
        out = jnp.einsum('bthg,btgd->bthd', att, v)
        out = out.reshape(B, T, D)
        return out @ Wout + bout

    def _L1_xattn_ref(query, context, w_q, w_kv, w_out, b_out):
        import jax, jax.numpy as jnp
        import numpy as np
        NUM_HEADS = 16
        HEAD_DIM = 64
        INNER = NUM_HEADS * HEAD_DIM
        QUERY_DIM = 128
        CONTEXT_DIM = 96
        SCALE = HEAD_DIM ** (-0.5)
        B, NQ, _ = query.shape
        NKV = context.shape[1]
        q = query @ w_q
        kv = context @ w_kv
        k, v = jnp.split(kv, 2, axis=-1)
        q = q.reshape(B, NQ, NUM_HEADS, HEAD_DIM).transpose(0, 2, 1, 3)
        k = k.reshape(B, NKV, NUM_HEADS, HEAD_DIM).transpose(0, 2, 1, 3)
        v = v.reshape(B, NKV, NUM_HEADS, HEAD_DIM).transpose(0, 2, 1, 3)
        scores = jnp.einsum('bhqd,bhkd->bhqk', q, k) * SCALE
        attn = jax.nn.softmax(scores, axis=-1)
        out = jnp.einsum('bhqk,bhkd->bhqd', attn, v)
        out = out.transpose(0, 2, 1, 3).reshape(B, NQ, INNER)
        return out @ w_out + b_out

    def _L1_ffn_ref(X, Wg, bg, W1, W2, W3):
        import jax, jax.numpy as jnp
        import numpy as np
        B, T, D = (1, 128, 128)
        E, S, H = (8, 2, 512)
        logits = jnp.einsum('btd,de->bte', X, Wg) + bg
        topv, topi = jax.lax.top_k(logits, S)
        w = jax.nn.softmax(topv, axis=-1)
        xs = X[:, :, None, :] * w[..., None]
        out = X
        for e in range(E):
            h = jax.nn.silu(jnp.einsum('btsd,dh->btsh', xs, W1[e])) * jnp.einsum('btsd,dh->btsh', xs, W3[e])
            y = jnp.einsum('btsh,hd->btsd', h, W2[e])
            mask = (topi == e)[..., None]
            out = out + jnp.where(mask, y, 0.0).sum(axis=2)
        return out
    x = x + _L0_attn_ref(_layernorm(x, axis=-1), L0_attn_w_q, L0_attn_w_k, L0_attn_w_v, L0_attn_w_o)
    x = x + _L0_xattn_ref(_layernorm(x, axis=-1), ctx_768, L0_xattn_wq, L0_xattn_bq, L0_xattn_wk, L0_xattn_bk, L0_xattn_wv, L0_xattn_bv, L0_xattn_wo, L0_xattn_bo)
    x = x + _L0_ffn_ref(_layernorm(x, axis=-1), L0_ffn_rw1, L0_ffn_rb1, L0_ffn_rw2, L0_ffn_rb2, L0_ffn_W1, L0_ffn_b1, L0_ffn_W2, L0_ffn_b2)
    x = x + _L1_attn_ref(_layernorm(x, axis=-1), L1_attn_Wq, L1_attn_bq, L1_attn_Wdown, L1_attn_bdown, L1_attn_Wup, L1_attn_bup, L1_attn_Wout, L1_attn_bout)
    x = x + _L1_xattn_ref(_layernorm(x, axis=-1), ctx_768, L1_xattn_w_q, L1_xattn_w_kv, L1_xattn_w_out, L1_xattn_b_out)
    x = x + _L1_ffn_ref(_layernorm(x, axis=-1), L1_ffn_Wg, L1_ffn_bg, L1_ffn_W1, L1_ffn_W2, L1_ffn_W3)
    return x

_drawn_inputs = setup_inputs


def setup_inputs(seed=0):
    import zlib

    import numpy as np

    out = dict(_drawn_inputs(seed))
    spreads = {'L0_ffn_rb1': (0.0, 0.1),
     'L0_ffn_rb2': (0.0, 0.1),
     'L0_ffn_b1': (0.0, 0.1),
     'L0_ffn_b2': (0.0, 0.1),
     'L1_attn_bq': (0.0, 0.346),
     'L1_attn_bdown': (0.0, 0.1),
     'L1_attn_bup': (0.0, 0.1),
     'L1_attn_bout': (0.0, 0.1),
     'L1_ffn_bg': (0.0, 0.8)}
    factors = {'L0_xattn_bq': 4.796,
     'L0_xattn_bk': 8.0,
     'L0_xattn_bv': 3.339,
     'L1_xattn_b_out': 7.069,
     'L1_ffn_Wg': 8.0,
     'L1_ffn_W1': 8.0,
     'L1_ffn_W2': 8.0,
     'L1_ffn_W3': 8.0}
    for name, (base, spread) in spreads.items():
        noise = np.random.default_rng([zlib.crc32(name.encode()), seed]).standard_normal(out[name].shape)
        drawn = base * np.exp(spread * noise) if base else spread * noise
        out[name] = jnp.asarray(drawn.astype(out[name].dtype))
    for name, factor in factors.items():
        out[name] = (out[name] * factor).astype(out[name].dtype)
    return out
```

```python
from contextlib import ExitStack

import numpy as np

import concourse.bass as bass
from concourse import mybir

F32 = mybir.dt.float32
F32R = mybir.dt.float32r
BF16 = mybir.dt.bfloat16
U32 = mybir.dt.uint32
I32 = mybir.dt.int32
ACT = mybir.ActivationFunctionType
ALU = mybir.AluOpType
AX = mybir.AxisListType.X

T = 1024
NT = 8
D = 128
S = 6404
KT = 50
NKT = 51
E = 8
F = 512


class Lane:

    def __init__(self, nc, ctx, name):
        self.nc, self.ctx, self.name = nc, ctx, name
        self.queue, self.seen, self.sems = [], {}, {}
        self.last = None

    def wait(self, *tokens):
        for tok in tokens:
            if tok is None:
                continue
            if isinstance(tok, list):
                self.wait(*tok)
                continue
            sem, n = tok
            if self.seen.get(id(sem), 0) < n:
                self.seen[id(sem)] = n
                self.queue.append(lambda e, sem=sem, n=n: e.wait_ge(sem, n))

    def count(self, kind, k):
        if kind not in self.sems:
            self.sems[kind] = [self.ctx.enter_context(self.nc.semaphore(f"{self.name}_{kind}")), 0]
        self.sems[kind][1] += k
        return tuple(self.sems[kind])

    def op(self, fn, *tokens, up=None, k=1):
        self.wait(*tokens)
        if self.name == "gp":
            self.wait(self.last)
            self.last = self.count("done", 1)
            self.queue.append(lambda e: fn(e).then_inc(self.last[0], 1))
            return self.last
        if up is None:
            self.queue.append(fn)
            return None
        tok = self.count(up, k)
        self.queue.append(lambda e: fn(e).then_inc(tok[0], k))
        return tok

    def now(self, kind):
        return tuple(self.sems[kind])

    def mm(self, out, lhsT, rhs, *tokens, start=True, stop=True, up=None, skip=False):
        return self.op(lambda e: e.matmul(out, lhsT, rhs, start=start, stop=stop, skip_group_check=skip),
                       *tokens, up=up)

    def tr(self, out, in_, ident, *tokens, up=None):
        return self.op(lambda e: e.transpose(out, in_, ident), *tokens, up=up)

    def act(self, out, in_, func, *tokens, up=None, **kw):
        return self.op(lambda e: e.activation(out, in_, func, **kw), *tokens, up=up)

    def tt(self, out, a, b, o, *tokens, up=None):
        return self.op(lambda e: e.tensor_tensor(out, a, b, o), *tokens, up=up)

    def ts(self, out, a, s1, s2, o0, o1, *tokens, up=None):
        return self.op(lambda e: e.tensor_scalar(out, a, s1, s2, o0, o1), *tokens, up=up)

    def stt(self, out, a, s, b, o0, o1, *tokens, up=None):
        return self.op(lambda e: e.scalar_tensor_tensor(out, a, s, b, o0, o1), *tokens, up=up)

    def copy(self, out, in_, *tokens, up=None):
        return self.op(lambda e: e.tensor_copy(out, in_), *tokens, up=up)

    def load_flag(self, ap, *tokens):
        self.wait(*tokens)
        box = []
        self.queue.append(lambda e: box.append(e.value_load(ap, min_val=0, max_val=1)))
        return box

    def when(self, box, body):
        def go(e):
            with e.If(box[0] == 1):
                body(e)
        self.queue.append(go)

    def dma(self, out, in_, *tokens, up):
        return self.op(lambda e: e.dma_start(out, in_), *tokens, up=up, k=16)


class Relay:

    def __init__(self, outer, inner, dma):
        self.sem = dict(outer=outer, inner=inner)
        self.dma = dma
        self.stages = dict(outer=[], inner=[])

    def stage(self, loop, lane, *fns):
        self.stages[loop].append((lane, fns))

    def run(self, e, lane, start, load):
        so, si = self.sem["outer"], self.sem["inner"]
        no, ni = len(self.stages["outer"]), len(self.stages["inner"])
        start(e)
        if lane == "dv":
            e.sem_inc(so, 1)
            e.sem_inc(si, 1)
        with e.Fori(0, 16) as h:
            if lane == "sp":
                e.wait_ge(si, h * (8 * ni) + 1)
                load(e, h)
            base = h * no + 1
            for k, (who, fns) in enumerate(self.stages["outer"]):
                if who == lane:
                    e.wait_ge(so, base + k)
                    if k == 0:
                        e.wait_ge(self.dma, (h + 1) * 16)
                    for fn in fns[:-1]:
                        fn(e, h, None)
                    fns[-1](e, h, None).then_inc(so, 1)
            if any(who == lane for who, _ in self.stages["inner"]):
                with e.Fori(0, 8) as q:
                    base = (h * 8 + q) * ni + 1
                    for k, (who, fns) in enumerate(self.stages["inner"]):
                        if who == lane:
                            e.wait_ge(si, base + k)
                            if k == 0:
                                e.wait_ge(so, (h + 1) * no + 1)
                            for fn in fns[:-1]:
                                fn(e, h, q)
                            fns[-1](e, h, q).then_inc(si, 1)
        e.wait_ge(si, 16 * 8 * ni + 1)


class Ring:

    def __init__(self, aps):
        self.aps, self.freed, self.i = aps, [None] * len(aps), 0

    def take(self):
        s = self.i % len(self.aps)
        self.i += 1
        return s, self.aps[s], self.freed[s]

    def free(self, s, tok):
        self.freed[s] = tok


CST = {}
_c = 0
for _n, _w in [("id", 128), ("qs", 1), ("qb", 1), ("ks", 1), ("kb", 1), ("k1", 1), ("mh", 8),
               ("cos", NT * 4), ("sin", NT * 4), ("iota", 8), ("one", 1),
               ("sel4", 4), ("sel2", 32)]:
    CST[_n] = (_c, _c + _w)
    _c += _w
NCST = _c
WA = dict(q=(0, 512), k=(512, 1024), v=(1024, 1152), o=(1152, 1280))
NWA = 1280
WX = dict(q=(0, 512), k=(512, 1024), v=(1024, 1168), o=(1168, 1296), bq=(1296, 1300), bo=(1300, 1428))
NWX = 1428
WF0 = dict(rw1=(0, 512), rb1=(512, 516), rw2=(516, 548), rb2=(548, 556), b1=(556, 588), b2=(588, 716))
NWF0 = 716
WB = dict(q=(0, 128), down=(128, 160), up=(160, 416), out=(416, 544), bq=(544, 672), bup=(672, 928), bout=(928, 1056),
          bdown=(1056, 1057))
NWB = 1057
NKV = 2048
WY = dict(q=(0, 1024), kv=(1024, 3072), out=(3072, 4096), b=(4096, 4224))
NWY = 4224
WF1 = dict(g=(0, 8), bg=(8, 16), sel=(16, 1040))
NWF1 = 1040


def program(nc, out, x, ctx_in, cst, wa, wx, wf0, f0w1, f0w2, wb, wy, wf1, f1w1, f1w3, f1w2, ga, gx, gy, gc, limit=60.0):
    ctx = ExitStack()
    with ctx:
        pe, ac, dv, gp, sp = [Lane(nc, ctx, n) for n in ("pe", "ac", "dv", "gp", "sp")]
        PS = ctx.enter_context(nc.psum_tensor("PS", [128, 4096], F32))
        ring = Ring([PS[:, 1024 * i:1024 * i + 1024] for i in range(3)])
        O = PS[:, 3072:4096]

        BASE = 16512

        class Region:

            def __init__(self, at):
                self.at = at

            def __call__(self, name, shape, dt=F32):
                size = (2 if dt == BF16 else 4) * int(np.prod(shape[1:]))
                t = nc.alloc_sbuf_tensor_at(name, shape, dt, offset=BASE + self.at)
                self.at += (size + 31) // 32 * 32
                assert BASE + self.at <= 229344, (name, self.at)
                return t

        glob = Region(0)
        X = glob("X", [128, NT, D])
        xn = glob("xn", [128, NT, D])
        xT = glob("xT", [128, T])
        C = glob("C", [128, NCST])
        st = glob("st", [128, NT, 6])
        mv = glob("mv", [128, NT, 2])
        ve = glob("ve", [128, NT])
        rstd = glob("rstd", [128, NT])
        rs = glob("rs", [128, 32])
        On = glob("On", [128, NT, D])
        Osb = glob("Osb", [128, T])
        flags = glob("flags", [1, 8], I32)
        fm = glob("fm", [1, 8])
        nm = glob("nm", [128, 32])
        nr = glob("nr", [32, 1])
        fl = glob("fl", [1, 32])
        mq = glob("mq", [128, 4])
        mk = glob("mk", [128, 4, 7])
        mkr = glob("mkr", [128, 4])
        ctxT = glob("ctxT", [97, S])

        def c(name):
            return C[:, CST[name][0]:CST[name][1]]

        ident = c("id")

        xf = X[:].rearrange("p i d -> p (i d)")
        x_in = sp.dma(X[:], x.rearrange("a (i p) d -> p (a i) d", p=128), up="x")
        c_in = sp.dma(C[:], cst, up="cst")

        def layernorm(ready, xT_free):
            dv.wait(ready, xT_free)
            for i in range(NT):
                t = dv.op(lambda e, i=i: e.bn_stats(st[:, i, :], X[:, i, :]), up="st")
            dv.wait(t)
            for i in range(NT):
                t = dv.op(lambda e, i=i: e.bn_aggr(mv[:, i, :], st[:, i, :]), up="ag")
            t = dv.ts(ve[:], mv[:, :, 1], 1e-5, None, ALU.add, ALU.bypass, t, up="ve")
            t = gp.tt(rstd[:], ve[:], c("mh"), ALU.pow, t, c_in, up="rstd")
            dv.wait(t)
            for i in range(NT):
                n = dv.ts(xn[:, i, :], X[:, i, :], mv[:, i, 0:1], rstd[:, i:i + 1], ALU.subtract, ALU.mult, up="xn")
                if i == 3:
                    half = n
            s, ps, fr = ring.take()
            toks = []
            for h, tok in enumerate((half, n)):
                for i in range(4 * h, 4 * h + 4):
                    t = pe.tr(ps[:, 128 * i:128 * i + 128], xn[:, i, :], ident, tok, fr, c_in, up="xT")
                toks.append(ac.act(xT[:, 512 * h:512 * h + 512], ps[:, 512 * h:512 * h + 512], ACT.Copy, t, xT_free, up="xT"))
            ring.free(s, toks[-1])
            return n, toks

        def split_tile(dst, tmp, src, sgn, sel, bias, tok, dst_free, up):
            t = dv.ts(tmp, src, sgn, bias, ALU.mult, ALU.add, tok, tmp_free[0], up="tmp")
            parts = dst if isinstance(dst, list) else [(slice(0, 128), dst)]
            for rows, d in parts:
                r = dv.stt(d, src[rows, :], sel[rows, :], tmp[rows, :].bitcast(F32), ALU.mult, ALU.add, t, dst_free, up=up)
            tmp_free[0] = r
            return r

        def q_parts(g):
            return [(slice(32 * j, 32 * j + 32), Qz[g % 2][32 * j:32 * j + 32, j, :]) for j in range(4)]

        tmp_free = [None]
        mid = Region(glob.at)
        WXs = mid("WXs", [128, NWX])
        Region_Kx = mid.at
        Kx = mid("Kx", [128, S], F32R)
        V0 = mid("V0", [128, NKT, 144])
        Qz = [mid(f"Qz{i}", [128, 4, T], F32R) for i in range(2)]
        tmp = mid("tmp", [128, T], F32R)
        Qb = mid("Qb", [128, T])
        NP = 8
        P = [mid(f"P{i}", [128, T]) for i in range(NP)]
        first = Region(mid.at)
        WAs = first("WAs", [128, NWA])
        Va = first("Va", [128, NT, 16, 9])
        nq = first("nq", [128, 128])
        Ka = [first(f"Ka{i}", [128, T], F32R) for i in range(2)]
        CN = 10
        cn = [first(f"cn{i}", [128, CN, 96]) for i in range(2)]
        ct = first("ct", [4, 96])
        wa_in = sp.dma(WAs[:], wa, up="wa")
        wx_in = sp.dma(WXs[:], wx, up="wx")
        va1 = gp.op(lambda e: e.memset(Va[:], 1.0), up="va")
        c1 = gp.op(lambda e: e.memset(ctxT[96:97, :], 1.0), va1, up="c1")
        o0 = dv.op(lambda e: e.memset(O, 0.0), up="o0")
        for q in Qz:
            qz0 = gp.op(lambda e, q=q: e.memset(q[:].bitcast(F32), 0.0))

        def w(a, g, n=128):
            return WAs[:, WA[a][0] + n * g:WA[a][0] + n * (g + 1)]

        def wxs(a, g, n=128, rows=128):
            return WXs[0:rows, WX[a][0] + n * g:WX[a][0] + n * (g + 1)]

        cmain = ctx_in[0, 0:128 * KT, :].rearrange("(p t) d -> p t d", t=KT)
        ct_in = sp.dma(ct[:], ctx_in[0, 128 * KT:S, :], up="ct")
        cn_free = [None, None]
        cn_in = {}

        def load_ctx(b):
            cn_in[b] = sp.dma(cn[b % 2][:], cmain[:, CN * b:CN * (b + 1), :], cn_free[b % 2], up=f"cn{b}")

        load_ctx(0)
        load_ctx(1)
        ctx_t = {}

        def ctx_task(m):
            def go():
                s, ps, fr = ring.take()
                for i in range(8):
                    kt = 8 * m + i
                    if kt > KT:
                        break
                    b = kt // CN
                    if kt == KT:
                        t = pe.tr(ps[0:96, 128 * i:128 * i + 4], ct[:], ident[0:4, 0:4], ct_in, fr, up="ctxT")
                    else:
                        t = pe.tr(ps[0:96, 128 * i:128 * i + 128], cn[b % 2][:, kt % CN, :], ident, cn_in[b], fr, up="ctxT")
                        if kt % CN == CN - 1:
                            cn_free[b % 2] = t
                            if b + 2 < KT // CN:
                                load_ctx(b + 2)
                n = min(1024, S - 1024 * m)
                r = dv.copy(ctxT[0:96, 1024 * m:1024 * m + n], ps[0:96, 0:n], t, up="ctxT")
                ctx_t[m] = r
                ring.free(s, r)
            return go

        v0_t = {}

        def v0_task(m):
            def go():
                s, ps, fr = ring.take()
                n = min(6, NKT - 6 * m)
                for i in range(n):
                    kt = 6 * m + i
                    k = 128 if kt < KT else 4
                    o = 512 * (i // 3) + 144 * (i % 3)
                    t = pe.mm(ps[0:k, o:o + 144], ctxT[0:97, 128 * kt:128 * kt + k], wxs("v", 0, 144, 97), fr, ctx_t[kt // 8],
                              c1, wx_in, up="v0")
                if n == 6:
                    r = dv.copy(V0[:, 6 * m:6 * m + 6, :].rearrange("p (a b) c -> p a (b c)", a=2),
                                ps.rearrange("p (a b) -> p a b", a=2)[:, :, 0:432], t, up="v0")
                else:
                    dv.copy(V0[:, 6 * m:6 * m + 2, :].rearrange("p b c -> p (b c)"), ps[:, 0:288], t)
                    r = dv.copy(V0[0:4, 6 * m + 2, :], ps[0:4, 288:432], up="v0")
                v0_t[m] = r
                ring.free(s, r)
            return go

        def chunks(n):
            return [(a, min(a + 512, n)) for a in range(0, n, 512)]

        def k_task(key, m, dst, wk, rows, src, src_t, bias, dst_free, done):
            def go():
                s, ps, fr = ring.take()
                n = min(1024, src.shape[1] - 1024 * m)
                for a, b in chunks(n):
                    t = pe.mm(ps[:, a:b], wk, src[0:rows, 1024 * m + a:1024 * m + b], fr, src_t(m), up="kproj")
                if key != "a":
                    dv.op(lambda e: e.tensor_reduce(mk[:, key, m:m + 1], ps[:, 0:n], AX, ALU.max, apply_absolute_value=True), t,
                          up="mk")
                r = split_tile(dst[:, 1024 * m:1024 * m + n], tmp[:, 0:n], ps[:, 0:n], c("ks"), c("kb"), bias, t, dst_free(),
                               "kt")
                if key == "a":
                    done[len(done)] = r
                else:
                    done[key, m] = r
                ring.free(s, r)
            return go

        SC = float(1 / np.sqrt(8))

        def general(name, region, hd, src, rows, nkeys, weights, W, scale, causal, out, final, flag, flag_t, ready):
            nt = -(-nkeys // 128)
            g = Region(region)
            Wg = g(name + "W", [128, W])
            QT = g(name + "QT", [hd, T])
            Qc = g(name + "Qc", [hd, 128])
            KT_ = g(name + "KT", [hd, nkeys])
            Vg = g(name + "V", [128, nt, hd])
            Sg = g(name + "S", [128, nkeys])
            PT = g(name + "PT", [128, 512])
            sc4 = g(name + "s", [128, 4])
            if causal:
                io = g(name + "io", [128, T + NT])
                msk = g(name + "mk", [128, T])
            if final:
                Oc = g(name + "Oc", [128, hd])
                OT = g(name + "OT", [hd, 128])
            outer, inner, gdma, cdma = [ctx.enter_context(nc.semaphore(f"{name}_{n}"))
                                        for n in ("outer", "inner", "dma", "const")]
            r = Relay(outer, inner, gdma)
            P0, P1 = PS[:, 0:512], PS[:, 512:1024]
            big = PS[:, 1024:3072]

            def mm(o, a, b, st=True, sp_=True):
                return lambda e, h, q: e.matmul(o, a, b, start=st, stop=sp_)

            def cp(o, a):
                return lambda e, h, q: e.tensor_copy(o, a)

            r.stage("outer", "pe", *[mm(PS[0:hd, a:a + 512], Wg[:, 0:hd], xT[:, a:a + 512]) for a in (0, 512)])
            r.stage("outer", "dv", lambda e, h, q: e.tensor_scalar(QT[:], PS[0:hd, 0:1024], Wg[0:hd, 3 * hd:3 * hd + 1], None,
                                                                    ALU.add, ALU.bypass))
            for a in range(0, nkeys, 2048):
                n = min(2048, nkeys - a)
                r.stage("outer", "pe", *[mm(big[0:hd, b:min(b + 512, n)], Wg[0:rows, hd:2 * hd],
                                            src[0:rows, a + b:a + min(b + 512, n)]) for b in range(0, n, 512)])
                r.stage("outer", "dv", cp(KT_[:, a:a + n], big[0:hd, 0:n]))
            per = 2048 // hd
            for a in range(0, nt, per):
                ts_ = range(a, min(a + per, nt))
                r.stage("outer", "pe", *[mm(big[0:min(128, nkeys - 128 * t), hd * (t - a):hd * (t - a) + hd],
                                            src[0:rows, 128 * t:min(128 * t + 128, nkeys)], Wg[0:rows, 2 * hd:3 * hd])
                                         for t in ts_])
                full = [t for t in ts_ if 128 * t + 128 <= nkeys]
                r.stage("outer", "dv", cp(Vg[:, a:a + len(full), :].rearrange("p t d -> p (t d)"), big[:, 0:hd * len(full)]))
                if len(full) < len(ts_):
                    t = ts_[-1]
                    r.stage("outer", "dv", cp(Vg[0:nkeys - 128 * t, t, :],
                                              big[0:nkeys - 128 * t, hd * (t - a):hd * (t - a) + hd]))
            r.stage("inner", "dv", lambda e, h, q: e.tensor_copy(Qc[:], QT[:, bass.ds(q * 128, 128)]))
            for a in range(0, nkeys, 2048):
                n = min(2048, nkeys - a)
                r.stage("inner", "pe", *[mm(big[:, b:min(b + 512, n)], Qc[:], KT_[:, a + b:a + min(b + 512, n)])
                                         for b in range(0, n, 512)])
                r.stage("inner", "dv", cp(Sg[:, a:a + n], big[:, 0:n]))
            if causal:
                r.stage("inner", "dv", lambda e, h, q: e.tensor_copy(sc4[:, 3:4], io[:, bass.ds(q + T, 1)]))
                r.stage("inner", "dv", lambda e, h, q: e.tensor_scalar(msk[:], io[:, 0:T], sc4[:, 3:4], -3e38, ALU.is_gt,
                                                                        ALU.mult))
                r.stage("inner", "dv", lambda e, h, q: e.tensor_tensor(Sg[:], Sg[:], msk[:], ALU.add))
            r.stage("inner", "dv", lambda e, h, q: e.tensor_reduce(sc4[:, 0:1], Sg[:], AX, ALU.max))
            r.stage("inner", "dv", lambda e, h, q: e.tensor_scalar(sc4[:, 1:2], sc4[:, 0:1], -scale, None, ALU.mult,
                                                                    ALU.bypass))
            r.stage("inner", "ac", lambda e, h, q: e.activation(Sg[:], Sg[:], ACT.Exp, bias=sc4[:, 1:2], scale=scale,
                                                                 accum_out=sc4[:, 2:3]))
            for a in range(0, nt, 4):
                ts_ = range(a, min(a + 4, nt))
                ws = [min(128, nkeys - 128 * t) for t in ts_]
                r.stage("inner", "pe", *[(lambda e, h, q, t=t, w=w, a=a: e.transpose(
                    P0[0:w, 128 * (t - a):128 * (t - a) + 128], Sg[:, 128 * t:128 * t + w], ident))
                    for t, w in zip(ts_, ws)])
                nf = sum(w == 128 for w in ws)
                if nf:
                    r.stage("inner", "dv", cp(PT[:, 0:128 * nf], P0[:, 0:128 * nf]))
                if nf < len(ws):
                    r.stage("inner", "dv", cp(PT[0:ws[-1], 128 * nf:128 * nf + 128], P0[0:ws[-1], 128 * nf:128 * nf + 128]))
                r.stage("inner", "pe", *[mm(P1[:, 0:hd], PT[0:w, 128 * (t - a):128 * (t - a) + 128], Vg[0:w, t, :], t == 0,
                                            t == nt - 1) for t, w in zip(ts_, ws)])
            r.stage("inner", "dv", lambda e, h, q: e.reciprocal(sc4[:, 0:1], sc4[:, 2:3]))
            if not final:
                r.stage("inner", "dv", lambda e, h, q: e.tensor_scalar(
                    out[:, bass.ds(q * 16 + h, 1), :], P1[:, 0:hd].unsqueeze(1), sc4[:, 0:1], None, ALU.mult, ALU.bypass))
            else:
                r.stage("inner", "dv", lambda e, h, q: e.tensor_scalar(Oc[:], P1[:, 0:hd], sc4[:, 0:1], None, ALU.mult,
                                                                        ALU.bypass))
                r.stage("inner", "pe", mm(P0[0:hd, 0:128], Oc[:], ident))
                r.stage("inner", "dv", cp(OT[:], P0[0:hd, 0:128]))
                r.stage("inner", "pe", mm(P1[:, 0:128], OT[:], Wg[0:hd, 3 * hd + 1:3 * hd + 129]))
                r.stage("inner", "dv", lambda e, h, q: e.tensor_tensor(out[:, bass.ds(q, 1), :], out[:, bass.ds(q, 1), :],
                                                                        P1[:, 0:128].unsqueeze(1), ALU.add))

            def start(name_):
                def go(e):
                    for sem, n in ready:
                        e.wait_ge(sem, n)
                    if name_ == "sp" and causal:
                        e.dma_start(io[:], gc).then_inc(cdma, 16)
                    if name_ == "dv" and causal:
                        e.wait_ge(cdma, 16)
                    if name_ == "dv" and final:
                        e.memset(out, 0.0).then_inc(cdma, 1)
                        e.wait_ge(cdma, 1)
                return go

            def load(e, h):
                e.dma_start(Wg[:], weights[bass.ds(h, 1)].rearrange("a p f -> (a p) f")).then_inc(gdma, 16)

            for lane in (pe, ac, dv, sp):
                box = lane.load_flag(flag, flag_t)
                lane.when(box, lambda e, lane=lane: r.run(e, lane.name, start(lane.name), load))

        def flat(*toks):
            out = []
            for t in toks:
                if isinstance(t, list):
                    out += flat(*t)
                elif t is not None:
                    out.append(t)
            return out
        osb_free = [None, None]
        on_t = [None]
        p_free = [None] * NP
        unit = [0]
        o_free = [o0]
        q_free = [None, None]

        def attend8(nkt, width, K, Vt, v_tok, q_t, k_tok, tasks, k_used, causal):
            pv_q = []

            def emit_pv(final=False):
                while pv_q and (final or unit[0] >= pv_q[0][0]):
                    pv_q.pop(0)[1]()

            for g in range(4):
                for kt in range(nkt):
                    kw = width(kt)
                    lo = 128 * kt if causal else 0
                    tile = []
                    todo = list(tasks.get((g, kt), []))
                    for j in range(4):
                        s, ps, fr = ring.take()
                        for a, b in ((lo, 512), (max(lo, 512), 1024)):
                            if a < b:
                                t = pe.mm(ps[0:kw, a:b], K(g)[:, 128 * kt:128 * kt + kw], Qz[g % 2][:, j, a:b], fr,
                                          q_t[g], k_tok(g, kt), up="qk")
                        pb = unit[0] % NP
                        unit[0] += 1
                        t2 = ac.act(P[pb][0:kw, lo:T], ps[0:kw, lo:T], ACT.Exp, t, p_free[pb], scale=SC, up="exp")
                        ring.free(s, t2)
                        if causal:
                            t2 = gp.op(lambda e, pb=pb, lo=lo: e.affine_select(
                                out=P[pb][:, lo:lo + 128], in_=P[pb][:, lo:lo + 128], compare_op=ALU.is_ge, fill=0.0,
                                base=0, pattern=[[1, 128]], channel_multiplier=-1), t2, up="mask")
                        tile.append((pb, t2))
                        emit_pv()
                        if j == 3:
                            k_used[g, kt] = t
                            q_free[g % 2] = t
                        if todo and j >= 4 - len(todo):
                            todo.pop(0)()

                    def pv(h, g=g, kt=kt, kw=kw, lo=lo, tile=tile):
                        a, b = max(lo, 512 * h), 512 * h + 512
                        t = None
                        if a < b:
                            last = (b // 128 if causal else nkt) - 1
                            for j, (pb, tk) in enumerate(tile):
                                t = pe.mm(O[32 * j:32 * j + 9, a:b], Vt(kt, 4 * g + j), P[pb][0:kw, a:b], tk, o_free[0],
                                          v_tok(kt), start=kt == 0, stop=kt == last, skip=True, up="pv")
                        if h == 1:
                            for pb, _ in tile:
                                p_free[pb] = t
                        if h == 1 and kt == nkt - 1:
                            finish_group(g, t)

                    pv_q.append((unit[0] + LAG, lambda pv=pv: pv(0)))
                    pv_q.append((unit[0] + LAG + 2, lambda pv=pv: pv(1)))
            emit_pv(True)

        LAG = 2

        def finish_group(g, pv_t):
            ob = Osb
            t = ac.act(ob[:], O, ACT.Copy, pv_t, osb_free[0], up="osb")
            o_free[0] = t
            s, ps, fr = ring.take()
            for i in range(NT):
                t = pe.tr(ps[:, 128 * i:128 * i + 128], ob[:, 128 * i:128 * i + 128], ident, t, fr, up="otr")
            osb_free[0] = t
            v = ps.rearrange("p (i j c) -> p i j c", i=NT, j=4)
            r3 = rs[:].rearrange("p (i j) -> p i j", j=4)
            r = dv.op(lambda e: e.reciprocal(r3, v[:, :, :, 8]), t, on_t[0], up="rs")
            n = dv.tt(On[:].rearrange("p i (h c) -> p i h c", c=8)[:, :, 4 * g:4 * g + 4, :], v[:, :, :, 0:8],
                      r3.unsqueeze(3).to_broadcast([128, NT, 4, 8]), ALU.mult, r, up="on")
            on_t[0] = n
            ring.free(s, n)

        def out_proj(wo, w_in, extra_free):
            s, ps, fr = ring.take()
            for i in range(NT):
                t = pe.tr(ps[:, 128 * i:128 * i + 128], On[:, i, :], ident, fr, on_t[0], up="onT")
            t = ac.act(Osb[:], ps, ACT.Copy, t, osb_free[0], up="ont")
            ring.free(s, t)
            s, ps, fr = ring.take()
            for i in range(NT):
                t2 = pe.mm(ps[:, 128 * i:128 * i + 128], Osb[:, 128 * i:128 * i + 128], wo, fr, t, w_in, up="oproj")
            osb_free[0] = t2
            on_t[0] = t2
            r = dv.tt(xf, xf, ps, ALU.add, t2, extra_free, up="res")
            ring.free(s, r)
            return r

        def compare(k, src, scale, square, tok):
            bar = (limit / scale) * (abs(limit) / scale if square else 1)
            t = dv.op(lambda e: e.tensor_reduce(fm[:, k:k + 1], src, AX, ALU.max), tok, up="fm")
            return dv.ts(flags[0:1, k:k + 1], fm[:, k:k + 1], bar, None, ALU.is_gt, ALU.bypass, t, up="flag")

        xn_t, xT_t = layernorm(x_in, None)
        s, ps, fr = ring.take()
        for i in range(NT):
            t = pe.mm(ps[:, 128 * i:128 * i + 128], xT[:, 128 * i:128 * i + 128], w("v", 0), fr, xT_t, wa_in, up="va")
        va_t = dv.copy(Va[:].rearrange("p i h c -> p (i h) c")[:, :, 0:8], ps.rearrange("p (n c) -> p n c", c=8), t, va1,
                       up="va")
        ring.free(s, va_t)
        ka, qa_t, ka_used, kx, kx_used = {}, {}, {}, {}, {}

        def qa_task(g):
            def go():
                s, ps, fr = ring.take()
                for a, b in chunks(T):
                    t = pe.mm(ps[:, a:b], w("q", g), xT[:, a:b], fr, xT_t, wa_in, up="qproj")
                r = split_tile(q_parts(g), tmp[:], ps, c("qs"), c("qb"), 0.0, t, [q_free[g % 2], qz0], "qt")
                qa_t[g] = r
                ring.free(s, r)
            return go

        def ka_task(g):
            return k_task("a", 0, Ka[g % 2], w("k", g), 128, xT, lambda m: xT_t + [wa_in], c("k1"),
                          lambda: ka_used.get((g - 2, NT - 1)), ka)

        def kx_task(g, m):
            return k_task(g, m, Kx, wxs("k", g, 128, 97), 97, ctxT, lambda m: [ctx_t[m], c1, wx_in], 0.0,
                          lambda: kx_used.get((g - 1, min(8 * m + 7, NKT - 1))), kx)

        def spread(tasks, slots, into):
            for i, task in enumerate(tasks):
                into.setdefault(slots[i * len(slots) // len(tasks)], []).append(task)

        nm_t = {}

        def norm_task(k, name):
            def go():
                s, ps, fr = ring.take()
                wv_ = w(name, 0, 512).rearrange("p (h c) -> p h c", c=32)[:, :, 0:8]
                for i in range(NT):
                    t = pe.mm(ps[:, 128 * i:128 * i + 128], xT[:, 128 * i:128 * i + 128], wv_, fr, xT_t, wa_in, up="nm")
                t = ac.act(Osb[:], ps, ACT.Square, t, osb_free[0], up="nm")
                ring.free(s, t)
                t = dv.op(lambda e: e.tensor_reduce(nq[:], Osb[:].rearrange("p (n c) -> p n c", c=8), AX, ALU.add), t,
                          nm_t.get(0), up="nm")
                osb_free[0] = t
                nm_t[k] = dv.op(lambda e: e.tensor_reduce(nm[:, 16 * k:16 * k + 16], nq[:].rearrange("p (i h) -> p h i", h=16),
                                                          AX, ALU.max), t, up="nm")
            return go

        def norm_flag():
            s, ps, fr = ring.take()
            t = pe.tr(ps[0:32, 0:128], nm[:], ident, nm_t[1], fr, up="nm")
            t = dv.op(lambda e: e.tensor_reduce(nr[:], ps[0:32, 0:128], AX, ALU.max), t, up="nm")
            t = pe.tr(ps[0:1, 512:544], nr[:], ident[0:32, 0:32], t, up="nm")
            t = dv.copy(fl[:], ps[0:1, 512:544], t, up="nm")
            ring.free(s, t)
            t = dv.tt(fl[:, 0:16], fl[:, 0:16], fl[:, 16:32], ALU.mult, t, up="nm")
            fl_t[0] = compare(0, fl[:, 0:16], SC, True, t)

        fl_t = {}

        def a0_tasks():
            tasks = {}
            for g in range(3):
                tasks[g, 3] = [qa_task(g + 1)]
                tasks[g, 5] = [ka_task(g + 1)]
            rest = [ctx_task(m) for m in range(7)] + [v0_task(m) for m in range(9)] + [kx_task(0, m) for m in range(7)]
            rest = [norm_task(0, "q"), norm_task(1, "k"), norm_flag] + rest
            spread(rest, [(g, kt) for g in range(4) for kt in (0, 1, 2, 4, 6, 7)], tasks)
            return tasks

        qa_task(0)()
        ka_task(0)()
        attend8(NT, lambda kt: 128, lambda g: Ka[g % 2], lambda kt, h: Va[:, kt, h, :], lambda kt: va_t, qa_t,
                lambda g, kt: ka[g], a0_tasks(), ka_used, True)
        general("ga", mid.at - 4096 * NP, 8, xT, 128, T, ga, 25, SC, True, On[:].rearrange("p i (h c) -> p (i h) c", c=8),
                False, flags[0:1, 0:1], fl_t[0], flat(ring.freed, on_t, p_free, o_free))
        x_t = a0_end = out_proj(w("o", 0), wa_in, xn_t)

        xn_t, xT_t = layernorm(x_t, None)
        bo_t = gp.tt(X[:], X[:], WXs[:, WX["bo"][0]:WX["bo"][1]].unsqueeze(1).to_broadcast([128, NT, D]), ALU.add,
                     xn_t, wx_in, up="bo")
        qx_t = {}

        def qx_task(g):
            def go():
                s, ps, fr = ring.take()
                for a, b in chunks(T):
                    t = pe.mm(ps[:, a:b], wxs("q", g), xT[:, a:b], fr, xT_t, wx_in, up="qproj")
                y = dv.ts(Qb[:], ps, wxs("bq", g, 1), None, ALU.add, ALU.bypass, t, tmp_free[0], up="qb")
                ring.free(s, y)
                dv.op(lambda e: e.tensor_reduce(mq[:, g:g + 1], Qb[:], AX, ALU.max, apply_absolute_value=True), y, up="mq")
                qx_t[g] = split_tile(q_parts(g), tmp[:], Qb[:], c("qs"), c("qb"), 0.0, y, q_free[g % 2], "qt")
            return go

        def width(kt):
            return 128 if kt < KT else 4

        tasks = {}
        for g in range(3):
            for m in range(6):
                tasks[g, 8 * m + 9] = [kx_task(g + 1, m)]
            tasks[g + 1, 1] = [kx_task(g + 1, 6)]
            tasks[g, 44] = [qx_task(g + 1)]

        def dim_flag():
            s, ps, fr = ring.take()
            t = dv.op(lambda e: e.tensor_reduce(mkr[:], mk[:], AX, ALU.max), dv.now("mk"), up="mkr")
            t = dv.tt(mkr[:], mkr[:], mq[:], ALU.mult, t, dv.now("mq"), up="mkr")
            for g in range(4):
                t2 = pe.mm(ps[0:1, 4 * g:4 * g + 4], mkr[:, g:g + 1], c("sel4"), t, fr, up="fl")
            fl_t[1] = compare(1, ps[0:1, 0:16], SC, False, t2)
            ring.free(s, fl_t[1])

        tasks[3, 10] = [dim_flag]
        qx_task(0)()
        attend8(NKT, width, lambda g: Kx, lambda kt, h: V0[0:width(kt), kt, 9 * h:9 * h + 9],
                lambda kt: v0_t[kt // 6], qx_t, lambda g, kt: kx[g, kt // 8], tasks, kx_used, False)
        general("gx", Region_Kx, 8, ctxT, 97, S, gx, 25, SC, False, On[:].rearrange("p i (h c) -> p (i h) c", c=8),
                False, flags[0:1, 1:2], fl_t[1], flat(ring.freed, on_t, p_free, o_free))
        x_t = out_proj(wxs("o", 0), wx_in, bo_t)

        def gates(G, ps, bias, tok, w_in, gfree, g):
            sc, m8, ix, ixf, d, p1, eq = g
            t = dv.tt(sc[:], ps.rearrange("p (i e) -> p i e", e=8), bias.unsqueeze(1).to_broadcast([128, NT, 8]), ALU.add,
                      tok, w_in, up="sc")
            r = t
            for i in range(NT):
                t = dv.op(lambda e, i=i: e.max(m8[:, i, :], sc[:, i, :]), t, up="m8")
            dv.wait(t)
            for i in range(NT):
                t2 = dv.op(lambda e, i=i: e.max_index(ix[:, i, :], m8[:, i, :], sc[:, i, :]), up="ix")
            t2 = dv.copy(ixf[:], ix[:, :, 0:2], t2, up="ixf")
            t = dv.tt(d[:], m8[:, :, 1], m8[:, :, 0], ALU.subtract, up="gd")
            t = ac.act(d[:], d[:], ACT.Exp, t, up="ge")
            t = dv.ts(p1[:, 0, :], d[:], 1.0, None, ALU.add, ALU.bypass, t, up="g1")
            t = dv.op(lambda e: e.reciprocal(p1[:, 1, :], p1[:, 0, :]), t, up="g2")
            t = dv.tt(p1[:, 0, :], p1[:, 1, :], d[:], ALU.mult, t, up="g3")
            io = c("iota").unsqueeze(1).to_broadcast([128, NT, 8])
            for k in range(2):
                q = dv.tt(eq[:, k], io, ixf[:, :, k:k + 1].to_broadcast([128, NT, 8]), ALU.is_equal, t2, up="eq")
                q = dv.tt(eq[:, k], eq[:, k], p1[:, 1 - k, :].unsqueeze(2).to_broadcast([128, NT, 8]), ALU.mult, q, t, up="eqm")
            return r, dv.tt(G[:], eq[:, 0], eq[:, 1], ALU.add, q, gfree, up="G")

        def gate_bufs(reg, n):
            return (reg(f"gsc{n}", [128, NT, 8]), reg(f"gm8{n}", [128, NT, 8]), reg(f"gix{n}", [128, NT, 8], U32),
                    reg(f"gixf{n}", [128, NT, 2]), reg(f"gd{n}", [128, NT]), reg(f"gp{n}", [128, 2, NT]),
                    reg(f"geq{n}", [128, 2, NT, 8]))

        def transposed_gates(G, GT, tok, gt_free):
            s, ps, fr = ring.take()
            for i in range(NT):
                t = pe.tr(ps[0:8, 128 * i:128 * i + 128], G[:, i, :], ident, tok, fr, up="GT")
            t = ac.act(GT[:], ps[0:8, :], ACT.Copy, t, gt_free, up="GT")
            ring.free(s, t)
            return t

        f0 = Region(mid.at)
        W1f = f0("W1f", [128, E * F])
        WF0s = f0("WF0s", [128, NWF0])
        G = f0("G", [128, NT, 8])
        gb = gate_bufs(f0, 0)
        GT = Qb
        f0b = Region(mid.at - 4096 * (NP + 10))
        H = [f0b(f"H{i}", [128, 4, T]) for i in range(2)]
        W2f = f0b("W2f", [128, E * F])
        w1_in = sp.dma(W1f[:], f0w1, a0_end, up="w1")
        wf0_in = sp.dma(WF0s[:], wf0, up="wf0")
        w2_in = sp.dma(W2f[:], f0w2, p_free[:], up="w2")
        GT = f0b("GT", [8, T])

        def wf(a, rows=128):
            return WF0s[0:rows, WF0[a][0]:WF0[a][1]]

        xn_t, xT_t = layernorm(x_t, None)
        h_free = [p_free[:], p_free[:] + q_free]

        def hidden(Hb, w, bias, w_in, free):
            toks = []
            for cc in range(4):
                s, ps, fr = ring.take()
                for a, b in chunks(T):
                    t = pe.mm(ps[:, a:b], w[:, 128 * cc:128 * cc + 128], xT[:, a:b], fr, xT_t, w_in, up="h")
                t = ac.act(Hb[:, cc, :], ps, ACT.Relu, t, free, bias=bias[:, cc:cc + 1], up="h")
                ring.free(s, t)
            return t

        h_t = hidden(H[1], wf("rw1"), wf("rb1"), wf0_in, h_free[1])
        s, ps, fr = ring.take()
        rw2 = wf("rw2").rearrange("p (c e) -> p c e", e=8)
        for i in range(NT):
            for cc in range(4):
                t = pe.mm(ps[:, 8 * i:8 * i + 8], H[1][:, cc, 128 * i:128 * i + 128], rw2[:, cc, :], h_t, fr,
                          start=cc == 0, stop=cc == 3, up="sc")
        h_free[1] = t
        r, g_t = gates(G, ps[:, 0:64], wf("rb2"), t, wf0_in, None, gb)
        ring.free(s, r)
        gt_t = transposed_gates(G, GT, g_t, p_free[:])
        prev = None
        for e in range(E + 1):
            if e < E:
                h_t = hidden(H[e % 2], W1f[:, F * e:F * e + F], WF0s[:, WF0["b1"][0] + 4 * e:WF0["b1"][0] + 4 * e + 4],
                             w1_in, h_free[e % 2])
                now = (e, h_t)
            if prev is not None:
                pe_, h_t = prev
                s, ps, fr = ring.take()
                for i in range(NT):
                    for cc in range(4):
                        t = pe.mm(ps[:, 128 * i:128 * i + 128], H[pe_ % 2][:, cc, 128 * i:128 * i + 128],
                                  W2f[:, 512 * pe_ + 128 * cc:512 * pe_ + 128 * cc + 128], h_t, fr, w2_in,
                                  start=cc == 0, stop=cc == 3, up="y")
                h_free[pe_ % 2] = t
                dv.wait(t, g_t, xn_t, x_t)
                for i in range(NT):
                    x_t = dv.stt(X[:, i, :], ps[:, 128 * i:128 * i + 128], G[:, i, pe_:pe_ + 1], X[:, i, :], ALU.mult,
                                 ALU.add, up="y")
                ring.free(s, x_t)
            prev = now
        s, ps, fr = ring.take()
        for i in range(NT):
            t = pe.mm(ps[:, 128 * i:128 * i + 128], GT[:, 128 * i:128 * i + 128], wf("b2", 8), fr, gt_t, wf0_in, up="b2")
        x_t = dv.tt(xf, xf, ps, ALU.add, t, x_t, up="res")
        ring.free(s, x_t)
        f0_pe = t

        b1 = Region(glob.at)
        WBs = b1("WBs", [128, NWB])
        lat = b1("lat", [32, T])
        QK = b1("QK", [128, NT, 32, 8])
        QR = b1("QR", [128, NT, 32, 8])
        Vt = b1("Vt", [128, NT, D])
        R1 = b1("R1", [128, NT, 32, 4])
        R2 = b1("R2", [128, NT, 32, 4])
        pr = [b1(f"pr{i}", [128, 2048]) for i in range(2)]
        att = b1("att", [128, NT, 16, 16])
        mx = b1("mx", [128, NT, 16])
        sm = b1("sm", [128, NT, 16])
        Ou = b1("Ou", [128, NT, 16, 8])
        wb_in = sp.dma(WBs[:], wb, f0_pe, x_t, up="wb")

        def wbs(a, rows=128):
            return WBs[0:rows, WB[a][0]:WB[a][1]]

        xn_t, xT_t = layernorm(x_t, None)
        s, ps, fr = ring.take()
        for a, b in chunks(T):
            t = pe.mm(ps[0:32, a:b], wbs("down"), xT[:, a:b], fr, xT_t, wb_in, up="lat")
        l_t = ac.act(lat[:], ps[0:32, :], ACT.Identity, t, bias=wbs("bdown", 32), up="lat")
        ring.free(s, l_t)
        s, ps, fr = ring.take()
        for i in range(NT):
            t = pe.mm(ps[:, 128 * i:128 * i + 128], xT[:, 128 * i:128 * i + 128], wbs("q"), fr, xT_t, wb_in, up="q1")
        q_t = dv.tt(QK[:, :, 0:16, :].rearrange("p i h d -> p i (h d)"), ps.rearrange("p (i c) -> p i c", i=NT),
                    wbs("bq").unsqueeze(1).to_broadcast([128, NT, D]), ALU.add, t, wb_in, f0_pe, up="q1")
        ring.free(s, q_t)
        for h in range(2):
            s, ps, fr = ring.take()
            for i in range(4):
                t = pe.mm(ps[:, 256 * i:256 * i + 256], lat[:, 512 * h + 128 * i:512 * h + 128 * i + 128], wbs("up", 32),
                          fr, l_t, up="kv")
            p3 = ps.rearrange("p (i c) -> p i c", i=4)
            bu = wbs("bup").unsqueeze(1).to_broadcast([128, 4, 256])
            k_t = dv.tt(QK[:, 4 * h:4 * h + 4, 16:32, :].rearrange("p i h d -> p i (h d)"), p3[:, :, 0:128],
                        bu[:, :, 0:128], ALU.add, t, up="k1")
            k_t = dv.tt(Vt[:, 4 * h:4 * h + 4, :], p3[:, :, 128:256], bu[:, :, 128:256], ALU.add, up="k1")
            ring.free(s, k_t)

        def rope(out, a, ca, b, cb, o):
            cs = [c(n).rearrange("p (i f) -> p i f", i=NT).unsqueeze(2).to_broadcast([128, NT, 32, 4]) for n in (ca, cb)]
            w_ = [rope_t[0]]
            t1 = t2 = None
            for i in range(NT):
                t1 = dv.tt(R1[:, i], a[:, i], cs[0][:, i], ALU.mult, q_t, k_t, w_, up="r1")
                t2 = dv.tt(R2[:, i], b[:, i], cs[1][:, i], ALU.mult, up="r2")
            for i in range(NT):
                rope_t[0] = dv.tt(out[:, i], R1[:, i], R2[:, i], o, t1, t2, up="r3")
            return rope_t[0]

        rope_t = [None]
        x1, x2 = QK[:, :, :, 0:4], QK[:, :, :, 4:8]
        rope(QR[:, :, :, 0:4], x1, "cos", x2, "sin", ALU.subtract)
        r_t = rope(QR[:, :, :, 4:8], x1, "sin", x2, "cos", ALU.add)
        for i in range(NT):
            p = pr[i % 2]
            p4 = p[:].rearrange("p (h g d) -> p h g d", h=16, g=16)
            t = dv.tt(p4, QR[:, i, 0:16, :].unsqueeze(2).to_broadcast([128, 16, 16, 8]),
                      QR[:, i, 16:32, :].unsqueeze(1).to_broadcast([128, 16, 16, 8]), ALU.mult, r_t, up="p1")
            t = dv.op(lambda e, i=i, p4=p4: e.tensor_reduce(att[:, i], p4, AX, ALU.add), t, up="att")
            t = dv.op(lambda e, i=i: e.tensor_reduce(mx[:, i], att[:, i], AX, ALU.max), t, up="mx")
            t = dv.tt(att[:, i], att[:, i], mx[:, i].unsqueeze(2).to_broadcast([128, 16, 16]), ALU.subtract, t, up="sub")
            a_t = ac.act(att[:, i], att[:, i], ACT.Exp, t, scale=SC, up="att")
            if i >= 1:
                pass
            t = dv.op(lambda e, i=i: e.tensor_reduce(sm[:, i], att[:, i], AX, ALU.add), a_t, up="sm")
            p4 = p[:].rearrange("p (h d g) -> p h d g", h=16, d=8)
            t2 = dv.tt(p4, att[:, i].unsqueeze(2).to_broadcast([128, 16, 8, 16]),
                       Vt[:, i].rearrange("p (g d) -> p d g", d=8).unsqueeze(1).to_broadcast([128, 16, 8, 16]), ALU.mult,
                       up="p2")
            t2 = dv.op(lambda e, i=i, p4=p4: e.tensor_reduce(Ou[:, i], p4, AX, ALU.add), t2, up="ou")
            t = dv.op(lambda e, i=i: e.reciprocal(sm[:, i], sm[:, i]), t, up="rsm")
            t = dv.tt(On[:, i].rearrange("p (h d) -> p h d", d=8), Ou[:, i], sm[:, i].unsqueeze(2).to_broadcast([128, 16, 8]),
                      ALU.mult, t, t2, on_t[0], up="on")
        on_t[0] = t
        bo_t = gp.tt(X[:], X[:], wbs("bout").unsqueeze(1).to_broadcast([128, NT, D]), ALU.add, xn_t, wb_in)
        x_t = out_proj(wbs("out"), wb_in, bo_t)
        b1_end = x_t

        x1r = Region(glob.at)
        WYs = x1r("WYs", [128, NWY])
        y_region = x1r.at
        Q1 = [x1r(f"Q1{i}", [128, 2, T], F32R) for i in range(2)]
        Q2 = [x1r(f"Q2{i}", [128, T], F32R) for i in range(2)]
        K1 = [x1r(f"K1{i}", [128, 2, 512], F32R) for i in range(2)]
        V1 = [x1r(f"V1{i}", [128, 512]) for i in range(2)]
        NPY = 8
        Py = [x1r(f"Py{i}", [128, T]) for i in range(NPY)]
        acc = [x1r(f"acc{i}", [128, T]) for i in range(4)]
        rsy = [x1r(f"rsy{i}", [128, 16]) for i in range(2)]
        sqq = x1r("sqq", [128, T], BF16)
        sqk = [x1r(f"sqk{i}", [128, 512], BF16) for i in range(4)]
        sel2 = x1r("sel2", [128, 32], BF16)
        mqy = x1r("mqy", [64, 8])
        mky = x1r("mky", [128, 32])
        mkp = x1r("mkp", [128, 8])
        nf = x1r("nf", [8, 2, 32])
        sqq_free, sqk_free, sqk_t = [b1_end], [b1_end] * 4, {}
        q1_sq = [None, None]
        sel2_t = dv.copy(sel2[:], c("sel2"), b1_end, up="sel2")
        mky0 = dv.op(lambda e: e.memset(mky[:], 0.0), up="mky0")
        wy_in = sp.dma(WYs[:], wy, b1_end, up="wy")

        def wys(a, lo, n, r0=0, r1=128):
            return WYs[r0:r1, WY[a][0] + lo:WY[a][0] + lo + n]

        xn_t, xT_t = layernorm(x_t, None)
        bo_t = gp.tt(X[:], X[:], wys("b", 0, 128).unsqueeze(1).to_broadcast([128, NT, D]), ALU.add, xn_t, wy_in)
        x_t = bo_t
        A, B = slice(0, 64), slice(64, 128)
        pf = [b1_end] * NPY
        acc_free = [b1_end, b1_end]
        q1_free = [b1_end, b1_end]
        k1_free = [b1_end, b1_end]
        v1_free = [b1_end, b1_end]
        osb_free = [b1_end]
        o_free = [b1_end]
        ypend = []
        NCH = 13
        q_ready = {}
        k1_sq = [None, None]

        def q_pair(p):
            q1, q2 = Q1[p % 2], Q2[p % 2]
            s, ps, fr = ring.take()
            for a, b in chunks(T):
                t = pe.mm(ps[:, a:b], wys("q", 128 * p, 128), xT[:, a:b], fr, xT_t, wy_in, up="qp")
            f = [q1_free[p % 2], q1_sq[p % 2]]
            h1 = ac.act(q1[A, 0, :], ps[A, :], ACT.Copy, t, f, up="qh")
            h2 = ac.act(q1[B, 1, :], ps[B, :], ACT.Copy, up="qh")
            dv.copy(q1[B, 0, :], q1[A, 0, :].bitcast(F32), h1, f)
            dv.tt(q2[A, :], ps[A, :], q1[A, 0, :].bitcast(F32), ALU.subtract)
            dv.copy(q1[A, 1, :], q1[B, 1, :].bitcast(F32), h2)
            r = dv.tt(q2[B, :], ps[B, :], q1[B, 1, :].bitcast(F32), ALU.subtract, up="q")
            ring.free(s, r)
            q_ready[p] = r

            t = None
            for rows, hh in ((A, 0), (B, 1)):
                t = gp.tt(sqq[rows, :], q1[rows, hh, :].bitcast(F32), q1[rows, hh, :].bitcast(F32), ALU.mult, h1, h2,
                          sqq_free[0])
            q1_sq[p % 2] = t
            s, ps, fr = ring.take()
            for a, b in chunks(T):
                r0 = 32 * (a // 512)
                t2 = pe.mm(ps[r0:r0 + 32, 0:512], sel2[:], sqq[:, a:b], t, fr, sel2_t, up="nq")
            sqq_free[0] = t2
            r = dv.op(lambda e: e.tensor_reduce(mqy[:, p:p + 1], ps[0:64, 0:512], AX, ALU.max), t2, up="mqy")
            ring.free(s, r)

        def norm_batch(p, ms):
            s, ps, fr = ring.take()
            for j, m in enumerate(ms):
                n = min(512, S - 512 * m)
                t = pe.mm(ps[32 * j:32 * j + 32, 0:n], sel2[:], sqk[m % 4][:, 0:n], sqk_t[m % 4], fr, sel2_t, up="nk")
                sqk_free[m % 4] = t
            r_, c_ = (128, 512) if len(ms) == 4 else (32, n)
            r = dv.op(lambda e: e.tensor_reduce(mky[0:r_, 4 * p + ms[0] // 4:4 * p + ms[0] // 4 + 1], ps[0:r_, 0:c_], AX,
                                                ALU.max), t, mky0, up="mky")
            ring.free(s, r)

        def norm_flag1():
            s, ps, fr = ring.take()
            t = dv.op(lambda e: e.tensor_reduce(mkp[:], mky[:].rearrange("p (a b) -> p a b", b=4), AX, ALU.max),
                      dv.now("mky"), up="mkp")
            pe.tr(ps[0:8, 0:128], mkp[:], ident, t, fr)
            t = pe.tr(ps[0:8, 128:192], mqy[:], ident[0:64, 0:64], dv.now("mqy"), up="nf")
            dv.op(lambda e: e.tensor_reduce(nf[:, 0, :], ps[0:8, 0:128].rearrange("p (t c) -> p c t", c=32), AX, ALU.max), t)
            t = dv.op(lambda e: e.tensor_reduce(nf[:, 1, :], ps[0:8, 128:192].rearrange("p (t c) -> p c t", c=32), AX,
                                                ALU.max), up="nf")
            t = dv.tt(nf[:, 0, 0:2], nf[:, 0, 0:2], nf[:, 1, 0:2], ALU.mult, t, up="nf")
            t = dv.op(lambda e: e.tensor_reduce(nr[0:8, :], nf[:, 0, 0:2], AX, ALU.max), t, up="nf")
            t = pe.tr(ps[0:1, 512:520], nr[0:8, :], ident[0:8, 0:8], t, up="nf")
            fl_t[2] = compare(2, ps[0:1, 512:520], 0.125, True, t)
            ring.free(s, fl_t[2])

        kv_ready = {}

        def kv_chunk(p, m):
            b = (NCH * p + m) % 2
            n = min(512, S - 512 * m)
            nt = -(-n // 128)
            s, ps, fr = ring.take()
            t = pe.mm(ps[:, 0:n], wys("kv", 128 * p, 128, 0, 96), ctxT[0:96, 512 * m:512 * m + n], fr, wy_in, up="kp")
            for i in range(nt):
                w_ = min(128, n - 128 * i)
                tv = pe.mm(ps[0:w_, 512 + 128 * i:640 + 128 * i], ctxT[0:96, 512 * m + 128 * i:512 * m + 128 * i + w_],
                           wys("kv", 1024 + 128 * p, 128, 0, 96), up="vp")
            k = K1[b]
            f = [k1_free[b], k1_sq[b]]
            h1 = ac.act(k[A, 0, 0:n], ps[A, 0:n], ACT.Copy, t, f, up="kh")
            h2 = ac.act(k[B, 1, 0:n], ps[B, 0:n], ACT.Copy, up="kh")
            dv.tt(k[B, 0, 0:n], ps[A, 0:n], k[A, 0, 0:n].bitcast(F32), ALU.subtract, h1, f)
            r = dv.tt(k[A, 1, 0:n], ps[B, 0:n], k[B, 1, 0:n].bitcast(F32), ALU.subtract, h2, up="k")
            if n == 512:
                rv = dv.copy(V1[b][:], ps[:, 512:1024], tv, v1_free[b], up="v")
            else:
                dv.copy(V1[b][:, 0:256], ps[:, 512:768], tv, v1_free[b])
                rv = dv.copy(V1[b][0:4, 256:384], ps[0:4, 768:896], up="v")
            ring.free(s, rv)
            kv_ready[p, m] = (r, rv)
            for rows, hh in ((A, 0), (B, 1)):
                t = gp.tt(sqk[m % 4][rows, 0:n], k[rows, hh, 0:n].bitcast(F32), k[rows, hh, 0:n].bitcast(F32), ALU.mult,
                          h1, h2, sqk_free[m % 4])
            sqk_t[m % 4] = k1_sq[b] = t

        def finish_pair(p, pv_t, acc_t):
            ob = Osb
            t = ac.act(ob[:], O, ACT.Copy, pv_t, osb_free[0], up="osb")
            o_free[0] = t
            s1, ps1, fr1 = ring.take()
            s2, ps2, fr2 = ring.take()
            for h in range(2):
                ps_, fr_ = ((ps1, fr1), (ps2, fr2))[h]
                for i in range(NT):
                    ts_ = pe.mm(ps_[:, 128 * i:128 * i + 1], acc[2 * (p % 2) + h][:, 128 * i:128 * i + 128],
                                c("one"), acc_t, fr_, up="sum")
                r_ = dv.op(lambda e, h=h, ps_=ps_: e.reciprocal(
                    rsy[p % 2][:, 8 * h:8 * h + 8], ps_.rearrange("p (i c) -> p i c", i=NT)[:, :, 0]), ts_, up="rsy")
                for i in range(NT):
                    ty = pe.mm(ps_[:, 128 * i:128 * i + 128], ob[64 * h:64 * h + 64, 128 * i:128 * i + 128],
                               wys("out", 128 * p, 128, 64 * h, 64 * h + 64), t, r_, up="yp")
                dv.wait(ty, r_, y_state[0])
                for i in range(NT):
                    a_, b_ = ps_[:, 128 * i:128 * i + 128], rsy[p % 2][:, 8 * h + i:8 * h + i + 1]
                    if (p, h) == (0, 0):
                        y_state[0] = dv.ts(Y[:, i, :], a_, b_, None, ALU.mult, ALU.bypass, up="y1")
                    else:
                        y_state[0] = dv.stt(Y[:, i, :], a_, b_, Y[:, i, :], ALU.mult, ALU.add, up="y1")
                ring.free((s1, s2)[h], y_state[0])
            acc_free[p % 2] = ts_
            osb_free[0] = ty

        Y = On
        y_state = [b1_end]
        x_t_bo = x_t
        q_pair(0)
        kv_chunk(0, 0)
        pend = []
        un = 0
        for p in range(8):
            for kt in range(NKT):
                m, i = divmod(kt, 4)
                kw = 128 if kt < KT else 4
                b = (NCH * p + m) % 2
                if i == 1 and (p, m) != (7, NCH - 1):
                    kv_chunk(*((p, m + 1) if m < NCH - 1 else (p + 1, 0)))
                if kt == 40 and p < 7:
                    q_pair(p + 1)
                if kt in (20, 36, 48):
                    norm_batch(p, {20: (0, 1, 2, 3), 36: (4, 5, 6, 7), 48: (8, 9, 10, 11)}[kt])
                if kt == 2 and p > 0:
                    norm_batch(p - 1, (12,))
                k, (kt_, vt_) = K1[b], kv_ready[p, m]
                q1, q2 = Q1[p % 2], Q2[p % 2]
                sA, pA, fA = ring.take()
                sB, pB, fB = ring.take()
                cols = slice(128 * i, 128 * i + kw)
                for a, bb in chunks(T):
                    pe.mm(pA[0:kw, a:bb], k[:, 0, cols], q1[:, 0, a:bb], fA, kt_, q_ready[p], start=True, stop=False)
                for a, bb in chunks(T):
                    pe.mm(pB[0:kw, a:bb], k[:, 1, cols], q1[:, 1, a:bb], fB, start=True, stop=False)
                for a, bb in chunks(T):
                    tA = pe.mm(pA[0:kw, a:bb], k[A, 0, cols], q2[A, a:bb], start=False, stop=True, up="sA")
                    tB = pe.mm(pB[0:kw, a:bb], k[B, 1, cols], q2[B, a:bb], start=False, stop=True, up="sA")
                k1_free[b] = tB
                q1_free[p % 2] = tB
                es = []
                for h, (s, ps, t) in enumerate(((sA, pA, tA), (sB, pB, tB))):
                    pb = un % NPY
                    un += 1
                    t = ac.act(Py[pb][0:kw, :], ps[0:kw, :], ACT.Exp, t, pf[pb], scale=0.125, up="ey")
                    ring.free(s, t)
                    ac_ = acc[2 * (p % 2) + h]
                    if kt == 0:
                        t2 = dv.copy(ac_[:], Py[pb][:], t, acc_free[p % 2], up="acc")
                    else:
                        t2 = dv.tt(ac_[0:kw, :], ac_[0:kw, :], Py[pb][0:kw, :], ALU.add, t, ac_t[h], up="acc")
                    if kt == 0 and h == 0:
                        ac_t = [None, None]
                    ac_t[h] = t2
                    es.append((pb, t, t2))

                def pv(p=p, kt=kt, i=i, kw=kw, b=b, es=es, vt_=vt_):
                    for a, bb in chunks(T):
                        for h in range(2):
                            t = pe.mm(O[64 * h:64 * h + 64, a:bb], V1[b][0:kw, 128 * i + 64 * h:128 * i + 64 * h + 64],
                                      Py[es[h][0]][0:kw, a:bb], es[h][1], vt_, o_free[0], start=kt == 0,
                                      stop=kt == NKT - 1, skip=True, up="pvy")
                    v1_free[b] = t
                    for pb, _, t2 in es:
                        pf[pb] = [t, t2]
                    if kt == NKT - 1:
                        finish_pair(p, t, [es[0][2], es[1][2]])

                pend.append(pv)
                if len(pend) > 1:
                    pend.pop(0)()
        pend.pop(0)()
        norm_batch(7, (12,))
        norm_flag1()
        general("gy", y_region, 64, ctxT, 97, S, gy, 321, 0.125, False, On[:], True, flags[0:1, 2:3], fl_t[2],
                flat(ring.freed, y_state, pf, acc_free, o_free))
        x_t = dv.tt(xf, xf, Y[:].rearrange("p i d -> p (i d)"), ALU.add, y_state, x_t, up="res")
        x1_pe = osb_free[0]

        f1 = Region(glob.at)
        WF1s = f1("WF1s", [128, NWF1])
        A1 = f1("A1", [128, E * F])
        A3 = f1("A3", [128, E * F])
        A2 = f1("A2", [128, E * F])
        xe = [f1(f"xe{i}", [128, T]) for i in range(2)]
        th = [f1(f"th{i}", [128, T]) for i in range(2)]
        H1 = [f1(f"H1{i}", [128, 4, T]) for i in range(2)]
        G1 = f1("G1", [128, NT, 8])
        GT1 = f1("GT1", [8, T])
        gb1 = gate_bufs(f1, 1)
        wf1_in = sp.dma(WF1s[:], wf1, x_t, x1_pe, up="wf1")
        a1_in = sp.dma(A1[:], f1w1, up="a1")
        a3_in = sp.dma(A3[:], f1w3, up="a3")
        a2_in = sp.dma(A2[:], f1w2, up="a2")
        xn_t, xT_t = layernorm(x_t, None)
        x_t = dv.tt(xf, xf, xn[:].rearrange("p i d -> p (i d)"), ALU.add, xn_t, x_t, up="res")
        s, ps, fr = ring.take()
        for i in range(NT):
            t = pe.mm(ps[:, 8 * i:8 * i + 8], xT[:, 128 * i:128 * i + 128], WF1s[:, 0:8], fr, xT_t, wf1_in, up="lg")
        r, g_t = gates(G1, ps[:, 0:64], WF1s[:, 8:16], t, wf1_in, None, gb1)
        ring.free(s, r)
        gt_t = transposed_gates(G1, GT1, g_t, None)
        xe_free, th_free, h_free = [None, None], [None, None], [None, None]
        nth = 0
        prev = None
        for e in range(E + 1):
            if e < E:
                s, ps, fr = ring.take()
                for a, b in chunks(T):
                    t = pe.mm(ps[:, a:b], WF1s[0:8, WF1["sel"][0] + 128 * e:WF1["sel"][0] + 128 * e + 128], GT1[:, a:b], fr,
                              gt_t, wf1_in, up="gb")
                x_e = dv.tt(xe[e % 2][:], xT[:], ps, ALU.mult, t, xT_t, xe_free[e % 2], up="xe")
                ring.free(s, x_e)
                for cc in range(4):
                    su, pu, fu = ring.take()
                    sv, pv_, fv = ring.take()
                    col = slice(512 * e + 128 * cc, 512 * e + 128 * cc + 128)
                    for a, b in chunks(T):
                        tu = pe.mm(pu[:, a:b], A1[:, col], xe[e % 2][:, a:b], fu, x_e, a1_in, up="u")
                    for a, b in chunks(T):
                        tv = pe.mm(pv_[:, a:b], A3[:, col], xe[e % 2][:, a:b], fv, a3_in, up="u")
                    k = nth % 2
                    nth += 1
                    t = ac.act(th[k][:], pu, ACT.Tanh, tu, th_free[k], scale=0.5, up="th")
                    t = dv.stt(th[k][:], th[k][:], 1.0, pu, ALU.add, ALU.mult, t, up="sa")
                    ring.free(su, t)
                    h_t = dv.stt(H1[e % 2][:, cc, :], th[k][:], 0.5, pv_, ALU.mult, ALU.mult, t, tv, h_free[e % 2],
                                 up="hh")
                    th_free[k] = h_t
                    ring.free(sv, h_t)
                xe_free[e % 2] = tv
                now = (e, h_t)
            if prev is not None:
                e_, h_t = prev
                s, ps, fr = ring.take()
                for i in range(NT):
                    for cc in range(4):
                        t = pe.mm(ps[:, 128 * i:128 * i + 128], H1[e_ % 2][:, cc, 128 * i:128 * i + 128],
                                  A2[:, 512 * e_ + 128 * cc:512 * e_ + 128 * cc + 128], h_t, fr, a2_in,
                                  start=cc == 0, stop=cc == 3, up="y")
                h_free[e_ % 2] = t
                x_t = dv.tt(xf, xf, ps, ALU.add, t, x_t, up="res")
                ring.free(s, x_t)
            prev = now

        o_t = sp.dma(out.rearrange("a (i p) d -> p (a i) d", p=128), X[:], x_t, up="out")
        sp.wait(o_t)

        with nc.Block() as block:
            @block.tensor
            def _(e):
                for f in pe.queue:
                    f(e)

            @block.scalar
            def _(e):
                for f in ac.queue:
                    f(e)

            @block.vector
            def _(e):
                for f in dv.queue:
                    f(e)

            @block.gpsimd
            def _(e):
                for f in gp.queue:
                    f(e)

            @block.sync
            def _(e):
                for f in sp.queue:
                    f(e)


def constants():
    c = np.zeros((128, NCST), np.float32)

    def put(name, v):
        c[:, CST[name][0]:CST[name][1]] = v

    q = np.arange(128)
    r = q % 32
    put("id", np.eye(128))
    low = (r >= 16) & (r < 24) | (r == 25)
    put("qs", np.where(low, -1, 1)[:, None])
    put("qb", np.where(low, 1, 0)[:, None])
    low = (r >= 8) & (r < 16)
    put("ks", np.where(low, -1, 1)[:, None])
    put("kb", np.where(low, 1, 0)[:, None])
    put("k1", ((r == 24) | (r == 25))[:, None])
    put("mh", -0.5)
    inv = (1.0 / 10000.0 ** (np.arange(0, 8, 2, dtype=np.float32) / np.float32(8))).astype(np.float32)
    freq = np.arange(T, dtype=np.float32)[:, None] * inv[None]
    freq = freq.reshape(NT, 128, 4).transpose(1, 0, 2).reshape(128, NT * 4)
    put("cos", np.cos(freq))
    put("sin", np.sin(freq))
    put("iota", np.arange(8)[None])
    put("one", 1)
    put("sel4", (q[:, None] // 32 == np.arange(4)[None]) & (r[:, None] < 8))
    put("sel2", q[:, None] // 64 == np.arange(32)[None])
    g = np.zeros((128, T + NT), np.float32)
    g[:, :T] = np.arange(T)[None]
    g[:, T:] = q[:, None] + 128 * np.arange(NT)[None]
    return c, g


def layout(I):
    A = {"x": I["x"], "ctx_in": I["ctx_768"]}
    A["cst"], A["gc"] = constants()

    def z(*s):
        return np.zeros(s, np.float32)

    def rep(w):
        o = z(w.shape[0], 4, 4, 32)
        v = w.reshape(-1, 4, 4, 8)
        for k in range(3):
            o[..., 8 * k:8 * k + 8] = v
        return o.reshape(w.shape[0], 512)

    def put(dst, table, name, v):
        dst[0:v.shape[0], table[name][0]:table[name][1]] = v

    w = A["wa"] = z(128, NWA)
    put(w, WA, "q", rep(I["L0_attn_w_q"].T))
    put(w, WA, "k", rep(I["L0_attn_w_k"].T))
    put(w, WA, "v", I["L0_attn_w_v"].T)
    put(w, WA, "o", I["L0_attn_w_o"].T)
    w = A["wx"] = z(128, NWX)
    put(w, WX, "q", rep(I["L0_xattn_wq"]))
    put(w, WX, "k", rep(I["L0_xattn_wk"]))
    b = z(4, 4, 32)
    b[:, :, 0:24] = rep(I["L0_xattn_bk"][None]).reshape(4, 4, 32)[:, :, 0:24]
    b[:, :, 24:26] = 1
    w[96, WX["k"][0]:WX["k"][1]] = b.reshape(512)
    v = z(97, 16, 9)
    v[:96, :, :8] = I["L0_xattn_wv"].reshape(96, 16, 8)
    v[96, :, :8] = I["L0_xattn_bv"].reshape(16, 8)
    v[96, :, 8] = 1
    put(w, WX, "v", v.reshape(97, 144))
    put(w, WX, "o", I["L0_xattn_wo"])
    put(w, WX, "bq", rep(I["L0_xattn_bq"][None]).reshape(4, 128).T)
    w[:, WX["bo"][0]:WX["bo"][1]] = I["L0_xattn_bo"][None]

    w = A["wf0"] = z(128, NWF0)
    put(w, WF0, "rw1", I["L0_ffn_rw1"])
    put(w, WF0, "rb1", I["L0_ffn_rb1"].reshape(4, 128).T)
    put(w, WF0, "rw2", I["L0_ffn_rw2"].reshape(4, 128, 8).transpose(1, 0, 2).reshape(128, 32))
    w[:, WF0["rb2"][0]:WF0["rb2"][1]] = I["L0_ffn_rb2"][None]
    put(w, WF0, "b1", I["L0_ffn_b1"].reshape(8, 4, 128).transpose(2, 0, 1).reshape(128, 32))
    put(w, WF0, "b2", I["L0_ffn_b2"])
    A["f0w1"] = I["L0_ffn_W1"].transpose(1, 0, 2).reshape(128, 4096)
    A["f0w2"] = I["L0_ffn_W2"].reshape(8, 4, 128, 128).transpose(2, 0, 1, 3).reshape(128, 4096)

    w = A["wb"] = z(128, NWB)
    h = np.arange(16)[:, None] * 16 + np.arange(8)[None]
    perm = np.concatenate([h, h + 8]).reshape(-1)
    put(w, WB, "q", I["L1_attn_Wq"])
    put(w, WB, "down", I["L1_attn_Wdown"])
    put(w, WB, "up", I["L1_attn_Wup"][:, perm])
    put(w, WB, "out", I["L1_attn_Wout"])
    w[:, WB["bq"][0]:WB["bq"][1]] = I["L1_attn_bq"][None]
    w[:, WB["bup"][0]:WB["bup"][1]] = I["L1_attn_bup"][perm][None]
    w[:, WB["bout"][0]:WB["bout"][1]] = I["L1_attn_bout"][None]
    put(w, WB, "bdown", I["L1_attn_bdown"][:, None])

    w = A["wy"] = z(128, NWY)
    put(w, WY, "q", I["L1_xattn_w_q"])
    put(w, WY, "kv", I["L1_xattn_w_kv"])
    put(w, WY, "out", I["L1_xattn_w_out"].reshape(8, 128, 128).transpose(1, 0, 2).reshape(128, 1024))
    w[:, WY["b"][0]:WY["b"][1]] = I["L1_xattn_b_out"][None]

    w = A["wf1"] = z(128, NWF1)
    put(w, WF1, "g", I["L1_ffn_Wg"])
    w[:, WF1["bg"][0]:WF1["bg"][1]] = I["L1_ffn_bg"][None]
    put(w, WF1, "sel", np.repeat(np.eye(8, dtype=np.float32), 128, axis=1))
    A["f1w1"] = I["L1_ffn_W1"].transpose(1, 0, 2).reshape(128, 4096)
    A["f1w3"] = I["L1_ffn_W3"].transpose(1, 0, 2).reshape(128, 4096)
    A["f1w2"] = I["L1_ffn_W2"].reshape(8, 4, 128, 128).transpose(2, 0, 1, 3).reshape(128, 4096)

    g = A["ga"] = z(16, 128, 25)
    for k, n in enumerate("qkv"):
        g[:, :, 8 * k:8 * k + 8] = I["L0_attn_w_" + n].reshape(16, 8, 128).transpose(0, 2, 1)
    g = A["gx"] = z(16, 128, 25)
    g[:, :, :8] = I["L0_xattn_wq"].reshape(128, 16, 8).transpose(1, 0, 2)
    for k, n in enumerate("kv"):
        g[:, :96, 8 + 8 * k:16 + 8 * k] = I["L0_xattn_w" + n].reshape(96, 16, 8).transpose(1, 0, 2)
        g[:, 96, 8 + 8 * k:16 + 8 * k] = I["L0_xattn_b" + n].reshape(16, 8)
    g[:, :8, 24] = I["L0_xattn_bq"].reshape(16, 8)
    g = A["gy"] = z(16, 128, 321)
    g[:, :, :64] = I["L1_xattn_w_q"].reshape(128, 16, 64).transpose(1, 0, 2)
    kv = I["L1_xattn_w_kv"].reshape(96, 2, 16, 64)
    for k in range(2):
        g[:, :96, 64 + 64 * k:128 + 64 * k] = kv[:, k].transpose(1, 0, 2)
    g[:, :64, 193:] = I["L1_xattn_w_out"].reshape(16, 64, 128)
    return A


_OUT = (1, 1024, 128)


def kernel(**inputs):
    import concourse.bacc as bacc
    from concourse.bass_utils import run_bass_kernel_spmd

    nc = bacc.Bacc("TRN2", target_bir_lowering=False, num_devices=1)
    arrays, args = {}, {}
    for name, a in layout({k: np.asarray(v) for k, v in inputs.items()}).items():
        a = np.ascontiguousarray(a)
        arrays["in_" + name] = a
        args[name] = nc.dram_tensor("in_" + name, a.shape, mybir.dt.from_np(a.dtype), kind="ExternalInput").ap()
    out = nc.dram_tensor("out_0", _OUT, F32, kind="ExternalOutput").ap()
    program(nc, out, **args)
    r = run_bass_kernel_spmd(nc, [arrays], core_ids=[0])
    return r.results[0]["out_0"]
```

```python
from contextlib import ExitStack

import numpy as np

import concourse.bass as bass
from concourse import mybir

F32 = mybir.dt.float32
F32R = mybir.dt.float32r
BF16 = mybir.dt.bfloat16
U32 = mybir.dt.uint32
I32 = mybir.dt.int32
ACT = mybir.ActivationFunctionType
ALU = mybir.AluOpType
AX = mybir.AxisListType.X

T = 1024
NT = 8
D = 128
S = 6404
KT = 50
NKT = 51
E = 8
F = 512


class Lane:

    def __init__(self, nc, ctx, name):
        self.nc, self.ctx, self.name = nc, ctx, name
        self.queue, self.seen, self.sems = [], {}, {}
        self.last = None

    def wait(self, *tokens):
        for tok in tokens:
            if tok is None:
                continue
            if isinstance(tok, list):
                self.wait(*tok)
                continue
            sem, n = tok
            if self.seen.get(id(sem), 0) < n:
                self.seen[id(sem)] = n
                self.queue.append(lambda e, sem=sem, n=n: e.wait_ge(sem, n))

    def count(self, kind, k):
        if kind not in self.sems:
            self.sems[kind] = [self.ctx.enter_context(self.nc.semaphore(f"{self.name}_{kind}")), 0]
        self.sems[kind][1] += k
        return tuple(self.sems[kind])

    def op(self, fn, *tokens, up=None, k=1):
        self.wait(*tokens)
        if self.name == "gp":
            self.wait(self.last)
            self.last = self.count("done", 1)
            self.queue.append(lambda e: fn(e).then_inc(self.last[0], 1))
            return self.last
        if up is None:
            self.queue.append(fn)
            return None
        tok = self.count(up, k)
        self.queue.append(lambda e: fn(e).then_inc(tok[0], k))
        return tok

    def now(self, kind):
        return tuple(self.sems[kind])

    def mm(self, out, lhsT, rhs, *tokens, start=True, stop=True, up=None, skip=False):
        return self.op(lambda e: e.matmul(out, lhsT, rhs, start=start, stop=stop, skip_group_check=skip),
                       *tokens, up=up)

    def tr(self, out, in_, ident, *tokens, up=None):
        return self.op(lambda e: e.transpose(out, in_, ident), *tokens, up=up)

    def act(self, out, in_, func, *tokens, up=None, **kw):
        return self.op(lambda e: e.activation(out, in_, func, **kw), *tokens, up=up)

    def tt(self, out, a, b, o, *tokens, up=None):
        return self.op(lambda e: e.tensor_tensor(out, a, b, o), *tokens, up=up)

    def ts(self, out, a, s1, s2, o0, o1, *tokens, up=None):
        return self.op(lambda e: e.tensor_scalar(out, a, s1, s2, o0, o1), *tokens, up=up)

    def stt(self, out, a, s, b, o0, o1, *tokens, up=None):
        return self.op(lambda e: e.scalar_tensor_tensor(out, a, s, b, o0, o1), *tokens, up=up)

    def copy(self, out, in_, *tokens, up=None):
        return self.op(lambda e: e.tensor_copy(out, in_), *tokens, up=up)

    def load_flag(self, ap, *tokens):
        self.wait(*tokens)
        box = []
        self.queue.append(lambda e: box.append(e.value_load(ap, min_val=0, max_val=1)))
        return box

    def when(self, box, body):
        def go(e):
            with e.If(box[0] == 1):
                body(e)
        self.queue.append(go)

    def dma(self, out, in_, *tokens, up):
        return self.op(lambda e: e.dma_start(out, in_), *tokens, up=up, k=16)


class Relay:

    def __init__(self, outer, inner, dma):
        self.sem = dict(outer=outer, inner=inner)
        self.dma = dma
        self.stages = dict(outer=[], inner=[])

    def stage(self, loop, lane, *fns):
        self.stages[loop].append((lane, fns))

    def run(self, e, lane, start, load):
        so, si = self.sem["outer"], self.sem["inner"]
        no, ni = len(self.stages["outer"]), len(self.stages["inner"])
        start(e)
        if lane == "dv":
            e.sem_inc(so, 1)
            e.sem_inc(si, 1)
        with e.Fori(0, 16) as h:
            if lane == "sp":
                e.wait_ge(si, h * (8 * ni) + 1)
                load(e, h)
            base = h * no + 1
            for k, (who, fns) in enumerate(self.stages["outer"]):
                if who == lane:
                    e.wait_ge(so, base + k)
                    if k == 0:
                        e.wait_ge(self.dma, (h + 1) * 16)
                    for fn in fns[:-1]:
                        fn(e, h, None)
                    fns[-1](e, h, None).then_inc(so, 1)
            if any(who == lane for who, _ in self.stages["inner"]):
                with e.Fori(0, 8) as q:
                    base = (h * 8 + q) * ni + 1
                    for k, (who, fns) in enumerate(self.stages["inner"]):
                        if who == lane:
                            e.wait_ge(si, base + k)
                            if k == 0:
                                e.wait_ge(so, (h + 1) * no + 1)
                            for fn in fns[:-1]:
                                fn(e, h, q)
                            fns[-1](e, h, q).then_inc(si, 1)
        e.wait_ge(si, 16 * 8 * ni + 1)


class Ring:

    def __init__(self, ap, banks):
        self.ap, self.banks, self.freed, self.i = ap, banks, [None] * banks, 0

    def take(self, n=2):
        if self.i + n > self.banks:
            self.i = 0
        b = range(self.i, self.i + n)
        self.i = (self.i + n) % self.banks
        return b, self.ap[:, 512 * b[0]:512 * b[-1] + 512], [self.freed[k] for k in b]

    def free(self, b, tok):
        for k in b:
            self.freed[k] = tok


CST = {}
_c = 0
for _n, _w in [("id", 128), ("qs", 1), ("qb", 1), ("ks", 1), ("kb", 1), ("mh", 8),
               ("cos", NT * 4), ("sin", NT * 4), ("iota", 8), ("one", 1),
               ("selh", 32), ("sel2", 32)]:
    CST[_n] = (_c, _c + _w)
    _c += _w
NCST = _c
WA = dict(q0=(0, 128), k0=(128, 256), q=(256, 384), k=(384, 512), v=(512, 640), o=(640, 768))
NWA = 768
WX = dict(q0=(0, 128), q=(128, 256), k=(256, 384), v=(384, 528), o=(528, 656), bq0=(656, 657), bq=(657, 658),
          bo=(658, 786))
NWX = 786
WF0 = dict(rw1=(0, 512), rb1=(512, 516), rw2=(516, 548), rb2=(548, 556), b1=(556, 588), b2=(588, 716))
NWF0 = 716
WB = dict(q=(0, 128), down=(128, 160), up=(160, 416), out=(416, 544), bq=(544, 672), bout=(672, 800), bdown=(800, 801))
NWB = 801
NKV = 2048
WY = dict(q=(0, 1024), kv=(1024, 3072), out=(3072, 4096), b=(4096, 4224))
NWY = 4224
WF1 = dict(g=(0, 8), bg=(8, 16))
NWF1 = 16


def program(nc, out, x, ctx_in, cst, wa, wx, wf0, f0w1, f0w2, wb, wy, wf1, f1w1, f1w3, f1w2, ga, gx, gy, gc, limit=60.0):
    ctx = ExitStack()
    with ctx:
        pe, ac, dv, gp, sp = [Lane(nc, ctx, n) for n in ("pe", "ac", "dv", "gp", "sp")]
        PS = ctx.enter_context(nc.psum_tensor("PS", [128, 4096], F32))
        ring = Ring(PS, 6)
        O = PS[:, 3072:4096]

        BASE = 16512

        class Region:

            def __init__(self, at):
                self.at = at

            def __call__(self, name, shape, dt=F32):
                size = (2 if dt == BF16 else 4) * int(np.prod(shape[1:]))
                t = nc.alloc_sbuf_tensor_at(name, shape, dt, offset=BASE + self.at)
                self.at += (size + 31) // 32 * 32
                assert BASE + self.at <= 229344, (name, self.at)
                return t

        glob = Region(0)
        X = glob("X", [128, NT, D])
        xn = glob("xn", [128, NT, D])
        xT = glob("xT", [128, T])
        C = glob("C", [128, NCST])
        st = glob("st", [128, NT, 6])
        mv = glob("mv", [128, NT, 2])
        ve = glob("ve", [128, NT])
        rstd = glob("rstd", [128, NT])
        rs = glob("rs", [128, 32])
        On = glob("On", [128, NT, D])
        Osb = glob("Osb", [128, T])
        flags = glob("flags", [1, 8], I32)
        fm = glob("fm", [1, 8])
        nr = glob("nr", [64, 1])
        fl = glob("fl", [1, 64])
        mq = glob("mq", [128, 1])
        mk = glob("mk", [128, 13])
        mkr = glob("mkr", [128, 1])
        selh = glob("selh", [128, 32], BF16)
        WF1s = glob("WF1s", [128, NWF1])
        ctxT = glob("ctxT", [97, S])

        def c(name):
            return C[:, CST[name][0]:CST[name][1]]

        ident = c("id")

        xf = X[:].rearrange("p i d -> p (i d)")
        x_in = sp.dma(X[:], x.rearrange("a (i p) d -> p (a i) d", p=128), up="x")
        c_in = sp.dma(C[:], cst, up="cst")
        wf1_in = sp.dma(WF1s[:], wf1, up="wf1")

        def layernorm(ready, xT_free):
            norm, cols = [], []
            dv.wait(xT_free)
            pw = []
            for h in range(2):
                tiles, four = range(4 * h, 4 * h + 4), slice(4 * h, 4 * h + 4)
                dv.wait(ready[h])
                for i in tiles:
                    t = dv.op(lambda e, i=i: e.bn_stats(st[:, i, :], X[:, i, :]), up="ln")
                dv.wait(t)
                for i in tiles:
                    t = dv.op(lambda e, i=i: e.bn_aggr(mv[:, i, :], st[:, i, :]), up="ln")
                t = dv.ts(ve[:, four], mv[:, four, 1], 1e-5, None, ALU.add, ALU.bypass, t, up="ln")
                pw.append(gp.tt(rstd[:, four], ve[:, four], c("mh")[:, 0:4], ALU.pow, t, c_in))
            for h in range(2):
                dv.wait(pw[h])
                for i in range(4 * h, 4 * h + 4):
                    n = dv.ts(xn[:, i, :], X[:, i, :], mv[:, i, 0:1], rstd[:, i:i + 1], ALU.subtract, ALU.mult, up="xn")
                norm.append(n)
            for h in range(2):
                s, ps, fr = ring.take(1)
                for i in range(4):
                    t = pe.tr(ps[:, 128 * i:128 * i + 128], xn[:, 4 * h + i, :], ident, norm[h], fr, c_in, up="xT")
                t = ac.act(xT[:, 512 * h:512 * h + 512], ps, ACT.Copy, t, xT_free, up="xT")
                cols.append(t)
                ring.free(s, t)
            return norm, cols

        def chunks(n):
            return [(a, min(a + 512, n)) for a in range(0, n, 512)]

        mid = Region(glob.at)
        WXs = mid("WXs", [128, NWX])
        kx_at = mid.at
        Kx = mid("Kx", [128, S], F32R)
        V0 = mid("V0", [128, NKT, 144])
        Qz = [mid(f"Qz{i}", [128, 4, T], F32R) for i in range(2)]
        tmp = mid("tmp", [128, T], F32R)
        Qb = mid("Qb", [128, T])
        p_region = mid.at
        NP = 8
        P = [mid(f"P{i}", [128, T]) for i in range(NP)]
        first = Region(mid.at)
        WAs = first("WAs", [128, NWA])
        Va = first("Va", [128, NT, 16, 9])
        Ka = [first(f"Ka{i}", [128, T], F32R) for i in range(2)]
        sq = [Region(p_region + 4096 * 7 + 2048 * i)(f"sq{i}", [128, T], BF16) for i in range(2)]
        hilo = [(first(f"hi{i}", [128, T], F32R), first(f"lo{i}", [128, T], F32R)) for i in range(2)]
        kreg = Region(kx_at)
        CN = 10
        cn = kreg("cn", [128, KT, 96])
        ct = kreg("ct", [4, 96])

        def scratch(name, cols):
            return nc.dram_tensor(name, [4, 4, 4, 8, cols], F32, kind="Internal").ap()

        QDa, KDa, QDx, KDx = scratch("QDa", T), scratch("KDa", T), scratch("QDx", T), scratch("KDx", S)
        stores = []

        cmain = ctx_in[0, 0:128 * KT, :].rearrange("(p t) d -> p t d", t=KT)
        wa_in = sp.dma(WAs[:], wa, up="wa")
        cn_in = [sp.dma(cn[:, CN * b:CN * (b + 1), :], cmain[:, CN * b:CN * (b + 1), :], up=f"cn{b}") for b in range(KT // CN)]
        ct_in = sp.dma(ct[:], ctx_in[0, 128 * KT:S, :], up="ct")
        wx_in = sp.dma(WXs[:], wx, up="wx")
        o0 = dv.op(lambda e: e.memset(O, 0.0), up="const")

        def w(a):
            return WAs[:, WA[a][0]:WA[a][1]]

        def wxs(a, rows=128):
            return WXs[0:rows, WX[a][0]:WX[a][1]]

        ctx_t = {}

        def ctx_task(m):
            s, ps, fr = ring.take()
            for kt in range(8 * m, min(8 * m + 8, NKT)):
                i = kt - 8 * m
                if kt == KT:
                    t = pe.tr(ps[0:96, 128 * i:128 * i + 4], ct[:], ident[0:4, 0:4], ct_in, c_in, fr, up="ctxT")
                else:
                    t = pe.tr(ps[0:96, 128 * i:128 * i + 128], cn[:, kt, :], ident, cn_in[kt // CN], c_in, fr, up="ctxT")
            n = min(1024, S - 1024 * m)
            ctx_t[m] = ac.act(ctxT[0:96, 1024 * m:1024 * m + n], ps[0:96, 0:n], ACT.Copy, t, up="ctxT")
            ring.free(s, ctx_t[m])

        v0_t = {}

        def v0_task(m):
            s, ps, fr = ring.take()
            n = min(6, NKT - 6 * m)
            for i in range(n):
                kt = 6 * m + i
                k = 128 if kt < KT else 4
                o = 512 * (i // 3) + 144 * (i % 3)
                t = pe.mm(ps[0:k, o:o + 144], ctxT[0:97, 128 * kt:128 * kt + k], wxs("v", 97), fr, ctx_t[kt // 8], c1, wx_in,
                          up="v0")
            if n == 6:
                r = dv.copy(V0[:, 6 * m:6 * m + 6, :].rearrange("p (a b) c -> p a (b c)", a=2),
                            ps.rearrange("p (a b) -> p a b", a=2)[:, :, 0:432], t, up="v0")
            else:
                dv.copy(V0[:, 6 * m:6 * m + 2, :].rearrange("p b c -> p (b c)"), ps[:, 0:288], t)
                r = dv.copy(V0[0:4, 6 * m + 2, :], ps[0:4, 288:432], up="v0")
            v0_t[m] = r
            ring.free(s, r)

        part_free = [None, None]
        sq_t = {}
        part_i = [0]

        def store_parts(src, n, tok, dst, which, pool, top=None, square=None):
            b = part_i[0] % 2
            part_i[0] += 1
            hi, lo_ = hilo[b]
            h = dv.copy(hi[:, 0:n], src, tok, part_free[b], up="parts")
            t = t2 = dv.tt(lo_[:, 0:n], src, hi[:, 0:n].bitcast(F32), ALU.subtract, h, up="parts")
            if square is not None:
                t2 = sq_t[square] = ac.act(sq[square][:], hi[:].bitcast(F32), ACT.Square, h, up="sq")
            if top is not None:
                t2 = dv.op(lambda e: e.tensor_reduce(top, hi[:, 0:n].bitcast(F32), AX, ALU.max, apply_absolute_value=True),
                           up="mk")
            out = []
            for r, p in enumerate(which):
                if p is None:
                    continue
                out.append(sp.dma(dst[:, :, r, :, :].rearrange("g j d c -> (g j) d c"), (hi, lo_)[p][:, 0:n].bitcast(F32), t, up=pool))
            part_free[b] = [out[-1], t, t2]
            stores.append(out[-1])
            return t, out[-1]

        tmp_free = [None]

        def direct(parts, wk, y_bias, sgn, sel, w_in, dst_free, src_t, src):
            s, ps, fr = ring.take()
            toks = []
            for a, b in chunks(T):
                t = pe.mm(ps[:, a:b], wk, src[:, a:b], fr, src_t[a // 512], w_in, up="dir")
            if y_bias is None:
                y, yt = ps, t
            else:
                y, yt = Qb[:], ac.act(Qb[:], ps, ACT.Identity, t, qb_free[0], bias=y_bias, up="qb")
            t = ac.act(tmp[:], y, ACT.Copy, yt, tmp_free[0], scale=sgn, up="tmp")
            for rows, d in parts:
                toks.append(dv.stt(d, y[rows, :], sel[rows, :], tmp[rows, :].bitcast(F32), ALU.mult, ALU.add, t, dst_free,
                                   up="dir"))
            tmp_free[0] = qb_free[0] = toks[-1]
            ring.free(s, toks[-1])
            return toks

        qb_free = [None]
        q0_parts = [(slice(32 * j, 32 * j + 32), Qz[0][32 * j:32 * j + 32, j, :]) for j in range(4)]

        def load_q(g, QD, stored, free):
            return [sp.dma(Qz[g % 2][32 * j:32 * j + 24, j, :].bitcast(F32), QD[g, j, 0:3].rearrange("r d c -> (r d) c"), stored, free, qz1,
                           up=f"lq{g % 2}") for j in range(4)][-1]

        SC = float(1 / np.sqrt(8))

        def flat(*toks):
            out = []
            for t in toks:
                if isinstance(t, list):
                    out += flat(*t)
                elif t is not None:
                    out.append(t)
            return out

        def general(name, region, hd, src, rows, nkeys, weights, W, scale, causal, out, final, flag, ready):
            nt = -(-nkeys // 128)
            g = Region(region)
            Wg = g(name + "W", [128, W])
            QT = g(name + "QT", [hd, T])
            Qc = g(name + "Qc", [hd, 128])
            KT_ = g(name + "KT", [hd, nkeys])
            Vg = g(name + "V", [128, nt, hd])
            Sg = g(name + "S", [128, nkeys])
            PT = g(name + "PT", [128, 512])
            sc4 = g(name + "s", [128, 4])
            if causal:
                io = g(name + "io", [128, T + NT])
                msk = g(name + "mk", [128, T])
            if final:
                Oc = g(name + "Oc", [128, hd])
                OT = g(name + "OT", [hd, 128])
            outer, inner, gdma, cdma = [ctx.enter_context(nc.semaphore(f"{name}_{n}"))
                                        for n in ("outer", "inner", "dma", "const")]
            r = Relay(outer, inner, gdma)
            P0, P1 = PS[:, 0:512], PS[:, 512:1024]
            big = PS[:, 1024:3072]

            def mm(o, a, b, st=True, sp_=True):
                return lambda e, h, q: e.matmul(o, a, b, start=st, stop=sp_)

            def cp(o, a):
                return lambda e, h, q: e.tensor_copy(o, a)

            r.stage("outer", "pe", *[mm(PS[0:hd, a:a + 512], Wg[:, 0:hd], xT[:, a:a + 512]) for a in (0, 512)])
            r.stage("outer", "dv", lambda e, h, q: e.tensor_scalar(QT[:], PS[0:hd, 0:1024], Wg[0:hd, 3 * hd:3 * hd + 1], None,
                                                                    ALU.add, ALU.bypass))
            for a in range(0, nkeys, 2048):
                n = min(2048, nkeys - a)
                r.stage("outer", "pe", *[mm(big[0:hd, b:min(b + 512, n)], Wg[0:rows, hd:2 * hd],
                                            src[0:rows, a + b:a + min(b + 512, n)]) for b in range(0, n, 512)])
                r.stage("outer", "dv", cp(KT_[:, a:a + n], big[0:hd, 0:n]))
            per = 2048 // hd
            for a in range(0, nt, per):
                ts_ = range(a, min(a + per, nt))
                r.stage("outer", "pe", *[mm(big[0:min(128, nkeys - 128 * t), hd * (t - a):hd * (t - a) + hd],
                                            src[0:rows, 128 * t:min(128 * t + 128, nkeys)], Wg[0:rows, 2 * hd:3 * hd])
                                         for t in ts_])
                full = [t for t in ts_ if 128 * t + 128 <= nkeys]
                r.stage("outer", "dv", cp(Vg[:, a:a + len(full), :].rearrange("p t d -> p (t d)"), big[:, 0:hd * len(full)]))
                if len(full) < len(ts_):
                    t = ts_[-1]
                    r.stage("outer", "dv", cp(Vg[0:nkeys - 128 * t, t, :],
                                              big[0:nkeys - 128 * t, hd * (t - a):hd * (t - a) + hd]))
            r.stage("inner", "dv", lambda e, h, q: e.tensor_copy(Qc[:], QT[:, bass.ds(q * 128, 128)]))
            for a in range(0, nkeys, 2048):
                n = min(2048, nkeys - a)
                r.stage("inner", "pe", *[mm(big[:, b:min(b + 512, n)], Qc[:], KT_[:, a + b:a + min(b + 512, n)])
                                         for b in range(0, n, 512)])
                r.stage("inner", "dv", cp(Sg[:, a:a + n], big[:, 0:n]))
            if causal:
                r.stage("inner", "dv", lambda e, h, q: e.tensor_copy(sc4[:, 3:4], io[:, bass.ds(q + T, 1)]))
                r.stage("inner", "dv", lambda e, h, q: e.tensor_scalar(msk[:], io[:, 0:T], sc4[:, 3:4], -3e38, ALU.is_gt,
                                                                        ALU.mult))
                r.stage("inner", "dv", lambda e, h, q: e.tensor_tensor(Sg[:], Sg[:], msk[:], ALU.add))
            r.stage("inner", "dv", lambda e, h, q: e.tensor_reduce(sc4[:, 0:1], Sg[:], AX, ALU.max))
            r.stage("inner", "dv", lambda e, h, q: e.tensor_scalar(sc4[:, 1:2], sc4[:, 0:1], -scale, None, ALU.mult,
                                                                    ALU.bypass))
            r.stage("inner", "ac", lambda e, h, q: e.activation(Sg[:], Sg[:], ACT.Exp, bias=sc4[:, 1:2], scale=scale,
                                                                 accum_out=sc4[:, 2:3]))
            for a in range(0, nt, 4):
                ts_ = range(a, min(a + 4, nt))
                ws = [min(128, nkeys - 128 * t) for t in ts_]
                r.stage("inner", "pe", *[(lambda e, h, q, t=t, w=w, a=a: e.transpose(
                    P0[0:w, 128 * (t - a):128 * (t - a) + 128], Sg[:, 128 * t:128 * t + w], ident))
                    for t, w in zip(ts_, ws)])
                nf = sum(w == 128 for w in ws)
                if nf:
                    r.stage("inner", "dv", cp(PT[:, 0:128 * nf], P0[:, 0:128 * nf]))
                if nf < len(ws):
                    r.stage("inner", "dv", cp(PT[0:ws[-1], 128 * nf:128 * nf + 128], P0[0:ws[-1], 128 * nf:128 * nf + 128]))
                r.stage("inner", "pe", *[mm(P1[:, 0:hd], PT[0:w, 128 * (t - a):128 * (t - a) + 128], Vg[0:w, t, :], t == 0,
                                            t == nt - 1) for t, w in zip(ts_, ws)])
            r.stage("inner", "dv", lambda e, h, q: e.reciprocal(sc4[:, 0:1], sc4[:, 2:3]))
            if not final:
                r.stage("inner", "dv", lambda e, h, q: e.tensor_scalar(
                    out[:, bass.ds(q * 16 + h, 1), :], P1[:, 0:hd].unsqueeze(1), sc4[:, 0:1], None, ALU.mult, ALU.bypass))
            else:
                r.stage("inner", "dv", lambda e, h, q: e.tensor_scalar(Oc[:], P1[:, 0:hd], sc4[:, 0:1], None, ALU.mult,
                                                                        ALU.bypass))
                r.stage("inner", "pe", mm(P0[0:hd, 0:128], Oc[:], ident))
                r.stage("inner", "dv", cp(OT[:], P0[0:hd, 0:128]))
                r.stage("inner", "pe", mm(P1[:, 0:128], OT[:], Wg[0:hd, 3 * hd + 1:3 * hd + 129]))
                r.stage("inner", "dv", lambda e, h, q: e.tensor_tensor(out[:, bass.ds(q, 1), :], out[:, bass.ds(q, 1), :],
                                                                        P1[:, 0:128].unsqueeze(1), ALU.add))

            def start(name_):
                def go(e):
                    for sem, n in ready:
                        e.wait_ge(sem, n)
                    if name_ == "sp" and causal:
                        e.dma_start(io[:], gc).then_inc(cdma, 16)
                    if name_ == "dv" and causal:
                        e.wait_ge(cdma, 16)
                    if name_ == "dv" and final:
                        e.memset(out, 0.0).then_inc(cdma, 1)
                        e.wait_ge(cdma, 1)
                return go

            def load(e, h):
                e.dma_start(Wg[:], weights[bass.ds(h, 1)].rearrange("a p f -> (a p) f")).then_inc(gdma, 16)

            for lane in (pe, ac, dv, sp):
                lane.when(flag[lane.name], lambda e, lane=lane: r.run(e, lane.name, start(lane.name), load))

        def load_flags(k):
            return {lane.name: lane.load_flag(flags[0:1, k:k + 1], fl_t[k]) for lane in (pe, ac, dv, sp)}

        osb_free = [None, None]
        on_t = [None, None]
        p_free = [None] * NP
        unit = [0]
        o_free = [[o0, o0]]
        q_free = [None, None]

        def attend8(nkt, width, K, Vt, v_tok, q_t, k_tok, tasks, k_used, causal):
            pv_q = []
            pv_last = [None, None]

            def emit_pv(final=False):
                while pv_q and (final or unit[0] >= pv_q[0][0]):
                    pv_q.pop(0)[1]()

            for g in range(4):
                for kt in range(nkt):
                    kw = width(kt)
                    lo = 128 * kt if causal else 0
                    tile = []
                    todo = list(tasks.get((g, kt), []))
                    for j in range(4):
                        off = 512 if lo >= 512 else 0
                        s, ps, fr = ring.take(1 if off else 2)
                        for a, b in ((lo, 512), (max(lo, 512), 1024)):
                            if a < b:
                                t = pe.mm(ps[0:kw, a - off:b - off], K(g)[:, 128 * kt:128 * kt + kw], Qz[g % 2][:, j, a:b], fr,
                                          q_t[g][j], k_tok(g, kt), up="qk")
                        pb = unit[0] % NP
                        unit[0] += 1
                        t2 = ac.act(P[pb][0:kw, lo:T], ps[0:kw, lo - off:T - off], ACT.Exp, t, p_free[pb], scale=SC, up="exp")
                        ring.free(s, t2)
                        if causal:
                            t2 = gp.op(lambda e, pb=pb, lo=lo: e.affine_select(
                                out=P[pb][:, lo:lo + 128], in_=P[pb][:, lo:lo + 128], compare_op=ALU.is_ge, fill=0.0,
                                base=0, pattern=[[1, 128]], channel_multiplier=-1), t2, up="mask")
                        tile.append((pb, t2))
                        emit_pv()
                        if j == 3:
                            k_used[g, kt] = t
                            q_free[g % 2] = t
                        if todo and j >= 4 - len(todo):
                            todo.pop(0)()

                    def pv(h, g=g, kt=kt, kw=kw, lo=lo, tile=tile):
                        a, b = max(lo, 512 * h), 512 * h + 512
                        t = pv_last[h]
                        if a < b:
                            last = (b // 128 if causal else nkt) - 1
                            for j, (pb, tk) in enumerate(tile):
                                t = pe.mm(O[32 * j:32 * j + 9, a:b], Vt(kt, 4 * g + j), P[pb][0:kw, a:b], tk, o_free[0][h],
                                          v_tok(kt), start=kt == 0, stop=kt == last, skip=True, up="pv")
                        pv_last[h] = t
                        if h == 1:
                            for pb, _ in tile:
                                p_free[pb] = t
                        if h == 1 and kt == nkt - 1:
                            finish_group(g, pv_last)

                    pv_q.append((unit[0] + LAG, lambda pv=pv: pv(0)))
                    pv_q.append((unit[0] + LAG + 2, lambda pv=pv: pv(1)))
            emit_pv(True)

        LAG = 2

        def finish_group(g, pv_t):
            o_free[0] = []
            for h in range(2):
                cols, tiles = slice(512 * h, 512 * h + 512), slice(4 * h, 4 * h + 4)
                e_t = ac.act(Osb[:, cols], O[:, cols], ACT.Copy, pv_t[h], osb_free[h], up="osb")
                o_free[0].append(e_t)
                s, ps, fr = ring.take(1)
                pe.wait(e_t, fr)
                for i in range(4):
                    t = pe.tr(ps[:, 128 * i:128 * i + 128], Osb[:, 512 * h + 128 * i:512 * h + 128 * i + 128], ident, up="otr")
                osb_free[h] = t
                v = ps.rearrange("p (i j c) -> p i j c", i=4, j=4)
                r3 = rs[:, 16 * h:16 * h + 16].rearrange("p (i j) -> p i j", j=4)
                r = dv.op(lambda e, v=v, r3=r3: e.reciprocal(r3, v[:, :, :, 8]), t, on_t[h], up="rs")
                on_t[h] = dv.tt(On[:].rearrange("p i (h c) -> p i h c", c=8)[:, tiles, 4 * g:4 * g + 4, :], v[:, :, :, 0:8],
                                r3.unsqueeze(3).to_broadcast([128, 4, 4, 8]), ALU.mult, r, up="on")
                ring.free(s, on_t[h])

        def out_proj(wo, w_in, extra_free):
            done = []
            mid_t = []
            for h in range(2):
                cols = slice(512 * h, 512 * h + 512)
                s, ps, fr = ring.take(1)
                for i in range(4):
                    t = pe.tr(ps[:, 128 * i:128 * i + 128], On[:, 4 * h + i, :], ident, fr, on_t[h], up="onT")
                t = ac.act(Osb[:, cols], ps, ACT.Copy, t, osb_free[h], up="ont")
                ring.free(s, t)
                mid_t.append(t)
            for h in range(2):
                s, ps, fr = ring.take(1)
                for i in range(4 * h, 4 * h + 4):
                    t2 = pe.mm(ps[:, 128 * (i - 4 * h):128 * (i - 4 * h) + 128], Osb[:, 128 * i:128 * i + 128], wo, fr, mid_t[h],
                               w_in, up="oproj")
                osb_free[h] = t2
                on_t[h] = t2
                cols = slice(512 * h, 512 * h + 512)
                done.append(dv.tt(xf[:, cols], xf[:, cols], ps, ALU.add, t2, extra_free, up="res"))
                ring.free(s, done[h])
            return done

        def gates(G, ps, bias, tok, w_in, gfree, g):
            sc, m8, ix, ixf, d, p1, eq = g
            t = dv.tt(sc[:], ps.rearrange("p (i e) -> p i e", e=8), bias.unsqueeze(1).to_broadcast([128, NT, 8]), ALU.add,
                      tok, w_in, up="sc")
            r = t
            for i in range(NT):
                t = dv.op(lambda e, i=i: e.max(m8[:, i, :], sc[:, i, :]), t, up="gate")
            dv.wait(t)
            for i in range(NT):
                t2 = dv.op(lambda e, i=i: e.max_index(ix[:, i, :], m8[:, i, :], sc[:, i, :]), up="gate")
            t2 = dv.copy(ixf[:], ix[:, :, 0:2], t2, up="gate")
            t = dv.tt(d[:], m8[:, :, 1], m8[:, :, 0], ALU.subtract, up="gate")
            t = ac.act(d[:], d[:], ACT.Exp, t, up="ge")
            t = dv.ts(p1[:, 0, :], d[:], 1.0, None, ALU.add, ALU.bypass, t, up="gate")
            t = dv.op(lambda e: e.reciprocal(p1[:, 1, :], p1[:, 0, :]), t, up="gate")
            t = dv.tt(p1[:, 0, :], p1[:, 1, :], d[:], ALU.mult, t, up="gate")
            io = c("iota").unsqueeze(1).to_broadcast([128, NT, 8])
            for k in range(2):
                q = dv.tt(eq[:, k], io, ixf[:, :, k:k + 1].to_broadcast([128, NT, 8]), ALU.is_equal, t2, up="gate")
                q = dv.tt(eq[:, k], eq[:, k], p1[:, 1 - k, :].unsqueeze(2).to_broadcast([128, NT, 8]), ALU.mult, q, t, up="gate")
            return r, dv.tt(G[:], eq[:, 0], eq[:, 1], ALU.add, q, gfree, up="gate")

        def gate_bufs(reg, n):
            return (reg(f"gsc{n}", [128, NT, 8]), reg(f"gm8{n}", [128, NT, 8]), reg(f"gix{n}", [128, NT, 8], U32),
                    reg(f"gixf{n}", [128, NT, 2]), reg(f"gd{n}", [128, NT]), reg(f"gp{n}", [128, 2, NT]),
                    reg(f"geq{n}", [128, 2, NT, 8]))

        stage = Region(mid.at)
        WF0s = stage("WF0s", [128, NWF0])
        WBs = stage("WBs", [128, NWB])
        G = stage("G", [128, NT, 8])
        gb = gate_bufs(stage, 0)
        W1f = stage("W1f", [128, E * F])

        def compare(k, src, scale, square, tok):
            bar = (limit / scale) * (abs(limit) / scale if square else 1)
            t = dv.op(lambda e: e.tensor_reduce(fm[:, k:k + 1], src, AX, ALU.max), tok, up="flag")
            return dv.ts(flags[0:1, k:k + 1], fm[:, k:k + 1], bar, None, ALU.is_gt, ALU.bypass, t, up="flag")

        ctx_task(0)
        ctx_task(1)
        xn_t, xT_t = layernorm([x_in, x_in], None)
        qz0 = gp.op(lambda e: e.memset(Qz[0][:].bitcast(F32), 0.0))
        va1 = gp.op(lambda e: e.memset(Va[:], 1.0))
        c1 = gp.op(lambda e: e.memset(ctxT[96:97, :], 1.0))
        qz1 = gp.op(lambda e: e.memset(Qz[1][:].bitcast(F32), 0.0))
        selh_t = dv.copy(selh[:], c("selh"), c_in, up="const")
        rows = slice(0, 128)
        k0_t = direct([(rows, Ka[0][:])], w("k0"), None, c("ks"), c("kb"), wa_in, None, xT_t, xT)
        qa_t, ka_t, ka_used, kx_t, kx_used, fl_t = {}, {0: k0_t}, {}, {}, {}, {}
        qa_t[0] = direct(q0_parts, w("q0"), None, c("qs"), c("qb"), wa_in, qz0, xT_t, xT)
        s, ps, fr = ring.take()
        for i in range(NT):
            t = pe.mm(ps[:, 128 * i:128 * i + 128], xT[:, 128 * i:128 * i + 128], w("v"), fr, xT_t, wa_in, up="proj")
        va_t = dv.copy(Va[:].rearrange("p i h c -> p (i h) c")[:, :, 0:8], ps.rearrange("p (n c) -> p n c", c=8), t, va1,
                       up="proj")
        ring.free(s, va_t)

        def all_task(name, k):
            def go():
                s, ps, fr = ring.take()
                for a, b in chunks(T):
                    t = pe.mm(ps[:, a:b], w(name), xT[:, a:b], fr, xT_t, wa_in, up="proj")
                r, st_ = store_parts(ps, T, t, (KDa if k else QDa), (0, 1, 0, 0) if k else (0, 0, 1, None), f"sa{k}",
                                     square=k)
                ring.free(s, r)
                if k == 0:
                    qa_t[1] = [load_q(1, QDa, st_, None)] * 4
                    qa_t["st"] = st_
                else:
                    ka_t["st"] = st_
                    load_ka(1)
            return go

        def load_ka(g):
            ka_t[g] = [sp.dma(Ka[g % 2][:].bitcast(F32), KDa[g].rearrange("j r d c -> (j r d) c"), ka_t["st"], ka_used.get((g - 2, NT - 1)),
                              up=f"lka{g % 2}")]

        def next_a(g):
            def go():
                qa_t[g] = [load_q(g, QDa, qa_t["st"], q_free[g % 2])] * 4
                load_ka(g)
            return go

        def norm_flag():
            s, ps, fr = ring.take()
            for k in range(2):
                for a, b in chunks(T):
                    t = pe.mm(ps[32 * k:32 * k + 32, a:b], selh[:], sq[k][:, a:b], fr, sq_t[k], selh_t, up="nm")
            t = dv.op(lambda e: e.tensor_reduce(nr[:], ps[0:64, :], AX, ALU.max), t, up="nm")
            t = pe.tr(ps[0:1, 0:64], nr[:], ident[0:64, 0:64], t, up="nm")
            t = dv.copy(fl[:], ps[0:1, 0:64], t, up="nm")
            ring.free(s, t)
            t = dv.tt(fl[:, 0:16], fl[:, 0:16], fl[:, 32:48], ALU.mult, t, up="nm")
            fl_t[0] = compare(0, fl[:, 0:16], SC, True, t)

        def kx_task(m):
            def go():
                s, ps, fr = ring.take(1)
                n = min(512, S - 512 * m)
                t = pe.mm(ps[:, 0:n], wxs("k", 97), ctxT[0:97, 512 * m:512 * m + n], fr, ctx_t[m // 2], c1, wx_in, up="proj")
                r, st_ = store_parts(ps[:, 0:n], n, t, KDx[:, :, :, :, 512 * m:512 * m + n], (0, 1, 0, 0), f"sk{m}",
                                     mk[:, m:m + 1])
                ring.free(s, r)
                kx_t["st", m // 2] = [kx_t.get(("st", m // 2)), st_]
                if m % 2 or m == 12:
                    load_kx(0, m // 2)
            return go

        def load_kx(g, m):
            n = min(1024, S - 1024 * m)
            kx_t[g, m] = sp.dma(Kx[:, 1024 * m:1024 * m + n].bitcast(F32), KDx[g].rearrange("j r d c -> (j r d) c")[:, 1024 * m:1024 * m + n],
                                kx_t["st", m], ctx_t[6], kx_used.get((g - 1, min(8 * m + 7, NKT - 1))), up=f"lk{m}")

        def spread(tasks, slots, into):
            for i, task in enumerate(tasks):
                into.setdefault(slots[i * len(slots) // len(tasks)], []).append(task)

        all_task("q", 0)()
        all_task("k", 1)()
        norm_flag()
        fl_r = {0: load_flags(0)}
        tasks = {(1, 0): [next_a(2)], (2, 0): [next_a(3)]}
        rest = [lambda m=m: ctx_task(m) for m in range(2, 7)]
        kxs, v0s = [kx_task(m) for m in range(13)], [lambda m=m: v0_task(m) for m in range(9)]
        for i in range(13):
            rest += kxs[i:i + 1] + v0s[i:i + 1]
        spread(rest, [(g, kt) for g in range(4) for kt in range(8) ], tasks)
        attend8(NT, lambda kt: 128, lambda g: Ka[g % 2], lambda kt, h: Va[:, kt, h, :], lambda kt: va_t, qa_t,
                lambda g, kt: ka_t[g], tasks, ka_used, True)
        general("ga", p_region, 8, xT, 128, T, ga, 25, SC, True, On[:].rearrange("p i (h c) -> p (i h) c", c=8),
                False, fl_r[0], flat(ring.freed, on_t, p_free, o_free))
        x_t = a0_end = out_proj(w("o"), wa_in, xn_t)

        xn_t, xT_t = layernorm(x_t, None)
        bo_t = gp.tt(X[:], X[:], wxs("bo").unsqueeze(1).to_broadcast([128, NT, D]), ALU.add, xn_t, wx_in)
        qx_t = {0: direct(q0_parts, wxs("q0"), wxs("bq0"), c("qs"), c("qb"), wx_in, q_free[0], xT_t, xT)}

        def width(kt):
            return 128 if kt < KT else 4

        def all_q():
            s, ps, fr = ring.take()
            for a, b in chunks(T):
                t = pe.mm(ps[:, a:b], wxs("q"), xT[:, a:b], fr, xT_t, wx_in, up="proj")
            y = dv.ts(Qb[:], ps, wxs("bq"), None, ALU.add, ALU.bypass, t, qb_free[0], up="qb")
            ring.free(s, y)
            dv.op(lambda e: e.tensor_reduce(mq[:], Qb[:], AX, ALU.max, apply_absolute_value=True), y, up="mq")
            r, qx_t["st"] = store_parts(Qb[:], T, y, QDx, (0, 0, 1, None), "sq")
            qx_t[1] = [load_q(1, QDx, qx_t["st"], q_free[1])] * 4

        def dim_flag():
            s, ps, fr = ring.take()
            t = dv.op(lambda e: e.tensor_reduce(mkr[:], mk[:], AX, ALU.max), dv.now("mk"), up="nm")
            t = dv.tt(mkr[:], mkr[:], mq[:], ALU.mult, t, dv.now("mq"), up="nm")
            t = pe.mm(ps[0:1, 0:32], mkr[:], c("selh"), t, fr, up="nm")
            fl_t[1] = compare(1, ps[0:1, 0:32], SC, False, t)
            ring.free(s, fl_t[1])

        def prefetch():
            pre["wf0"] = sp.dma(WF0s[:], wf0, a0_end, part_free, up="wf0")
            pre["wb"] = sp.dma(WBs[:], wb, up="wb")
            pre["w1"] = sp.dma(W1f[:], f0w1, up="w1")

        pre = {}

        def next_x(g):
            def go():
                qx_t[g] = [load_q(g, QDx, qx_t["st"], q_free[g % 2])] * 4
            return go

        tasks = {(0, 3): [all_q], (0, 20): [dim_flag], (0, 24): [lambda: fl_r.update({1: load_flags(1)})],
                 (0, 30): [prefetch], (1, 0): [next_x(2)], (2, 0): [next_x(3)]}
        for g in range(3):
            for m in range(7):
                at = (g, 8 * m + 8) if m < 6 else (g + 1, 0)
                tasks.setdefault(at, []).append(lambda g=g, m=m: load_kx(g + 1, m))
        attend8(NKT, width, lambda g: Kx, lambda kt, h: V0[0:width(kt), kt, 9 * h:9 * h + 9],
                lambda kt: v0_t[kt // 6], qx_t, lambda g, kt: kx_t[g, kt // 8], tasks, kx_used, False)
        general("gx", kx_at, 8, ctxT, 97, S, gx, 25, SC, False, On[:].rearrange("p i (h c) -> p (i h) c", c=8),
                False, fl_r[1], flat(ring.freed, on_t, p_free, o_free))
        x_t = out_proj(wxs("o"), wx_in, bo_t)

        def transposed_gates(G, GT, tok, gt_free):
            s, ps, fr = ring.take()
            for i in range(NT):
                t = pe.tr(ps[0:8, 128 * i:128 * i + 128], G[:, i, :], ident, tok, fr, up="GT")
            t = ac.act(GT[:], ps[0:8, :], ACT.Copy, t, gt_free, up="GT")
            ring.free(s, t)
            return t

        f0b = Region(glob.at)
        H = [f0b(f"H{i}", [128, 4, T]) for i in range(2)]
        W2f = f0b("W2f", [128, E * F])
        GT = f0b("GT", [8, T])
        xh, xl = f0b("xh", [128, T], F32R), f0b("xl", [128, T], F32R)
        WS = [[f0b(f"ws{i}{k}", [128, F], F32R) for k in range(2)] for i in range(2)]
        w2_in = sp.dma(W2f[:], f0w2, p_free, q_free, v0_t[8], kx_used[3, NKT - 1], up="w2")
        x0_end = [p_free, q_free, kx_used[3, NKT - 1]]

        def wf(a, rows=128):
            return WF0s[0:rows, WF0[a][0]:WF0[a][1]]

        wf0_in, wb_in, w1_in = pre["wf0"], pre["wb"], pre["w1"]
        xn_t, xT_t = layernorm(x_t, None)

        def split(hi, lo_, src, tok, free, up):
            h = ac.act(hi, src, ACT.Copy, tok, free, up=up + "h")
            return dv.tt(lo_, src, hi.bitcast(F32), ALU.subtract, h, tok, free, up=up + "l")

        xs_t = [split(xh[:, a:b], xl[:, a:b], xT[:, a:b], xT_t[a // 512], x0_end, "x") for a, b in chunks(T)]
        h_free = [x0_end, x0_end]
        ws_free = [x0_end, x0_end]

        def three(ps, k, w_t, w_, col, fr, src, src_t, rows=slice(0, 128)):
            (wh, wl), (sh, sl) = w_, src
            for n, (p, q) in enumerate(((wh, sh), (wh, sl), (wl, sh))):
                for a, b in chunks(T):
                    t = pe.mm(ps[:, a:b], p[:, col], q[:, a:b], fr, src_t[a // 512], w_t, start=n == 0, stop=n == 2, up=k)
            return t

        def hidden(n, src, bias, w_in):
            b = n % 2
            w_t = split(WS[b][0][:], WS[b][1][:], src, w_in, ws_free[b], "w")
            for cc in range(4):
                s, ps, fr = ring.take()
                t = three(ps, "h", w_t, WS[b], slice(128 * cc, 128 * cc + 128), fr, (xh, xl), xs_t)
                r = ac.act(H[b][:, cc, :], ps, ACT.Relu, t, h_free[b], bias=bias[:, cc:cc + 1], up="hidden")
                ring.free(s, r)
            ws_free[b] = t
            return r

        def experts_out(e, h_t):
            s, ps, fr = ring.take()
            for i in range(NT):
                for cc in range(4):
                    t = pe.mm(ps[:, 128 * i:128 * i + 128], H[(e + 1) % 2][:, cc, 128 * i:128 * i + 128],
                              W2f[:, 512 * e + 128 * cc:512 * e + 128 * cc + 128], h_t, fr, w2_in, start=cc == 0,
                              stop=cc == 3, up="y")
            h_free[(e + 1) % 2] = t
            dv.wait(t, g_t, xn_t, x_t)
            toks = [dv.stt(X[:, i, :], ps[:, 128 * i:128 * i + 128], G[:, i, e:e + 1], X[:, i, :], ALU.mult, ALU.add,
                           up="y") for i in range(NT)]
            ring.free(s, toks[-1])
            return [toks[3], toks[7]]

        h_t = hidden(0, wf("rw1"), wf("rb1"), wf0_in)
        nxt = hidden(1, W1f[:, 0:F], WF0s[:, WF0["b1"][0]:WF0["b1"][0] + 4], w1_in)
        s, ps, fr = ring.take(1)
        rw2 = wf("rw2").rearrange("p (c e) -> p c e", e=8)
        for i in range(NT):
            for cc in range(4):
                t = pe.mm(ps[:, 8 * i:8 * i + 8], H[0][:, cc, 128 * i:128 * i + 128], rw2[:, cc, :], h_t, fr,
                          start=cc == 0, stop=cc == 3, up="sc")
        h_free[0] = t
        r, g_t = gates(G, ps[:, 0:64], wf("rb2"), t, wf0_in, None, gb)
        ring.free(s, r)
        for e in range(E):
            h_t = nxt
            if e < E - 1:
                nxt = hidden(e + 2, W1f[:, F * (e + 1):F * (e + 2)],
                             WF0s[:, WF0["b1"][0] + 4 * e + 4:WF0["b1"][0] + 4 * e + 8], w1_in)
            if e == 1:
                gt_t = transposed_gates(G, GT, g_t, x0_end)
                s, ps, fr = ring.take()
                for i in range(NT):
                    t = pe.mm(ps[:, 128 * i:128 * i + 128], GT[:, 128 * i:128 * i + 128], wf("b2", 8), fr, gt_t, wf0_in,
                              up="b2")
                r = dv.tt(xf, xf, ps, ALU.add, t, x_t, up="res")
                x_t = [r, r]
                ring.free(s, r)
            x_t = experts_out(e, h_t)
        f0_pe = h_free[E % 2]

        b1 = Region(glob.at)
        lat = b1("lat", [33, T])
        QK = b1("QK", [128, NT, 32, 8])
        QR = b1("QR", [128, NT, 32, 8])
        Vt = b1("Vt", [128, NT, D])
        R1 = b1("R1", [128, NT, 32, 4])
        R2 = b1("R2", [128, NT, 32, 4])
        pr = [b1(f"pr{i}", [128, 2048]) for i in range(3)]
        att = b1("att", [128, NT, 16, 16])
        mx = b1("mx", [128, NT, 16])
        sm = b1("sm", [128, NT, 16])
        on1 = b1("on1", [1, 128])
        f0_end = [f0_pe, x_t, h_free]

        def wbs(a, rows=128):
            return WBs[0:rows, WB[a][0]:WB[a][1]]

        xn_t, xT_t = layernorm(x_t, None)
        lat1 = gp.op(lambda e: e.memset(lat[32:33, :], 1.0), f0_end)
        one_t = gp.op(lambda e: e.memset(on1[:], 1.0))
        l_t = []
        for h in range(2):
            s, ps, fr = ring.take(1)
            a, b = 512 * h, 512 * h + 512
            t = pe.mm(ps[0:32, :], wbs("down"), xT[:, a:b], fr, xT_t[h], wb_in, up="proj")
            l_t.append(ac.act(lat[0:32, a:b], ps[0:32, :], ACT.Identity, t, f0_end, bias=wbs("bdown", 32), up="proj"))
            ring.free(s, l_t[h])
        q_t, k_t = [], []
        for h in range(2):
            s, ps, fr = ring.take(1)
            for i in range(4):
                o = ps[:, 128 * i:128 * i + 128]
                pe.mm(o, xT[:, 512 * h + 128 * i:512 * h + 128 * i + 128], wbs("q"), fr, xT_t[h], wb_in, stop=False)
                t = pe.mm(o, on1[:], wbs("bq", 1), one_t, start=False, up="proj")
            q_t.append(ac.act(QK[:, 4 * h:4 * h + 4, 0:16, :].rearrange("p i h d -> p i (h d)"),
                              ps.rearrange("p (i c) -> p i c", i=4), ACT.Copy, t, f0_end, up="proj"))
            ring.free(s, q_t[h])
            s, ps, fr = ring.take()
            for i in range(4):
                t = pe.mm(ps[:, 256 * i:256 * i + 256], lat[:, 512 * h + 128 * i:512 * h + 128 * i + 128], wbs("up", 33),
                          fr, l_t[h], lat1, up="proj")
            p3 = ps.rearrange("p (i c) -> p i c", i=4)
            k = ac.act(QK[:, 4 * h:4 * h + 4, 16:32, :].rearrange("p i h d -> p i (h d)"), p3[:, :, 0:128], ACT.Copy, t,
                       up="proj")
            k_t.append(ac.act(Vt[:, 4 * h:4 * h + 4, :], p3[:, :, 128:256], ACT.Copy, up="proj"))
            ring.free(s, k_t[h])

        def rope(lane, h, tiles):
            n = tiles.stop - tiles.start
            cs = {k: c(k).rearrange("p (i f) -> p i f", i=NT)[:, tiles].unsqueeze(2).to_broadcast([128, n, 32, 4])
                  for k in ("cos", "sin")}
            x1, x2 = QK[:, tiles, :, 0:4], QK[:, tiles, :, 4:8]
            t = None
            for d, (a, b, o) in enumerate((("cos", "sin", ALU.subtract), ("sin", "cos", ALU.add))):
                t1 = lane.tt(R1[:, tiles], x1, cs[a], ALU.mult, q_t[h], k_t[h], f0_end, c_in, t, up="rope")
                t2 = lane.tt(R2[:, tiles], x2, cs[b], ALU.mult, up="rope")
                t = lane.tt(QR[:, tiles, :, 4 * d:4 * d + 4], R1[:, tiles], R2[:, tiles], o, t1, t2, up="rope")
            return t

        ON_POOL1, ON_POOL2 = (1, 3, 5, 7), (2, 5)
        ON_DVE1, ON_DVE2 = (0,), (3, 6, 7)
        r_t = {}
        for tiles, lane, h in ((slice(0, 2), dv, 0), (slice(2, 4), gp, 0), (slice(4, 6), dv, 1), (slice(6, 8), gp, 1)):
            t = rope(lane, h, tiles)
            for i in range(tiles.start, tiles.stop):
                r_t[i] = t
        pr_free = [None, None, None]
        npr = [0]
        bcast = lambda ap: ap

        def product(lane, out4, a, b, *tok):
            k = npr[0] % 3
            npr[0] += 1
            t = lane.tt(out4(pr[k]), a, b, ALU.mult, pr_free[k], *tok, up="prod")
            return k, t

        def sums(k, t, on_dve, dst, view, n, slices):
            if on_dve:
                pr_free[k] = dv.op(lambda e: e.tensor_reduce(dst, view(pr[k]), AX, ALU.add), t, up="red")
                return dst, pr_free[k], None
            s, ps, fr = ring.take(1)
            m = view(pr[k])
            for j in range(slices):
                tt_ = pe.mm(ps[:, 0:n], ident, m[:, :, :, j], fr, t, start=j == 0, stop=j == slices - 1, up="red")
            pr_free[k] = tt_
            return ps[:, 0:n].rearrange("p (a b) -> p a b", a=16), tt_, s

        state = {}

        def scores(i):
            v = lambda p: p[:].rearrange("p (h g d) -> p h g d", h=16, g=16)
            k, t = product(gp if i in ON_POOL1 else dv, v, QR[:, i, 0:16, :].unsqueeze(2).to_broadcast([128, 16, 16, 8]),
                           QR[:, i, 16:32, :].unsqueeze(1).to_broadcast([128, 16, 16, 8]), r_t[i])
            state[i] = sums(k, t, i in ON_DVE1, att[:, i], v, 256, 8)

        def softmax(i):
            a, t, s = state[i]
            t = dv.op(lambda e: e.tensor_reduce(mx[:, i], a, AX, ALU.max), t, up="soft")
            t = dv.tt(att[:, i], a, mx[:, i].unsqueeze(2).to_broadcast([128, 16, 16]), ALU.subtract, t, up="soft")
            if s is not None:
                ring.free(s, t)
            state[i] = ac.act(att[:, i], att[:, i], ACT.Exp, t, scale=SC, up="att")

        def values(i):
            v = lambda p: p[:].rearrange("p (h d g) -> p h d g", h=16, d=8)
            k, t = product(gp if i in ON_POOL2 else dv, v, att[:, i].unsqueeze(2).to_broadcast([128, 16, 8, 16]),
                           Vt[:, i].rearrange("p (g d) -> p d g", d=8).unsqueeze(1).to_broadcast([128, 16, 8, 16]), state[i])
            t2 = dv.op(lambda e: e.tensor_reduce(sm[:, i], att[:, i], AX, ALU.add), state[i], up="soft")
            t2 = dv.op(lambda e: e.reciprocal(sm[:, i], sm[:, i]), t2, up="soft")
            state[i] = (t2,) + sums(k, t, i in ON_DVE2, mx8[:, i], v, 128, 16)

        def outs(i):
            t2, a, t, s = state[i]
            on_t[i // 4] = dv.tt(On[:, i].rearrange("p (h d) -> p h d", d=8), a,
                                 sm[:, i].unsqueeze(2).to_broadcast([128, 16, 8]), ALU.mult, t, t2, on_t[i // 4], up="on")
            if s is not None:
                ring.free(s, on_t[i // 4])

        mx8 = b1("mx8", [128, NT, 16, 8])
        for i in range(NT + 3):
            for k, f in enumerate((scores, softmax, values, outs)):
                if 0 <= i - k < NT:
                    f(i - k)
        bo_t = gp.tt(X[:], X[:], wbs("bout").unsqueeze(1).to_broadcast([128, NT, D]), ALU.add, xn_t, wb_in)
        x_t = out_proj(wbs("out"), wb_in, bo_t)
        b1_end = [x_t, osb_free]

        A, B = slice(0, 64), slice(64, 128)
        NPY = 8
        x1h = Region(glob.at + 1024 * 67)
        Py = [x1h(f"Py{i}", [128, T]) for i in range(NPY)]
        WYs = x1h("WYs", [128, NWY])
        K1 = [x1h(f"K1{i}", [128, 2, 512], F32R) for i in range(2)]
        V1 = [x1h(f"V1{i}", [128, 512]) for i in range(2)]
        A1_at = x1h.at
        A1, A3 = [x1h(f"A{k}", [128, E * F]) for k in (1, 3)]
        x1l = Region(glob.at)
        A2 = x1l("A2", [128, E * F])
        y_region = x1l.at
        Q1 = [x1l(f"Q1{i}", [128, 2, T], F32R) for i in range(2)]
        Q2 = [x1l(f"Q2{i}", [128, T], F32R) for i in range(2)]
        acc = [x1l(f"acc{i}", [128, T]) for i in range(4)]
        rsy = [x1l(f"rsy{i}", [128, 16]) for i in range(2)]
        sqq = x1l("sqq", [128, T], BF16)
        sqk = [x1l(f"sqk{i}", [128, 512], BF16) for i in range(4)]
        sel2 = x1l("sel2", [128, 32], BF16)
        mqy = x1l("mqy", [64, 8])
        mky = x1l("mky", [128, 32])
        mkp = x1l("mkp", [128, 8])
        nf = x1l("nf", [8, 2, 32])
        assert x1l.at <= glob.at + 1024 * 67
        wy_in = sp.dma(WYs[:], wy, f0_end, up="wy")
        a1_in = sp.dma(A1[:], f1w1, b1_end, up="a1")
        a3_in = sp.dma(A3[:], f1w3, up="a3")
        a2_in = sp.dma(A2[:], f1w2, up="a2")
        sqq_free, sqk_free, sqk_t = [b1_end], [b1_end] * 4, {}
        q1_sq, k1_sq = [None, None], [None, None]

        def wys(a, lo, n, r0=0, r1=128):
            return WYs[r0:r1, WY[a][0] + lo:WY[a][0] + lo + n]

        xn_t, xT_t = layernorm(x_t, None)
        sel2_t = dv.copy(sel2[:], c("sel2"), b1_end, up="const")
        mky0 = dv.op(lambda e: e.memset(mky[:], 0.0), up="const")
        x_t = gp.tt(X[:], X[:], wys("b", 0, 128).unsqueeze(1).to_broadcast([128, NT, D]), ALU.add, xn_t, wy_in)
        pf = [b1_end] * NPY
        acc_free = [b1_end, b1_end]
        q1_free = [b1_end, b1_end]
        osb1_free = [b1_end, b1_end]
        oy_free = [[b1_end, b1_end]]
        Y = On
        y_t = [b1_end, b1_end]
        NCH = 13
        q_ready, kv_ready, norms = {}, {}, {}

        def kv_chunk(p, m):
            b = (NCH * p + m) % 2
            n = min(512, S - 512 * m)
            nt = -(-n // 128)
            s, ps, fr = ring.take(1)
            t = pe.mm(ps[:, 0:n], wys("kv", 128 * p, 128, 0, 96), ctxT[0:96, 512 * m:512 * m + n], fr, wy_in, up="proj")
            k = K1[b]
            f = [k1_free[b], k1_sq[b]]
            h1 = ac.act(k[A, 0, 0:n], ps[A, 0:n], ACT.Copy, t, f, up="kh")
            h2 = ac.act(k[B, 1, 0:n], ps[B, 0:n], ACT.Copy, up="kh")
            dv.tt(k[B, 0, 0:n], ps[A, 0:n], k[A, 0, 0:n].bitcast(F32), ALU.subtract, h1, f)
            r = dv.tt(k[A, 1, 0:n], ps[B, 0:n], k[B, 1, 0:n].bitcast(F32), ALU.subtract, h2, up="k")
            ring.free(s, r)
            s, ps, fr = ring.take(1)
            for i in range(nt):
                w_ = min(128, n - 128 * i)
                tv = pe.mm(ps[0:w_, 128 * i:128 * i + 128], ctxT[0:96, 512 * m + 128 * i:512 * m + 128 * i + w_],
                           wys("kv", 1024 + 128 * p, 128, 0, 96), fr, up="proj")
            if n == 512:
                rv = dv.copy(V1[b][:], ps, tv, v1_free[b], up="v")
            else:
                dv.copy(V1[b][:, 0:256], ps[:, 0:256], tv, v1_free[b])
                rv = dv.copy(V1[b][0:4, 256:384], ps[0:4, 256:384], up="v")
            ring.free(s, rv)
            kv_ready[p, m] = (r, rv)
            for rows, hh in ((A, 0), (B, 1)):
                t = gp.tt(sqk[m % 4][rows, 0:n], k[rows, hh, 0:n].bitcast(F32), k[rows, hh, 0:n].bitcast(F32), ALU.mult,
                          h1, h2, sqk_free[m % 4])
            sqk_t[m % 4] = k1_sq[b] = t

        k1_free, v1_free = [f0_end, f0_end], [f0_end, f0_end]
        kv_chunk(0, 0)

        def q_pair(p):
            q1, q2 = Q1[p % 2], Q2[p % 2]
            s, ps, fr = ring.take()
            for a, b in chunks(T):
                t = pe.mm(ps[:, a:b], wys("q", 128 * p, 128), xT[:, a:b], fr, xT_t[a // 512], wy_in, up="proj")
            f = [q1_free[p % 2], q1_sq[p % 2]]
            h1 = ac.act(q1[A, 0, :], ps[A, :], ACT.Copy, t, f, up="qh")
            h2 = ac.act(q1[B, 1, :], ps[B, :], ACT.Copy, up="qh")
            dv.tt(q2[A, :], ps[A, :], q1[A, 0, :].bitcast(F32), ALU.subtract, h1, f)
            r = dv.tt(q2[B, :], ps[B, :], q1[B, 1, :].bitcast(F32), ALU.subtract, h2, up="q")
            ring.free(s, r)
            dv.copy(q1[B, 0, :], q1[A, 0, :].bitcast(F32))
            q_ready[p] = dv.copy(q1[A, 1, :], q1[B, 1, :].bitcast(F32), up="q")
            for rows, hh in ((A, 0), (B, 1)):
                t = gp.tt(sqq[rows, :], q1[rows, hh, :].bitcast(F32), q1[rows, hh, :].bitcast(F32), ALU.mult, h1, h2,
                          sqq_free[0])
            q1_sq[p % 2] = t

        def q_norm(p):
            s, ps, fr = ring.take(1)
            for a, b in chunks(T):
                r0 = 32 * (a // 512)
                t2 = pe.mm(ps[r0:r0 + 32, :], sel2[:], sqq[:, a:b], q1_sq[p % 2], fr, sel2_t, up="nq")
            sqq_free[0] = t2
            ring.free(s, dv.op(lambda e: e.tensor_reduce(mqy[:, p:p + 1], ps[0:64, :], AX, ALU.max), t2, up="mqy"))

        def k_norm(p, ms):
            s, ps, fr = ring.take(1)
            for j, m in enumerate(ms):
                n = min(512, S - 512 * m)
                t = pe.mm(ps[32 * j:32 * j + 32, 0:n], sel2[:], sqk[m % 4][:, 0:n], sqk_t[m % 4], fr, sel2_t, up="nk")
                sqk_free[m % 4] = t
            r_ = 32 * len(ms)
            col = 4 * p + ms[0] // 4
            ring.free(s, dv.op(lambda e: e.tensor_reduce(mky[0:r_, col:col + 1], ps[0:r_, 0:n], AX, ALU.max), t, mky0,
                               up="mky"))

        def norm_flag1():
            s, ps, fr = ring.take()
            t = dv.op(lambda e: e.tensor_reduce(mkp[:], mky[:].rearrange("p (a b) -> p a b", b=4), AX, ALU.max),
                      dv.now("mky"), up="nm")
            pe.tr(ps[0:8, 0:128], mkp[:], ident, t, fr)
            t = pe.tr(ps[0:8, 128:192], mqy[:], ident[0:64, 0:64], dv.now("mqy"), up="nm")
            dv.op(lambda e: e.tensor_reduce(nf[:, 0, :], ps[0:8, 0:128].rearrange("p (t c) -> p c t", c=32), AX, ALU.max), t)
            t = dv.op(lambda e: e.tensor_reduce(nf[:, 1, :], ps[0:8, 128:192].rearrange("p (t c) -> p c t", c=32), AX,
                                                ALU.max), up="nm")
            t = dv.tt(nf[:, 0, 0:2], nf[:, 0, 0:2], nf[:, 1, 0:2], ALU.mult, t, up="nm")
            t = dv.op(lambda e: e.tensor_reduce(nr[0:8, :], nf[:, 0, 0:2], AX, ALU.max), t, up="nm")
            t = pe.tr(ps[0:1, 512:520], nr[0:8, :], ident[0:8, 0:8], t, up="nm")
            fl_t[2] = compare(2, ps[0:1, 512:520], 0.125, True, t)
            ring.free(s, fl_t[2])

        def finish_sums(p, acc_t):
            s, ps, fr = ring.take(1)
            for h in range(2):
                for i in range(NT):
                    t = pe.mm(ps[:, 8 * h + i:8 * h + i + 1], acc[2 * (p % 2) + h][:, 128 * i:128 * i + 128], c("one"),
                              acc_t, fr, up="sum")
            acc_free[p % 2] = t
            norms[p] = dv.op(lambda e: e.reciprocal(rsy[p % 2][:], ps[:, 0:16]), t, y_t, up="rsy")
            ring.free(s, norms[p])

        def finish_head(p, h, osb_t):
            s, ps, fr = ring.take()
            for i in range(NT):
                t = pe.mm(ps[:, 128 * i:128 * i + 128], Osb[64 * h:64 * h + 64, 128 * i:128 * i + 128],
                          wys("out", 128 * p, 128, 64 * h, 64 * h + 64), osb_t[i // 4], fr, up="yp")
            dv.wait(t, norms[p], y_t)
            for i in range(NT):
                a_, b_ = ps[:, 128 * i:128 * i + 128], rsy[p % 2][:, 8 * h + i:8 * h + i + 1]
                if (p, h) == (0, 0):
                    y_t[i // 4] = dv.ts(Y[:, i, :], a_, b_, None, ALU.mult, ALU.bypass, up="y1")
                else:
                    y_t[i // 4] = dv.stt(Y[:, i, :], a_, b_, Y[:, i, :], ALU.mult, ALU.add, up="y1")
            ring.free(s, y_t[1])
            if h == 1:
                osb1_free[0] = osb1_free[1] = t

        todo = []
        pend = []
        un = 0
        q_pair(0)
        q_norm(0)
        for p in range(8):
            ac_t = [None, None]
            for kt in range(NKT):
                m, i = divmod(kt, 4)
                kw = 128 if kt < KT else 4
                b = (NCH * p + m) % 2
                k, (kt_, vt_) = K1[b], kv_ready[p, m]
                q1, q2 = Q1[p % 2], Q2[p % 2]
                sA, pA, fA = ring.take()
                sB, pB, fB = ring.take()
                cols = slice(128 * i, 128 * i + kw)
                for a, bb in chunks(T):
                    pe.mm(pA[0:kw, a:bb], k[:, 0, cols], q1[:, 0, a:bb], fA, kt_, q_ready[p], start=True, stop=False)
                for a, bb in chunks(T):
                    pe.mm(pB[0:kw, a:bb], k[:, 1, cols], q1[:, 1, a:bb], fB, start=True, stop=False)
                for a, bb in chunks(T):
                    tA = pe.mm(pA[0:kw, a:bb], k[A, 0, cols], q2[A, a:bb], start=False, stop=True, up="sA")
                    tB = pe.mm(pB[0:kw, a:bb], k[B, 1, cols], q2[B, a:bb], start=False, stop=True, up="sA")
                k1_free[b] = tB
                q1_free[p % 2] = tB
                es = []
                for h, (s, ps, t) in enumerate(((sA, pA, tA), (sB, pB, tB))):
                    pb = un % NPY
                    un += 1
                    t = ac.act(Py[pb][0:kw, :], ps[0:kw, :], ACT.Exp, t, pf[pb], scale=0.125, up="ey")
                    ring.free(s, t)
                    ac_ = acc[2 * (p % 2) + h]
                    if kt == 0:
                        ac_t[h] = dv.copy(ac_[:], Py[pb][:], t, acc_free[p % 2], up="acc")
                    else:
                        ac_t[h] = dv.tt(ac_[0:kw, :], ac_[0:kw, :], Py[pb][0:kw, :], ALU.add, t, ac_t[h], up="acc")
                    es.append((pb, t, ac_t[h]))

                def pv(p=p, kt=kt, i=i, kw=kw, b=b, es=es, vt_=vt_):
                    last = []
                    for a, bb in chunks(T):
                        for h in range(2):
                            t = pe.mm(O[64 * h:64 * h + 64, a:bb], V1[b][0:kw, 128 * i + 64 * h:128 * i + 64 * h + 64],
                                      Py[es[h][0]][0:kw, a:bb], es[h][1], vt_, oy_free[0][a // 512], start=kt == 0,
                                      stop=kt == NKT - 1, skip=True, up="pvy")
                        last.append(t)
                    v1_free[b] = t
                    for pb, _, t2 in es:
                        pf[pb] = [t, t2]
                    if kt == NKT - 1:
                        o = [ac.act(Osb[:, a:bb], O[:, a:bb], ACT.Copy, last[a // 512], osb1_free[a // 512], up="osb")
                             for a, bb in chunks(T)]
                        oy_free[0] = o
                        acc_t = [es[0][2], es[1][2]]
                        todo.extend([lambda: finish_sums(p, acc_t), lambda: finish_head(p, 0, o),
                                     lambda: finish_head(p, 1, o)])

                pend.append(pv)
                if len(pend) > 1:
                    pend.pop(0)()
                if i == 0 and (p, m) != (7, NCH - 1):
                    kv_chunk(*((p, m + 1) if m < NCH - 1 else (p + 1, 0)))
                elif todo:
                    todo.pop(0)()
                if kt in (19, 35, 47):
                    todo.append(lambda p=p, n=(kt // 16 - 1) * 4: k_norm(p, range(n, n + 4)))
                if kt == 2 and p > 0:
                    todo.append(lambda p=p: k_norm(p - 1, [12]))
                if kt == 40 and p < 7:
                    todo.append(lambda p=p: q_pair(p + 1))
                    todo.append(lambda p=p: q_norm(p + 1))
        pend.pop(0)()
        k_norm(7, [12])
        norm_flag1()
        fl_r[2] = load_flags(2)
        for f in todo:
            f()
        general("gy", y_region, 64, ctxT, 97, S, gy, 321, 0.125, False, On[:], True, fl_r[2],
                flat(ring.freed, y_t, pf, acc_free, oy_free, osb1_free))
        x_t = [dv.tt(xf[:, a:b], xf[:, a:b], Y[:].rearrange("p i d -> p (i d)")[:, a:b], ALU.add, y_t, x_t, up="res")
               for a, b in chunks(T)]
        x1_end = [pf, acc_free, osb1_free, y_t]

        f1 = Region(y_region)
        H1 = [f1(f"H1{i}", [128, 4, T]) for i in range(2)]
        xe = f1("xe", [128, T])
        XE = [[f1(f"xe{i}{k}", [128, T], F32R) for k in range(2)] for i in range(2)]
        WT = [[f1(f"wt{i}{k}", [128, 2, F], F32R) for k in range(2)] for i in range(2)]
        th = [f1(f"th{i}", [128, T]) for i in range(2)]
        G1 = f1("G1", [128, NT, 8])
        GH, GL = f1("GH", [8, T], F32R), f1("GL", [8, T], F32R)
        id8 = f1("id8", [8, 8], F32R)
        gb1 = gate_bufs(f1, 1)
        assert f1.at <= A1_at, (f1.at, A1_at)
        xn_t, xT_t = layernorm(x_t, None)
        x_t = dv.tt(xf, xf, xn[:].rearrange("p i d -> p (i d)"), ALU.add, xn_t, x_t, up="res")
        s, ps, fr = ring.take(1)
        for i in range(NT):
            t = pe.mm(ps[:, 8 * i:8 * i + 8], xT[:, 128 * i:128 * i + 128], WF1s[:, 0:8], fr, xT_t[i // 4], wf1_in, up="lg")
        id8_t = dv.copy(id8[:], ident[0:8, 0:8], x1_end, up="const")
        r, g_t = gates(G1, ps[:, 0:64], WF1s[:, 8:16], t, wf1_in, x1_end, gb1)
        ring.free(s, r)
        s, ps, fr = ring.take()
        for i in range(NT):
            t = pe.tr(ps[0:8, 128 * i:128 * i + 128], G1[:, i, :], ident, g_t, fr, up="GT")
        t = ac.act(GH[:], ps[0:8, :], ACT.Copy, t, x1_end, up="GH")
        gt_t = dv.tt(GL[:], ps[0:8, :], GH[:].bitcast(F32), ALU.subtract, t, up="GL")
        ring.free(s, gt_t)
        xe_free, xeb_free, wt_free, th_free, h_free = None, [None, None], [None, None], [None, None], [None, None]
        wt_t, xe_t = {}, {}

        def weights(e):
            b = e % 2
            for k, (src, w_in) in enumerate(((A1, a1_in), (A3, a3_in))):
                wt_t[e, k] = split(WT[b][0][:, k, :], WT[b][1][:, k, :], src[:, F * e:F * e + F], w_in,
                                   [wt_free[b], x1_end], "wt")

        def tokens_in(e):
            nonlocal xe_free
            b = e % 2
            s, ps, fr = ring.take()
            for g_, st_ in ((GH, True), (GL, False)):
                for a, bb in chunks(T):
                    t = pe.mm(ps[:, a:bb], id8[:, e:e + 1].to_broadcast([8, 128]), g_[:, a:bb], fr, gt_t, id8_t, start=st_,
                              stop=not st_, up="gb")
            t = dv.tt(xe[:], xT[:], ps, ALU.mult, t, xT_t, xe_free, x1_end, up="xe")
            ring.free(s, t)
            xe_free = split(XE[b][0][:], XE[b][1][:], xe[:], t, xeb_free[b], "xe")
            xe_t[e] = [xe_free, xe_free]

        nth = 0
        weights(0)
        tokens_in(0)
        for e in range(E + 1):
            if e < E:
                b = e % 2
                for cc in range(4):
                    col = slice(128 * cc, 128 * cc + 128)
                    su, pu, fu = ring.take()
                    tu = three(pu, "u", wt_t[e, 0], (WT[b][0][:, 0, :], WT[b][1][:, 0, :]), col, fu, XE[b], xe_t[e])
                    sv, pv_, fv = ring.take()
                    tv = three(pv_, "u", wt_t[e, 1], (WT[b][0][:, 1, :], WT[b][1][:, 1, :]), col, fv, XE[b], xe_t[e])
                    k = nth % 2
                    nth += 1
                    t = ac.act(th[k][:], pu, ACT.Tanh, tu, th_free[k], x1_end, scale=0.5, up="hidden")
                    t = dv.stt(th[k][:], th[k][:], 1.0, pu, ALU.add, ALU.mult, t, up="hidden")
                    ring.free(su, t)
                    h_t = dv.stt(H1[b][:, cc, :], th[k][:], 0.5, pv_, ALU.mult, ALU.mult, t, tv, h_free[b], up="hidden")
                    th_free[k] = h_t
                    ring.free(sv, h_t)
                    if cc == 1 and e < E - 1:
                        weights(e + 1)
                    if cc == 2 and e < E - 1:
                        tokens_in(e + 1)
                xeb_free[b] = wt_free[b] = tv
                now = (e, h_t)
            if e:
                e_, h_t = prev
                s, ps, fr = ring.take()
                for i in range(NT):
                    for cc in range(4):
                        t = pe.mm(ps[:, 128 * i:128 * i + 128], H1[e_ % 2][:, cc, 128 * i:128 * i + 128],
                                  A2[:, 512 * e_ + 128 * cc:512 * e_ + 128 * cc + 128], h_t, fr, a2_in,
                                  start=cc == 0, stop=cc == 3, up="y")
                h_free[e_ % 2] = t
                x_t = dv.tt(xf, xf, ps, ALU.add, t, x_t, up="res")
                ring.free(s, x_t)
            prev = now

        o_t = sp.dma(out.rearrange("a (i p) d -> p (a i) d", p=128), X[:], x_t, up="out")
        sp.wait(o_t, *stores)

        with nc.Block() as block:
            @block.tensor
            def _(e):
                for f in pe.queue:
                    f(e)

            @block.scalar
            def _(e):
                for f in ac.queue:
                    f(e)

            @block.vector
            def _(e):
                for f in dv.queue:
                    f(e)

            @block.gpsimd
            def _(e):
                for f in gp.queue:
                    f(e)

            @block.sync
            def _(e):
                for f in sp.queue:
                    f(e)


def constants():
    c = np.zeros((128, NCST), np.float32)

    def put(name, v):
        c[:, CST[name][0]:CST[name][1]] = v

    q = np.arange(128)
    r = q % 32
    put("id", np.eye(128))
    low = (r >= 16) & (r < 24)
    put("qs", np.where(low, -1, 1)[:, None])
    put("qb", np.where(low, 1, 0)[:, None])
    low = (r >= 8) & (r < 16)
    put("ks", np.where(low, -1, 1)[:, None])
    put("kb", np.where(low, 1, 0)[:, None])
    put("mh", -0.5)
    inv = (1.0 / 10000.0 ** (np.arange(0, 8, 2, dtype=np.float32) / np.float32(8))).astype(np.float32)
    freq = np.arange(T, dtype=np.float32)[:, None] * inv[None]
    freq = freq.reshape(NT, 128, 4).transpose(1, 0, 2).reshape(128, NT * 4)
    put("cos", np.cos(freq))
    put("sin", np.sin(freq))
    put("iota", np.arange(8)[None])
    put("one", 1)
    put("selh", q[:, None] // 8 == np.arange(32)[None])
    put("sel2", q[:, None] // 64 == np.arange(32)[None])
    g = np.zeros((128, T + NT), np.float32)
    g[:, :T] = np.arange(T)[None]
    g[:, T:] = q[:, None] + 128 * np.arange(NT)[None]
    return c, g


def layout(I):
    A = {"x": I["x"], "ctx_in": I["ctx_768"]}
    A["cst"], A["gc"] = constants()

    def z(*s):
        return np.zeros(s, np.float32)

    def rep(w):
        o = z(w.shape[0], 4, 32)
        v = w[:, 0:32].reshape(-1, 4, 8)
        for k in range(3):
            o[..., 8 * k:8 * k + 8] = v
        return o.reshape(w.shape[0], 128)

    def put(dst, table, name, v):
        dst[0:v.shape[0], table[name][0]:table[name][1]] = v

    w = A["wa"] = z(128, NWA)
    put(w, WA, "q0", rep(I["L0_attn_w_q"].T))
    put(w, WA, "k0", rep(I["L0_attn_w_k"].T))
    for n in "qkvo":
        put(w, WA, n, I["L0_attn_w_" + n].T)
    w = A["wx"] = z(128, NWX)
    put(w, WX, "q0", rep(I["L0_xattn_wq"]))
    put(w, WX, "q", I["L0_xattn_wq"])
    put(w, WX, "k", I["L0_xattn_wk"])
    w[96, WX["k"][0]:WX["k"][1]] = I["L0_xattn_bk"]
    v = z(97, 16, 9)
    v[:96, :, :8] = I["L0_xattn_wv"].reshape(96, 16, 8)
    v[96, :, :8] = I["L0_xattn_bv"].reshape(16, 8)
    v[96, :, 8] = 1
    put(w, WX, "v", v.reshape(97, 144))
    put(w, WX, "o", I["L0_xattn_wo"])
    put(w, WX, "bq0", rep(I["L0_xattn_bq"][None]).T)
    put(w, WX, "bq", I["L0_xattn_bq"][:, None])
    w[:, WX["bo"][0]:WX["bo"][1]] = I["L0_xattn_bo"][None]

    w = A["wf0"] = z(128, NWF0)
    put(w, WF0, "rw1", I["L0_ffn_rw1"])
    put(w, WF0, "rb1", I["L0_ffn_rb1"].reshape(4, 128).T)
    put(w, WF0, "rw2", I["L0_ffn_rw2"].reshape(4, 128, 8).transpose(1, 0, 2).reshape(128, 32))
    w[:, WF0["rb2"][0]:WF0["rb2"][1]] = I["L0_ffn_rb2"][None]
    put(w, WF0, "b1", I["L0_ffn_b1"].reshape(8, 4, 128).transpose(2, 0, 1).reshape(128, 32))
    put(w, WF0, "b2", I["L0_ffn_b2"])
    A["f0w1"] = I["L0_ffn_W1"].transpose(1, 0, 2).reshape(128, 4096)
    A["f0w2"] = I["L0_ffn_W2"].reshape(8, 4, 128, 128).transpose(2, 0, 1, 3).reshape(128, 4096)

    w = A["wb"] = z(128, NWB)
    h = np.arange(16)[:, None] * 16 + np.arange(8)[None]
    perm = np.concatenate([h, h + 8]).reshape(-1)
    put(w, WB, "q", I["L1_attn_Wq"])
    put(w, WB, "down", I["L1_attn_Wdown"])
    put(w, WB, "up", I["L1_attn_Wup"][:, perm])
    put(w, WB, "out", I["L1_attn_Wout"])
    w[:, WB["bq"][0]:WB["bq"][1]] = I["L1_attn_bq"][None]
    w[32, WB["up"][0]:WB["up"][1]] = I["L1_attn_bup"][perm]
    w[:, WB["bout"][0]:WB["bout"][1]] = I["L1_attn_bout"][None]
    put(w, WB, "bdown", I["L1_attn_bdown"][:, None])

    w = A["wy"] = z(128, NWY)
    put(w, WY, "q", I["L1_xattn_w_q"])
    put(w, WY, "kv", I["L1_xattn_w_kv"])
    put(w, WY, "out", I["L1_xattn_w_out"].reshape(8, 128, 128).transpose(1, 0, 2).reshape(128, 1024))
    w[:, WY["b"][0]:WY["b"][1]] = I["L1_xattn_b_out"][None]

    w = A["wf1"] = z(128, NWF1)
    put(w, WF1, "g", I["L1_ffn_Wg"])
    w[:, WF1["bg"][0]:WF1["bg"][1]] = I["L1_ffn_bg"][None]
    A["f1w1"] = I["L1_ffn_W1"].transpose(1, 0, 2).reshape(128, 4096)
    A["f1w3"] = I["L1_ffn_W3"].transpose(1, 0, 2).reshape(128, 4096)
    A["f1w2"] = I["L1_ffn_W2"].reshape(8, 4, 128, 128).transpose(2, 0, 1, 3).reshape(128, 4096)

    g = A["ga"] = z(16, 128, 25)
    for k, n in enumerate("qkv"):
        g[:, :, 8 * k:8 * k + 8] = I["L0_attn_w_" + n].reshape(16, 8, 128).transpose(0, 2, 1)
    g = A["gx"] = z(16, 128, 25)
    g[:, :, :8] = I["L0_xattn_wq"].reshape(128, 16, 8).transpose(1, 0, 2)
    for k, n in enumerate("kv"):
        g[:, :96, 8 + 8 * k:16 + 8 * k] = I["L0_xattn_w" + n].reshape(96, 16, 8).transpose(1, 0, 2)
        g[:, 96, 8 + 8 * k:16 + 8 * k] = I["L0_xattn_b" + n].reshape(16, 8)
    g[:, :8, 24] = I["L0_xattn_bq"].reshape(16, 8)
    g = A["gy"] = z(16, 128, 321)
    g[:, :, :64] = I["L1_xattn_w_q"].reshape(128, 16, 64).transpose(1, 0, 2)
    kv = I["L1_xattn_w_kv"].reshape(96, 2, 16, 64)
    for k in range(2):
        g[:, :96, 64 + 64 * k:128 + 64 * k] = kv[:, k].transpose(1, 0, 2)
    g[:, :64, 193:] = I["L1_xattn_w_out"].reshape(16, 64, 128)
    return A


_OUT = (1, 1024, 128)


def kernel(**inputs):
    import concourse.bacc as bacc
    from concourse.bass_utils import run_bass_kernel_spmd

    nc = bacc.Bacc("TRN2", target_bir_lowering=False, num_devices=1)
    arrays, args = {}, {}
    for name, a in layout({k: np.asarray(v) for k, v in inputs.items()}).items():
        a = np.ascontiguousarray(a)
        arrays["in_" + name] = a
        args[name] = nc.dram_tensor("in_" + name, a.shape, mybir.dt.from_np(a.dtype), kind="ExternalInput").ap()
    out = nc.dram_tensor("out_0", _OUT, F32, kind="ExternalOutput").ap()
    program(nc, out, **args)
    r = run_bass_kernel_spmd(nc, [arrays], core_ids=[0])
    return r.results[0]["out_0"]
```

```python
from contextlib import ExitStack

import numpy as np

import concourse.bass as bass
from concourse import mybir

F32 = mybir.dt.float32
F32R = mybir.dt.float32r
BF16 = mybir.dt.bfloat16
U32 = mybir.dt.uint32
I32 = mybir.dt.int32
ACT = mybir.ActivationFunctionType
ALU = mybir.AluOpType
AX = mybir.AxisListType.X

T = 1024
NT = 8
D = 128
S = 6404
SP = 6432
KT = 50
NKT = 51
E = 8
F = 512


class Lane:

    def __init__(self, nc, ctx, name):
        self.nc, self.ctx, self.name = nc, ctx, name
        self.queue, self.seen, self.sems = [], {}, {}
        self.last = None

    def wait(self, *tokens):
        for tok in tokens:
            if tok is None:
                continue
            if isinstance(tok, list):
                self.wait(*tok)
                continue
            sem, n = tok
            if self.seen.get(id(sem), 0) < n:
                self.seen[id(sem)] = n
                self.queue.append(lambda e, sem=sem, n=n: e.wait_ge(sem, n))

    def count(self, kind, k):
        if kind not in self.sems:
            self.sems[kind] = [self.ctx.enter_context(self.nc.semaphore(f"{self.name}_{kind}")), 0]
        self.sems[kind][1] += k
        return tuple(self.sems[kind])

    def op(self, fn, *tokens, up=None, k=1):
        self.wait(*tokens)
        if self.name == "gp":
            self.wait(self.last)
            self.last = self.count("done", 1)
            self.queue.append(lambda e: fn(e).then_inc(self.last[0], 1))
            return self.last
        if up is None:
            self.queue.append(fn)
            return None
        tok = self.count(up, k)
        self.queue.append(lambda e: fn(e).then_inc(tok[0], k))
        return tok

    def now(self, kind):
        return tuple(self.sems[kind])

    def mm(self, out, lhsT, rhs, *tokens, start=True, stop=True, up=None, skip=False):
        return self.op(lambda e: e.matmul(out, lhsT, rhs, start=start, stop=stop, skip_group_check=skip),
                       *tokens, up=up)

    def tr(self, out, in_, ident, *tokens, up=None):
        return self.op(lambda e: e.transpose(out, in_, ident), *tokens, up=up)

    def act(self, out, in_, func, *tokens, up=None, **kw):
        return self.op(lambda e: e.activation(out, in_, func, **kw), *tokens, up=up)

    def tt(self, out, a, b, o, *tokens, up=None):
        return self.op(lambda e: e.tensor_tensor(out, a, b, o), *tokens, up=up)

    def ts(self, out, a, s1, s2, o0, o1, *tokens, up=None):
        return self.op(lambda e: e.tensor_scalar(out, a, s1, s2, o0, o1), *tokens, up=up)

    def stt(self, out, a, s, b, o0, o1, *tokens, up=None):
        return self.op(lambda e: e.scalar_tensor_tensor(out, a, s, b, o0, o1), *tokens, up=up)

    def copy(self, out, in_, *tokens, up=None):
        return self.op(lambda e: e.tensor_copy(out, in_), *tokens, up=up)

    def load_flag(self, ap, *tokens):
        self.wait(*tokens)
        box = []
        self.queue.append(lambda e: box.append(e.value_load(ap, min_val=0, max_val=1)))
        return box

    def when(self, box, body):
        def go(e):
            with e.If(box[0] == 1):
                body(e)
        self.queue.append(go)

    def dma(self, out, in_, *tokens, up):
        return self.op(lambda e: e.dma_start(out, in_), *tokens, up=up, k=16)


class Relay:

    def __init__(self, outer, inner, dma):
        self.sem = dict(outer=outer, inner=inner)
        self.dma = dma
        self.stages = dict(outer=[], inner=[])

    def stage(self, loop, lane, *fns):
        self.stages[loop].append((lane, fns))

    def run(self, e, lane, start, load):
        so, si = self.sem["outer"], self.sem["inner"]
        no, ni = len(self.stages["outer"]), len(self.stages["inner"])
        start(e)
        if lane == "dv":
            e.sem_inc(so, 1)
            e.sem_inc(si, 1)
        with e.Fori(0, 16) as h:
            if lane == "sp":
                e.wait_ge(si, h * (8 * ni) + 1)
                load(e, h)
            base = h * no + 1
            for k, (who, fns) in enumerate(self.stages["outer"]):
                if who == lane:
                    e.wait_ge(so, base + k)
                    if k == 0:
                        e.wait_ge(self.dma, (h + 1) * 16)
                    for fn in fns[:-1]:
                        fn(e, h, None)
                    fns[-1](e, h, None).then_inc(so, 1)
            if any(who == lane for who, _ in self.stages["inner"]):
                with e.Fori(0, 8) as q:
                    base = (h * 8 + q) * ni + 1
                    for k, (who, fns) in enumerate(self.stages["inner"]):
                        if who == lane:
                            e.wait_ge(si, base + k)
                            if k == 0:
                                e.wait_ge(so, (h + 1) * no + 1)
                            for fn in fns[:-1]:
                                fn(e, h, q)
                            fns[-1](e, h, q).then_inc(si, 1)
        e.wait_ge(si, 16 * 8 * ni + 1)


class Ring:

    def __init__(self, ap, banks):
        self.ap, self.banks, self.freed, self.i = ap, banks, [None] * banks, 0

    def take(self, n=2):
        self.i += self.i % n
        if self.i + n > self.banks:
            self.i = 0
        b = range(self.i, self.i + n)
        self.i = (self.i + n) % self.banks
        return b, self.ap[:, 512 * b[0]:512 * b[-1] + 512], [self.freed[k] for k in b]

    def free(self, b, tok):
        for k in b:
            self.freed[k] = tok


CST = {}
_c = 0
for _n, _w in [("id", 128), ("qs", 1), ("qb", 1), ("ks", 1), ("kb", 1), ("mh", 8),
               ("cos", NT * 4), ("sin", NT * 4), ("iota", 8), ("one", 1),
               ("selh", 32), ("sel2", 32), ("sel8", 8)]:
    CST[_n] = (_c, _c + _w)
    _c += _w
NCST = _c
WA = dict(q0=(0, 128), k0=(128, 256), q=(256, 384), k=(384, 512), v=(512, 640), o=(640, 768))
NWA = 768
WX = dict(q0=(0, 128), q=(128, 256), k=(256, 384), v=(384, 528), o=(528, 656), bq0=(656, 657), bq=(657, 658),
          bo=(658, 786))
NWX = 786
WF0 = dict(rw1=(0, 512), rb1=(512, 516), rb2=(516, 524), b1=(524, 556), b2=(556, 684), rw2=(684, 812))
NWF0 = 812
WB = dict(q=(0, 128), down=(128, 160), up=(160, 416), out=(416, 544), bq=(544, 672), bout=(672, 800), bdown=(800, 801))
NWB = 801
NKV = 2048
WY = dict(q=(0, 1024), out=(1024, 2048), b=(2048, 2176), kv=(2176, 4224))
NWY = 4224
WF1 = dict(g=(0, 8), bg=(8, 16))
NWF1 = 16


def program(nc, out, x, ctx_in, cst, wa, wx, wf0, f0w1, f0w2, wb, wy, wf1, f1w, ga, gx, gy, gc, limit=60.0):
    ctx = ExitStack()
    with ctx:
        pe, ac, dv, gp, sp = [Lane(nc, ctx, n) for n in ("pe", "ac", "dv", "gp", "sp")]
        PS = ctx.enter_context(nc.psum_tensor("PS", [128, 4096], F32))
        ring = Ring(PS, 6)
        O = PS[:, 3072:4096]

        BASE = 16512

        class Region:

            def __init__(self, at):
                self.at = at

            def __call__(self, name, shape, dt=F32):
                size = (2 if dt == BF16 else 4) * int(np.prod(shape[1:]))
                t = nc.alloc_sbuf_tensor_at(name, shape, dt, offset=BASE + self.at)
                self.at += (size + 31) // 32 * 32
                assert BASE + self.at <= 229344, (name, self.at)
                return t

        glob = Region(0)
        X = glob("X", [128, NT, D])
        xn = glob("xn", [128, NT, D])
        xT = glob("xT", [128, T])
        C = glob("C", [128, NCST])
        st = glob("st", [128, NT, 6])
        mv = glob("mv", [128, NT, 2])
        ve = glob("ve", [128, NT])
        rstd = glob("rstd", [128, NT])
        rs = glob("rs", [128, 32])
        On = glob("On", [128, NT, D])
        Osb = glob("Osb", [128, T])
        flags = glob("flags", [1, 8], I32)
        fm = glob("fm", [1, 8])
        nr = glob("nr", [64, 1])
        fl = glob("fl", [1, 64])
        mq = glob("mq", [128, 1])
        mk = glob("mk", [128, 13])
        mkr = glob("mkr", [128, 1])
        selh = glob("selh", [128, 32], BF16)
        WF1s = glob("WF1s", [128, NWF1])
        ctxT = glob("ctxT", [97, SP])

        def c(name):
            return C[:, CST[name][0]:CST[name][1]]

        ident = c("id")

        xf = X[:].rearrange("p i d -> p (i d)")
        x_in = sp.dma(X[:], x.rearrange("a (i p) d -> p (a i) d", p=128), up="x")
        c_in = sp.dma(C[:], cst, up="cst")
        wf1_in = sp.dma(WF1s[:], wf1, up="wf1")

        idle, settle = [], []

        def fill(n):
            for _ in range(min(n, len(idle))):
                settle.append(idle.pop(0)())

        def settled(n):
            for _ in range(min(n, len(settle))):
                f = settle.pop(0)
                if f:
                    f()

        def layernorm(ready, xT_free, X=X, fills=0, parts=None):
            norm, cols = [], []
            dv.wait(xT_free)
            pw = []
            for h in range(2):
                tiles, four = range(4 * h, 4 * h + 4), slice(4 * h, 4 * h + 4)
                if callable(ready[h]):
                    ready[h] = ready[h]()
                dv.wait(ready[h])
                for i in tiles:
                    t = dv.op(lambda e, i=i: e.bn_stats(st[:, i, :], X[:, i, :]), up="ln")
                dv.wait(t)
                for i in tiles:
                    t = dv.op(lambda e, i=i: e.bn_aggr(mv[:, i, :], st[:, i, :]), up="ln")
                t = dv.ts(ve[:, four], mv[:, four, 1], 1e-5, None, ALU.add, ALU.bypass, t, up="ln")
                pw.append(gp.tt(rstd[:, four], ve[:, four], c("mh")[:, 0:4], ALU.pow, t, c_in))
            fill(fills)
            for h in range(2):
                dv.wait(pw[h])
                for i in range(4 * h, 4 * h + 4):
                    norm.append(dv.ts(xn[:, i, :], X[:, i, :], mv[:, i, 0:1], rstd[:, i:i + 1], ALU.subtract, ALU.mult, up="xn"))
            for h in range(2):
                s, ps, fr = ring.take(1)
                for i in range(4):
                    t = pe.tr(ps[:, 128 * i:128 * i + 128], xn[:, 4 * h + i, :], ident, norm[4 * h + i], fr, c_in, up="xT")
                c_ = slice(512 * h, 512 * h + 512)
                if parts:
                    hi = ac.act(parts[0][:, c_], ps, ACT.Copy, t, xT_free, up="xh")
                    t = dv.tt(parts[1][:, c_], ps, parts[0][:, c_].bitcast(F32), ALU.subtract, hi, up="xl")
                    cols.append((hi, t))
                else:
                    t = ac.act(xT[:, c_], ps, ACT.Copy, t, xT_free, up="xT")
                    cols.append(t)
                ring.free(s, t)
            return norm[3::4], [list(t) for t in zip(*cols)] if parts else cols

        def chunks(n):
            return [(a, min(a + 512, n)) for a in range(0, n, 512)]

        mid = Region(glob.at)
        WXs = mid("WXs", [128, NWX])
        kx_at = mid.at
        Kx = mid("Kx", [128, SP], F32R)
        V0 = mid("V0", [128, NKT, 144])
        Qz = [mid(f"Qz{i}", [128, 4, T], F32R) for i in range(2)]
        tmp = mid("tmp", [128, T], F32R)
        Qb = mid("Qb", [128, T])
        p_region = mid.at
        NP = 8
        P = [mid(f"P{i}", [128, T]) for i in range(NP)]
        first = Region(mid.at)
        WAs = first("WAs", [128, NWA])
        Va = first("Va", [128, NT, 16, 9])
        Ka = [first(f"Ka{i}", [128, T], F32R) for i in range(2)]
        hilo = [(first(f"hi{i}", [128, T], F32R), first(f"lo{i}", [128, T], F32R)) for i in range(2)]
        kreg = Region(kx_at)
        CN = 10
        cn = kreg("cn", [128, KT, 96])
        ct = kreg("ct", [4, 96])
        sq = [kreg(f"sq{i}", [128, T], BF16) for i in range(2)]
        assert kreg.at <= kx_at + 4 * S

        def scratch(name, cols):
            return nc.dram_tensor(name, [4, 4, 4, 8, cols], F32, kind="Internal").ap()

        QDa, KDa, QDx, KDx = scratch("QDa", T), scratch("KDa", T), scratch("QDx", T), scratch("KDx", S)
        stores = []

        cmain = ctx_in[0, 0:128 * KT, :].rearrange("(p t) d -> p t d", t=KT)
        wa_in = sp.dma(WAs[:], wa, up="wa")
        cn_in = [sp.dma(cn[:, CN * b:CN * (b + 1), :], cmain[:, CN * b:CN * (b + 1), :], up=f"cn{b}") for b in range(KT // CN)]
        ct_in = sp.dma(ct[:], ctx_in[0, 128 * KT:S, :], up="ct")
        wx_in = sp.dma(WXs[:], wx, up="wx")
        o0 = dv.op(lambda e: e.memset(O, 0.0), up="const")

        def w(a):
            return WAs[:, WA[a][0]:WA[a][1]]

        def wxs(a, rows=128):
            return WXs[0:rows, WX[a][0]:WX[a][1]]

        ctx_t = {}

        def ctx_task(m):
            s, ps, fr = ring.take()
            for kt in range(8 * m, min(8 * m + 8, NKT)):
                i = kt - 8 * m
                if kt == KT:
                    t = pe.tr(ps[0:96, 128 * i:128 * i + 4], ct[:], ident[0:4, 0:4], ct_in, c_in, fr, up="ctxT")
                else:
                    t = pe.tr(ps[0:96, 128 * i:128 * i + 128], cn[:, kt, :], ident, cn_in[kt // CN], c_in, fr, up="ctxT")
            n = min(1024, S - 1024 * m)
            ctx_t[m] = ac.act(ctxT[0:96, 1024 * m:1024 * m + n], ps[0:96, 0:n], ACT.Copy, t, up="ctxT")
            ring.free(s, ctx_t[m])

        v0_t = {}

        def v0_task(m, lane=dv):
            s, ps, fr = ring.take()
            n = min(6, NKT - 6 * m)
            for i in range(n):
                kt = 6 * m + i
                k = 128 if kt < KT else 32
                o = 512 * (i // 3) + 144 * (i % 3)
                for r in range(0, 128, k):
                    t = pe.mm(ps[r:r + k, o:o + 144], ctxT[0:97, 128 * kt:128 * kt + k], wxs("v", 97), fr, ctx_t[kt // 8], c1,
                              wx_in, up="v0")
            cp = (lambda o, i_, *t, up=None: ac.act(o, i_, ACT.Copy, *t, up=up)) if lane is ac else dv.copy
            if n == 6:
                r = cp(V0[:, 6 * m:6 * m + 6, :].rearrange("p (a b) c -> p a (b c)", a=2),
                       ps.rearrange("p (a b) -> p a b", a=2)[:, :, 0:432], t, up="v0")
            else:
                r = cp(V0[:, 6 * m:6 * m + 3, :].rearrange("p b c -> p (b c)"), ps[:, 0:432], t, up="v0")
            v0_t[m] = r
            ring.free(s, r)

        part_free = [None, None]
        sq_t = {}
        part_i = [0]

        def store_parts(src, n, tok, dst, which, pool, at=0, top=None, square=None):
            if not at:
                part_i[0] += 1
            b = part_i[0] % 2
            hi, lo_ = [x[:, at:at + n] for x in hilo[b]]
            if not at:
                dv.wait(part_free[b])
                part_free[b] = []
            h = dv.copy(hi, src, tok, up="parts")
            t = t2 = dv.tt(lo_, src, hi.bitcast(F32), ALU.subtract, h, up="parts")
            if square is not None:
                t2 = sq_t[square] = gp.tt(sq[square][:, at:at + n], hi.bitcast(F32), hi.bitcast(F32), ALU.mult, h)
            if top is not None:
                t2 = dv.op(lambda e: e.tensor_reduce(top, hi.bitcast(F32), AX, ALU.max, apply_absolute_value=True), up="mk")
            out = []
            for r, p in enumerate(which):
                if p is None:
                    continue
                out.append(sp.dma(dst[:, :, r, :, :].rearrange("g j d c -> (g j) d c"), (hi, lo_)[p].bitcast(F32), t, up=pool))
            part_free[b] += [out[-1], t, t2]
            stores.append(out[-1])
            return t, out[-1]

        tmp_free = [None]

        def direct(parts, wk, y_bias, sgn, sel, w_in, dst_free, src_t, src):
            y, yt, tmp_t, banks = [], [], [], []
            for h in range(2):
                c_ = slice(512 * h, 512 * h + 512)
                s, ps, fr = ring.take(1)
                banks.append(s)
                t = pe.mm(ps, wk, src[:, c_], fr, src_t[h], w_in, up="dir")
                if y_bias is None:
                    y.append(ps)
                else:
                    y.append(Qb[:, c_])
                    t = ac.act(Qb[:, c_], ps, ACT.Identity, t, qb_free[0], bias=y_bias, up="qb")
                    ring.free(s, t)
                tmp_t.append(ac.act(tmp[:, c_], y[h], ACT.Copy, t, tmp_free[0], scale=sgn, up="tmp"))
            toks = []
            for rows, d in parts:
                for h in range(2):
                    c_ = slice(512 * h, 512 * h + 512)
                    t = dv.stt(d[:, c_], y[h][rows, :], sel[rows, :], tmp[rows, c_].bitcast(F32), ALU.mult, ALU.add, tmp_t[h],
                               dst_free, up="dir")
                    if y_bias is None and d is parts[-1][1]:
                        ring.free(banks[h], t)
                toks.append(t)
            tmp_free[0] = qb_free[0] = toks[-1]
            return toks

        qb_free = [None]
        q0_parts = [(slice(32 * j, 32 * j + 32), Qz[0][32 * j:32 * j + 32, j, :]) for j in range(4)]

        def load_q(g, QD, stored, free):
            return [sp.dma(Qz[g % 2][32 * j:32 * j + 24, j, :].bitcast(F32), QD[g, j, 0:3].rearrange("r d c -> (r d) c"),
                           stored, free, qz1, up=f"lq{g % 2}") for j in range(4)][-1]

        SC = float(1 / np.sqrt(8))

        def flat(*toks):
            out = []
            for t in toks:
                if isinstance(t, list):
                    out += flat(*t)
                elif t is not None:
                    out.append(t)
            return out

        def general(name, region, hd, src, rows, nkeys, weights, W, scale, causal, out, final, flag, ready):
            nt = -(-nkeys // 128)
            g = Region(region)
            Wg = g(name + "W", [128, W])
            QT = g(name + "QT", [hd, T])
            Qc = g(name + "Qc", [hd, 128])
            KT_ = g(name + "KT", [hd, nkeys])
            Vg = g(name + "V", [128, nt, hd])
            Sg = g(name + "S", [128, nkeys])
            PT = g(name + "PT", [128, 512])
            sc4 = g(name + "s", [128, 4])
            if causal:
                io = g(name + "io", [128, T + NT])
                msk = g(name + "mk", [128, T])
            if final is not False:
                Oc = g(name + "Oc", [128, hd])
                OT = g(name + "OT", [hd, 128])
            outer, inner, gdma, cdma = [ctx.enter_context(nc.semaphore(f"{name}_{n}"))
                                        for n in ("outer", "inner", "dma", "const")]
            r = Relay(outer, inner, gdma)
            P0, P1 = PS[:, 0:512], PS[:, 512:1024]
            big = PS[:, 1024:3072]

            def mm(o, a, b, st=True, sp_=True):
                return lambda e, h, q: e.matmul(o, a, b, start=st, stop=sp_)

            def cp(o, a):
                return lambda e, h, q: e.tensor_copy(o, a)

            r.stage("outer", "pe", *[mm(PS[0:hd, a:a + 512], Wg[:, 0:hd], xT[:, a:a + 512]) for a in (0, 512)])
            r.stage("outer", "dv", lambda e, h, q: e.tensor_scalar(QT[:], PS[0:hd, 0:1024], Wg[0:hd, 3 * hd:3 * hd + 1], None,
                                                                    ALU.add, ALU.bypass))
            for a in range(0, nkeys, 2048):
                n = min(2048, nkeys - a)
                r.stage("outer", "pe", *[mm(big[0:hd, b:min(b + 512, n)], Wg[0:rows, hd:2 * hd],
                                            src[0:rows, a + b:a + min(b + 512, n)]) for b in range(0, n, 512)])
                r.stage("outer", "dv", cp(KT_[:, a:a + n], big[0:hd, 0:n]))
            per = 2048 // hd
            for a in range(0, nt, per):
                ts_ = range(a, min(a + per, nt))
                r.stage("outer", "pe", *[mm(big[0:min(128, nkeys - 128 * t), hd * (t - a):hd * (t - a) + hd],
                                            src[0:rows, 128 * t:min(128 * t + 128, nkeys)], Wg[0:rows, 2 * hd:3 * hd])
                                         for t in ts_])
                full = [t for t in ts_ if 128 * t + 128 <= nkeys]
                r.stage("outer", "dv", cp(Vg[:, a:a + len(full), :].rearrange("p t d -> p (t d)"), big[:, 0:hd * len(full)]))
                if len(full) < len(ts_):
                    t = ts_[-1]
                    r.stage("outer", "dv", cp(Vg[0:nkeys - 128 * t, t, :],
                                              big[0:nkeys - 128 * t, hd * (t - a):hd * (t - a) + hd]))
            r.stage("inner", "dv", lambda e, h, q: e.tensor_copy(Qc[:], QT[:, bass.ds(q * 128, 128)]))
            for a in range(0, nkeys, 2048):
                n = min(2048, nkeys - a)
                r.stage("inner", "pe", *[mm(big[:, b:min(b + 512, n)], Qc[:], KT_[:, a + b:a + min(b + 512, n)])
                                         for b in range(0, n, 512)])
                r.stage("inner", "dv", cp(Sg[:, a:a + n], big[:, 0:n]))
            if causal:
                r.stage("inner", "dv", lambda e, h, q: e.tensor_copy(sc4[:, 3:4], io[:, bass.ds(q + T, 1)]))
                r.stage("inner", "dv", lambda e, h, q: e.tensor_scalar(msk[:], io[:, 0:T], sc4[:, 3:4], -3e38, ALU.is_gt,
                                                                        ALU.mult))
                r.stage("inner", "dv", lambda e, h, q: e.tensor_tensor(Sg[:], Sg[:], msk[:], ALU.add))
            r.stage("inner", "dv", lambda e, h, q: e.tensor_reduce(sc4[:, 0:1], Sg[:], AX, ALU.max))
            r.stage("inner", "dv", lambda e, h, q: e.tensor_scalar(sc4[:, 1:2], sc4[:, 0:1], -scale, None, ALU.mult,
                                                                    ALU.bypass))
            r.stage("inner", "ac", lambda e, h, q: e.activation(Sg[:], Sg[:], ACT.Exp, bias=sc4[:, 1:2], scale=scale,
                                                                 accum_out=sc4[:, 2:3]))
            for a in range(0, nt, 4):
                ts_ = range(a, min(a + 4, nt))
                ws = [min(128, nkeys - 128 * t) for t in ts_]
                r.stage("inner", "pe", *[(lambda e, h, q, t=t, w=w, a=a: e.transpose(
                    P0[0:w, 128 * (t - a):128 * (t - a) + 128], Sg[:, 128 * t:128 * t + w], ident))
                    for t, w in zip(ts_, ws)])
                nf = sum(w == 128 for w in ws)
                if nf:
                    r.stage("inner", "dv", cp(PT[:, 0:128 * nf], P0[:, 0:128 * nf]))
                if nf < len(ws):
                    r.stage("inner", "dv", cp(PT[0:ws[-1], 128 * nf:128 * nf + 128], P0[0:ws[-1], 128 * nf:128 * nf + 128]))
                r.stage("inner", "pe", *[mm(P1[:, 0:hd], PT[0:w, 128 * (t - a):128 * (t - a) + 128], Vg[0:w, t, :], t == 0,
                                            t == nt - 1) for t, w in zip(ts_, ws)])
            r.stage("inner", "dv", lambda e, h, q: e.reciprocal(sc4[:, 0:1], sc4[:, 2:3]))
            if final is False:
                r.stage("inner", "dv", lambda e, h, q: e.tensor_scalar(
                    out[:, bass.ds(q * 16 + h, 1), :], P1[:, 0:hd].unsqueeze(1), sc4[:, 0:1], None, ALU.mult, ALU.bypass))
            else:
                r.stage("inner", "dv", lambda e, h, q: e.tensor_scalar(Oc[:], P1[:, 0:hd], sc4[:, 0:1], None, ALU.mult,
                                                                        ALU.bypass))
                r.stage("inner", "pe", mm(P0[0:hd, 0:128], Oc[:], ident))
                r.stage("inner", "dv", cp(OT[:], P0[0:hd, 0:128]))
                r.stage("inner", "pe", mm(P1[:, 0:128], OT[:], Wg[0:hd, 3 * hd + 1:3 * hd + 129]))
                r.stage("inner", "dv", lambda e, h, q: e.tensor_tensor(out[:, bass.ds(q, 1), :], out[:, bass.ds(q, 1), :],
                                                                        P1[:, 0:128].unsqueeze(1), ALU.add))

            def start(name_):
                def go(e):
                    for sem, n in ready:
                        e.wait_ge(sem, n)
                    if name_ == "sp" and causal:
                        e.dma_start(io[:], gc).then_inc(cdma, 16)
                    if name_ == "dv" and causal:
                        e.wait_ge(cdma, 16)
                    if name_ == "dv" and final is not False:
                        e.tensor_copy(out, final).then_inc(cdma, 1)
                        e.wait_ge(cdma, 1)
                return go

            def load(e, h):
                e.dma_start(Wg[:], weights[bass.ds(h, 1)].rearrange("a p f -> (a p) f")).then_inc(gdma, 16)

            for lane in (pe, ac, dv, sp):
                lane.when(flag[lane.name], lambda e, lane=lane: r.run(e, lane.name, start(lane.name), load))

        def load_flags(k):
            return {lane.name: lane.load_flag(flags[0:1, k:k + 1], fl_t[k]) for lane in (pe, ac, dv, sp)}

        osb_free = [None, None]
        on_t = [None, None]
        p_free = [None] * NP
        unit = [0]
        o_free = [[o0, o0]]
        q_free = [None, None]

        def attend8(nkt, width, K, Vt, v_tok, q_t, k_tok, tasks, k_used, causal):
            pv_q = []
            pv_last = [None, None]

            def emit_pv(final=False):
                while pv_q and (final or unit[0] >= pv_q[0][0]):
                    pv_q.pop(0)[1]()

            order = list(range(nkt))
            lasts = [3, 7] if causal else [nkt - 1] * 2
            for g in range(4):
                for n, kt in enumerate(order):
                    kw = width(kt)
                    lo = 128 * kt if causal else 0
                    tile = []
                    todo = list(tasks.get((g, n), []))
                    last4 = not causal and kt == KT
                    for j in range(4):
                        if last4 and j:
                            break
                        off = 512 if lo >= 512 else 0
                        s, ps, fr = ring.take(1 if off else 2)
                        for a, b in ((lo, 512), (max(lo, 512), 1024)):
                            for jj in (range(4) if last4 else [j]):
                                if a < b:
                                    r = slice(32 * jj, 32 * jj + 32) if last4 else slice(0, 128)
                                    lhs, rhs = K(g)[:, 128 * kt:128 * kt + kw], Qz[g % 2][:, jj, a:b]
                                    if last4:
                                        lhs, rhs = lhs.bitcast(F32), rhs.bitcast(F32)
                                    t = pe.mm(ps[r, a - off:b - off], lhs, rhs, fr, q_t[g][jj], k_tok(g, kt), up="qk")
                        pb = unit[0] % NP
                        unit[0] += 1
                        t2 = ac.act(P[pb][:, lo:T], ps[:, lo - off:T - off], ACT.Exp, t, p_free[pb], scale=SC, up="exp")
                        ring.free(s, t2)
                        if causal:
                            t2 = gp.op(lambda e, pb=pb, lo=lo: e.affine_select(
                                out=P[pb][:, lo:lo + 128], in_=P[pb][:, lo:lo + 128], compare_op=ALU.is_ge, fill=0.0,
                                base=0, pattern=[[1, 128]], channel_multiplier=-1), t2, up="mask")
                        tile.append((pb, t2))
                        emit_pv()
                        if j == 3 or last4:
                            k_used[g, kt] = t
                            q_free[g % 2] = t
                        if todo and j >= 4 - len(todo):
                            todo.pop(0)()

                    if last4:
                        tile = 4 * tile

                    def pv(h, g=g, kt=kt, lo=lo, tile=tile, last4=last4):
                        a, b = max(lo, 512 * h), 512 * h + 512
                        t = pv_last[h]
                        if a < b:
                            for j, (pb, tk) in enumerate(tile):
                                r = slice(32 * j, 32 * j + 32) if last4 else slice(0, 128)
                                t = pe.mm(O[32 * j:32 * j + 9, a:b], Vt(kt, 4 * g + j)[r], P[pb][r, a:b], tk, o_free[0][h],
                                          v_tok(kt), start=kt == 0, stop=kt == lasts[h], skip=True, up="pv")
                        pv_last[h] = t
                        if h == 1:
                            for pb, _ in tile:
                                p_free[pb] = t
                        if h == 1 and kt == order[-1]:
                            finish_group(g, pv_last, lambda f: pv_q.append((unit[0] + 3, f)))

                    pv_q.append((unit[0] + LAG, lambda pv=pv: pv(0)))
                    pv_q.append((unit[0] + LAG + 2, lambda pv=pv: pv(1)))
            emit_pv(True)

        LAG = 2

        def finish_group(g, pv_t, later):
            o_free[0] = [ac.act(Osb[:, c_], O[:, c_], ACT.Copy, pv_t[h], osb_free[h], up="osb")
                         for h, c_ in enumerate((slice(0, 512), slice(512, 1024)))]
            e_t = list(o_free[0])

            def divide(h):
                tiles = slice(4 * h, 4 * h + 4)
                s, ps, fr = ring.take(1)
                pe.wait(e_t[h], fr)
                for i in range(4):
                    t = pe.tr(ps[:, 128 * i:128 * i + 128], Osb[:, 512 * h + 128 * i:512 * h + 128 * i + 128], ident, up="otr")
                osb_free[h] = t
                v = ps.rearrange("p (i j c) -> p i j c", i=4, j=4)
                r3 = rs[:, 16 * h:16 * h + 16].rearrange("p (i j) -> p i j", j=4)
                r = dv.op(lambda e, v=v, r3=r3: e.reciprocal(r3, v[:, :, :, 8]), t, on_t[h], up="rs")
                on_t[h] = dv.tt(On[:].rearrange("p i (h c) -> p i h c", c=8)[:, tiles, 4 * g:4 * g + 4, :], v[:, :, :, 0:8],
                                r3.unsqueeze(3).to_broadcast([128, 4, 4, 8]), ALU.mult, r, up="on")
                ring.free(s, on_t[h])

            for h in range(2):
                if g == 3:
                    fill(1)
                    divide(h)
                else:
                    later(lambda h=h: divide(h))

        def out_proj(wo, w_in, extra_free):
            done = []
            mid_t = []
            for h in range(2):
                cols = slice(512 * h, 512 * h + 512)
                s, ps, fr = ring.take(1)
                for i in range(4):
                    t = pe.tr(ps[:, 128 * i:128 * i + 128], On[:, 4 * h + i, :], ident, fr, on_t[h], up="onT")
                t = ac.act(Osb[:, cols], ps, ACT.Copy, t, osb_free[h], up="ont")
                ring.free(s, t)
                mid_t.append(t)
            fill(1)
            for h in range(2):
                s, ps, fr = ring.take(1)
                for i in range(4 * h, 4 * h + 4):
                    t2 = pe.mm(ps[:, 128 * (i - 4 * h):128 * (i - 4 * h) + 128], Osb[:, 128 * i:128 * i + 128], wo, fr, mid_t[h],
                               w_in, up="oproj")
                osb_free[h] = t2
                on_t[h] = t2
                cols = slice(512 * h, 512 * h + 512)
                done.append(dv.tt(xf[:, cols], xf[:, cols], ps, ALU.add, t2, extra_free, up="res"))
                ring.free(s, done[h])
            settled(9)
            return done

        def gates(G, ps, bias, tok, w_in, gfree, g):
            sc, m8, ix, ixf, d, p1, eq = g
            t = dv.tt(sc[:], ps.rearrange("p (i e) -> p i e", e=8), bias.unsqueeze(1).to_broadcast([128, NT, 8]), ALU.add,
                      tok, w_in, up="sc")
            r = t
            dv.wait(t)
            for i in range(NT):
                t = dv.op(lambda e, i=i: e.max(m8[:, i, :], sc[:, i, :]), up="gate")
            dv.wait(t)
            for i in range(NT):
                t2 = dv.op(lambda e, i=i: e.max_index(ix[:, i, :], m8[:, i, :], sc[:, i, :]), up="gate")
            t2 = dv.copy(ixf[:], ix[:, :, 0:2], t2, up="gate")
            t = dv.tt(d[:], m8[:, :, 1], m8[:, :, 0], ALU.subtract, up="gate")
            t = ac.act(d[:], d[:], ACT.Exp, t, up="ge")
            t = dv.ts(p1[:, 0, :], d[:], 1.0, None, ALU.add, ALU.bypass, t, up="gate")
            t = dv.op(lambda e: e.reciprocal(p1[:, 1, :], p1[:, 0, :]), t, up="gate")
            t = dv.tt(p1[:, 0, :], p1[:, 1, :], d[:], ALU.mult, t, up="gate")
            io = c("iota").unsqueeze(1).to_broadcast([128, NT, 8])
            for k in range(2):
                q = dv.tt(eq[:, k], io, ixf[:, :, k:k + 1].to_broadcast([128, NT, 8]), ALU.is_equal, t2, up="gate")
                q = dv.tt(eq[:, k], eq[:, k], p1[:, 1 - k, :].unsqueeze(2).to_broadcast([128, NT, 8]), ALU.mult, q, t, up="gate")
            return r, dv.tt(G[:], eq[:, 0], eq[:, 1], ALU.add, q, gfree, up="gate")

        def gate_bufs(reg, n):
            return (reg(f"gsc{n}", [128, NT, 8]), reg(f"gm8{n}", [128, NT, 8]), reg(f"gix{n}", [128, NT, 8], U32),
                    reg(f"gixf{n}", [128, NT, 2]), reg(f"gd{n}", [128, NT]), reg(f"gp{n}", [128, 2, NT]),
                    reg(f"geq{n}", [128, 2, NT, 8]))

        stage = Region(mid.at)
        W1f = stage("W1f", [128, E * F])
        WF0s = stage("WF0s", [128, NWF0])
        WBs_at = stage.at
        WBs = stage("WBs", [128, NWB])
        G = stage("G", [128, NT, 8])
        gb = gate_bufs(stage, 0)

        def compare(k, src, scale, square, tok):
            bar = (limit / scale) * (abs(limit) / scale if square else 1)
            t = dv.op(lambda e: e.tensor_reduce(fm[:, k:k + 1], src, AX, ALU.max), tok, up="flag")
            return dv.ts(flags[0:1, k:k + 1], fm[:, k:k + 1], bar, None, ALU.is_gt, ALU.bypass, t, up="flag")

        idle += [lambda m=m: ctx_task(m) for m in range(2)]
        xn_t, xT_t = layernorm([x_in, x_in], None, fills=2)
        qz0 = gp.op(lambda e: e.memset(Qz[0][:].bitcast(F32), 0.0))
        va1 = gp.op(lambda e: e.memset(Va[:], 1.0))
        gp.op(lambda e: e.memset(ctxT[96:97, 0:S], 1.0))
        gp.op(lambda e: e.memset(ctxT[:, S:SP], 0.0))
        c1 = gp.op(lambda e: e.memset(Kx[:, S:SP].bitcast(F32), 0.0))
        qz1 = gp.op(lambda e: e.memset(Qz[1][:].bitcast(F32), 0.0))
        selh_t = dv.copy(selh[:], c("selh"), c_in, up="const")
        rows = slice(0, 128)
        k0_t = direct([(rows, Ka[0][:])], w("k0"), None, c("ks"), c("kb"), wa_in, None, xT_t, xT)
        qa_t, ka_t, ka_used, kx_t, kx_used, fl_t = {}, {0: k0_t}, {}, {}, {}, {}
        qa_t[0] = direct(q0_parts, w("q0"), None, c("qs"), c("qb"), wa_in, qz0, xT_t, xT)
        s, ps, fr = ring.take()
        for i in range(NT):
            t = pe.mm(ps[:, 128 * i:128 * i + 128], xT[:, 128 * i:128 * i + 128], w("v"), fr, xT_t, wa_in, up="proj")
        va_t = dv.copy(Va[:].rearrange("p i h c -> p (i h) c")[:, :, 0:8], ps.rearrange("p (n c) -> p n c", c=8), t, va1,
                       up="proj")
        ring.free(s, va_t)
        ctx_task(2)

        def all_task(name, k, h):
            def go():
                a = 512 * h
                s, ps, fr = ring.take(1)
                t = pe.mm(ps, w(name), xT[:, a:a + 512], fr, xT_t[h], wa_in, up="proj")
                r, st_ = store_parts(ps, 512, t, (KDa if k else QDa)[..., a:a + 512], (0, 1, 0, 0) if k else (0, 0, 1, None),
                                     f"sa{k}", a, square=k)
                ring.free(s, r)
                if h == 0:
                    return
                if k == 0:
                    qa_t[1] = [load_q(1, QDa, st_, None)] * 4
                    qa_t["st"] = st_
                else:
                    ka_t["st"] = st_
                    load_ka(1)
            return go

        def load_ka(g):
            ka_t[g] = [sp.dma(Ka[g % 2][:].bitcast(F32), KDa[g].rearrange("j r d c -> (j r d) c"), ka_t["st"], ka_used.get((g - 2, NT - 1)),
                              up=f"lka{g % 2}")]

        def next_a(g):
            def go():
                qa_t[g] = [load_q(g, QDa, qa_t["st"], q_free[g % 2])] * 4
                load_ka(g)
            return go

        def norm_flag():
            s, ps, fr = ring.take()
            for k in range(2):
                for a, b in chunks(T):
                    t = pe.mm(ps[32 * k:32 * k + 32, a:b], selh[:], sq[k][:, a:b], fr, sq_t[k], selh_t, up="nm")
            kx_t["sq"] = t
            t = dv.op(lambda e: e.tensor_reduce(nr[:], ps[0:64, :], AX, ALU.max), t, up="nm")
            t = pe.tr(ps[0:1, 0:64], nr[:], ident[0:64, 0:64], t, up="nm")
            t = dv.copy(fl[:], ps[0:1, 0:64], t, up="nm")
            ring.free(s, t)
            t = dv.tt(fl[:, 0:16], fl[:, 0:16], fl[:, 32:48], ALU.mult, t, up="nm")
            fl_t[0] = compare(0, fl[:, 0:16], SC, True, t)

        def kx_task(m):
            def go():
                s, ps, fr = ring.take(1)
                n = min(512, S - 512 * m)
                t = pe.mm(ps[:, 0:n], wxs("k", 97), ctxT[0:97, 512 * m:512 * m + n], fr, ctx_t[m // 2], c1, wx_in, up="proj")
                r, st_ = store_parts(ps[:, 0:n], n, t, KDx[:, :, :, :, 512 * m:512 * m + n], (0, 1, 0, 0), f"sk{m}",
                                     top=mk[:, m:m + 1])
                ring.free(s, r)
                kx_t["st", m // 2] = [kx_t.get(("st", m // 2)), st_]
                if m % 2 or m == 12:
                    load_kx(0, m // 2)
            return go

        def load_kx(g, m):
            n = min(1024, S - 1024 * m)
            kx_t[g, m] = sp.dma(Kx[:, 1024 * m:1024 * m + n].bitcast(F32), KDx[g].rearrange("j r d c -> (j r d) c")[:, 1024 * m:1024 * m + n],
                                kx_t["st", m], ctx_t[6], kx_t["sq"], kx_used.get((g - 1, min(8 * m + 7, NKT - 1))), up=f"lk{m}")

        def spread(tasks, slots, into):
            for i, task in enumerate(tasks):
                into.setdefault(slots[i * len(slots) // len(tasks)], []).append(task)

        fl_r = {}
        tasks = {(0, 0): [all_task("q", 0, h) for h in range(2)], (0, 1): [all_task("k", 1, h) for h in range(2)], (0, 6): [norm_flag],
                 (1, 1): [lambda: fl_r.update({0: load_flags(0)})], (1, 0): [next_a(2)], (2, 0): [next_a(3)]}
        rest = [lambda m=m: ctx_task(m) for m in range(3, 7)] + [lambda m=m: kx_task(m)() for m in range(13)]
        spread(rest, [(g, kt) for g in range(4) for kt in range(8)][2:], tasks)
        idle += [lambda m=m: v0_task(m, ac) for m in range(9)]
        attend8(NT, lambda kt: 128, lambda g: Ka[g % 2], lambda kt, h: Va[:, kt, h, :], lambda kt: va_t, qa_t,
                lambda g, kt: ka_t[g], tasks, ka_used, True)
        general("ga", p_region, 8, xT, 128, T, ga, 25, SC, True, On[:].rearrange("p i (h c) -> p (i h) c", c=8),
                False, fl_r[0], flat(ring.freed, on_t, p_free, o_free))
        x_t = a0_end = out_proj(w("o"), wa_in, xn_t)

        xn_t, xT_t = layernorm(x_t, None, fills=3)
        bo_t = gp.tt(X[:], X[:], wxs("bo").unsqueeze(1).to_broadcast([128, NT, D]), ALU.add, xn_t, wx_in)
        qx_t = {0: direct(q0_parts, wxs("q0"), wxs("bq0"), c("qs"), c("qb"), wx_in, q_free[0], xT_t, xT)}

        fill(9)

        def width(kt):
            return 128 if kt < KT else 32

        def all_q():
            s, ps, fr = ring.take()
            for a, b in chunks(T):
                t = pe.mm(ps[:, a:b], wxs("q"), xT[:, a:b], fr, xT_t, wx_in, up="proj")
            y = dv.ts(Qb[:], ps, wxs("bq"), None, ALU.add, ALU.bypass, t, qb_free[0], up="qb")
            ring.free(s, y)
            dv.op(lambda e: e.tensor_reduce(mq[:], Qb[:], AX, ALU.max, apply_absolute_value=True), y, up="mq")
            r, qx_t["st"] = store_parts(Qb[:], T, y, QDx, (0, 0, 1, None), "sq")
            qx_t[1] = [load_q(1, QDx, qx_t["st"], q_free[1])] * 4

        def dim_flag():
            s, ps, fr = ring.take()
            t = dv.op(lambda e: e.tensor_reduce(mkr[:], mk[:], AX, ALU.max), dv.now("mk"), up="nm")
            t = dv.tt(mkr[:], mkr[:], mq[:], ALU.mult, t, dv.now("mq"), up="nm")
            t = pe.mm(ps[0:1, 0:32], mkr[:], c("selh"), t, fr, up="nm")
            fl_t[1] = compare(1, ps[0:1, 0:32], SC, False, t)
            ring.free(s, fl_t[1])

        def prefetch():
            pre["wf0"] = sp.dma(WF0s[:], wf0, a0_end, part_free, up="wf0")
            pre["wb"] = sp.dma(WBs[:], wb, up="wb")
            pre["w1"] = sp.dma(W1f[:], f0w1, up="w1")

        pre = {}

        def next_x(g):
            def go():
                qx_t[g] = [load_q(g, QDx, qx_t["st"], q_free[g % 2])] * 4
            return go

        tasks = {(0, 3): [all_q], (0, 20): [dim_flag], (0, 24): [lambda: fl_r.update({1: load_flags(1)})],
                 (0, 30): [prefetch], (1, 0): [next_x(2)], (2, 0): [next_x(3)]}
        for g in range(3):
            for m in range(7):
                at = (g, 8 * m + 8) if m < 6 else (g + 1, 0)
                tasks.setdefault(at, []).append(lambda g=g, m=m: load_kx(g + 1, m))
        attend8(NKT, width, lambda g: Kx, lambda kt, h: V0[:, kt, 9 * h:9 * h + 9],
                lambda kt: v0_t[kt // 6], qx_t, lambda g, kt: kx_t[g, kt // 8], tasks, kx_used, False)
        general("gx", kx_at, 8, ctxT, 97, S, gx, 25, SC, False, On[:].rearrange("p i (h c) -> p (i h) c", c=8),
                False, fl_r[1], flat(ring.freed, on_t, p_free, o_free))
        x_t = out_proj(wxs("o"), wx_in, bo_t)

        def transposed_gates(G, GT, tok, gt_free):
            s, ps, fr = ring.take()
            for i in range(NT):
                t = pe.tr(ps[0:8, 128 * i:128 * i + 128], G[:, i, :], ident, tok, fr, up="GT")
            t = ac.act(GT[:], ps[0:8, :], ACT.Copy, t, gt_free, up="GT")
            ring.free(s, t)
            return t

        f0b = Region(glob.at)
        H = [f0b(f"H{i}", [128, 4, T]) for i in range(2)]
        W2f = f0b("W2f", [128, E * F])
        GT = f0b("GT", [8, T])
        xh, xl = f0b("xh", [128, T], F32R), f0b("xl", [128, T], F32R)
        WS = [[f0b(f"ws{i}{k}", [128, F], F32R) for k in range(2)] for i in range(2)]
        w2_in = sp.dma(W2f[:], f0w2, p_free, q_free, v0_t[8], kx_used[3, NKT - 1], up="w2")
        x0_end = [p_free, q_free, kx_used[3, NKT - 1]]

        def wf(a, rows=128):
            return WF0s[0:rows, WF0[a][0]:WF0[a][1]]

        wf0_in, wb_in, w1_in = pre["wf0"], pre["wb"], pre["w1"]
        h_free = [x0_end, x0_end]
        ws_free = [x0_end, x0_end]
        w_t = {}

        def split(hi, lo_, src, tok, free, up, lane=dv):
            h = ac.act(hi, src, ACT.Copy, tok, free, up=up + "h")
            return lane.tt(lo_, src, hi.bitcast(F32), ALU.subtract, h, tok, free, up=up + "l")

        def first_weights(n):
            if n == 0:
                return wf("rw1"), wf("rb1"), wf0_in
            o = WF0["b1"][0] + 4 * (n - 1)
            return W1f[:, F * (n - 1):F * n], WF0s[:, o:o + 4], w1_in

        def split_weights(n, lane=dv):
            src, _, w_in = first_weights(n)
            w_t[n] = split(WS[n % 2][0][:], WS[n % 2][1][:], src, w_in, ws_free[n % 2], "w", lane)

        split_weights(0, gp)
        xn_t, xs_t = layernorm(x_t, x0_end, parts=(xh, xl))

        A, B = slice(0, 64), slice(64, 128)
        NCH, NKVB = 13, 3
        KV_at = glob.at + 1024 * 70
        x1h = Region(KV_at)
        WYs = x1h("WYs", [128, WY["kv"][0]])
        WKV = [x1h(f"WKV{k}", [96, 2048], F32R) for k in range(2)]
        CP = [[x1h(f"CP{i}{k}", [96, 512], F32R) for k in range(2)] for i in range(NKVB)]
        sel2 = x1h("sel2", [128, 32], BF16)
        mqy = x1h("mqy", [64, 8])
        mky = x1h("mky", [128, 48])
        mkp = x1h("mkp", [128, 1])
        mqp = x1h("mqp", [64, 1])
        kv_raw = Region(x1h.at)("kv_raw", [96, 2048])
        K1 = [x1h(f"K1{i}", [128, 2, 512], F32R) for i in range(NKVB)]
        V1 = [x1h(f"V1{i}", [128, 512]) for i in range(NKVB)]
        sqk = [x1h(f"sqk{i}", [128, 512], BF16) for i in range(NKVB)]
        assert x1h.at + 4096 <= WBs_at, (x1h.at, WBs_at)
        Vs = x1h("Vs", [128, NKT, 128])
        WR_at = x1h.at
        WR = [x1h("WR0", [128, 3, F])]
        wkv_in = sp.dma(kv_raw[:], wy[0:96, WY["kv"][0]:WY["kv"][1]], x0_end, up="wkv")
        wy_in = sp.dma(WYs[:], wy[:, 0:WY["kv"][0]], x0_end, up="wy")
        vs_free, v_ready = {}, {}
        PARTS = ((0, 0), (0, 1), (1, 0))
        cp_t, cp_free, kv_free, k1_sq, sqk_free, sqk_t, k_ready = {}, [x0_end] * NKVB, {}, {}, [None] * NKVB, {}, {}

        def wys(a, lo, n, r0=0, r1=128):
            return WYs[r0:r1, WY[a][0] + lo:WY[a][0] + lo + n]

        def split_kv_weights():
            kv_free["w"] = split(WKV[0][:], WKV[1][:], kv_raw[:], wkv_in, x0_end, "wk")
            dv.copy(sel2[:], c("sel2"), x0_end, up="const")
            kv_free["c"] = dv.op(lambda e: e.memset(mky[:], 0.0), up="const")

        def split_ctx(n, lane):
            b, m = n % NKVB, n % NCH
            w_ = min(512, SP - 512 * m)
            pieces = [(0, w_, ctxT[0:96, 512 * m:512 * m + w_])]
            if w_ < 512:
                pieces.append((w_, w_ + 32, ctxT[0:96, 128 * KT:SP]))
            for a, e_, src in pieces:
                t = ac.act(CP[b][0][:, a:e_], src, ACT.Copy, cp_free[b], up="cp")
                cp_t[n] = lane.tt(CP[b][1][:, a:e_], src, CP[b][0][:, a:e_].bitcast(F32), ALU.subtract, t, up="cp")

        def kv_chunk(n, early=False):
            b, (p, m) = n % NKVB, divmod(n, NCH)
            w_ = min(512, SP - 512 * m)
            sk, ps, fr = ring.take(1)
            for k, (i, j) in enumerate(PARTS):
                t = pe.mm(ps[:, 0:w_], WKV[i][:, 128 * p:128 * p + 128], CP[b][j][:, 0:w_], fr, cp_t[n], kv_free["w"],
                          start=k == 0, stop=k == 2, up="proj")
            cp_free[b] = t
            if p % 2 == 0:
                more = [v_part(n, lo, early) for lo in ((0, 2) if early else (0,))]
            else:
                v_ready[n] = v_ready[n - NCH]
                more = []

            def rest():
                k = K1[b]
                f = [kv_free.get(("k", b)), k1_sq.get(b), kv_free["w"], w1_used]
                h1 = ac.act(k[A, 0, 0:w_], ps[A, 0:w_], ACT.Copy, t, f, up="kh")
                if w_ == 512:
                    h2 = ac.act(k[B, 1, :], ps[B, :], ACT.Copy, up="kh")
                    dv.tt(k[B, 0, :], ps[A, :], k[A, 0, :].bitcast(F32), ALU.subtract, h1, f)
                    r = dv.tt(k[A, 1, :], ps[B, :], k[B, 1, :].bitcast(F32), ALU.subtract, h2, up="k")
                else:
                    ac.act(k[B, 1, 0:256], ps[B, 0:256], ACT.Copy)
                    h2 = ac.act(k[B, 1, 288:320], ps[B, 256:288], ACT.Copy, up="kh")
                    dv.tt(k[B, 0, 0:w_], ps[A, 0:w_], k[A, 0, 0:w_].bitcast(F32), ALU.subtract, h1, f)
                    dv.tt(k[A, 1, 0:256], ps[B, 0:256], k[B, 1, 0:256].bitcast(F32), ALU.subtract, h2)
                    dv.tt(k[A, 1, 288:320], ps[B, 256:288], k[B, 1, 288:320].bitcast(F32), ALU.subtract)
                    for z in (k[:, 0, 288:320], k[:, 1, 256:288], k[B, 0, 320:352], k[A, 0, 352:384]):
                        dv.op(lambda e, z=z: e.memset(z.bitcast(F32), 0.0))
                    dv.copy(k[A, 0, 320:352], k[A, 0, 256:288].bitcast(F32))
                    r = dv.copy(k[B, 0, 352:384], k[B, 1, 288:320].bitcast(F32), up="k")
                ring.free(sk, r)
                for f in more:
                    f()
                k_ready[n] = r
                n_ = 512 if w_ == 512 else 320
                for rows, hh in ((A, 0), (B, 1)):
                    x_ = k[rows, hh, 0:n_].bitcast(F32)
                    t2 = gp.tt(sqk[b][rows, 0:n_], x_, x_, ALU.mult, h1, h2, None if w_ == 512 else r, sqk_free[b], w1_used)
                sqk_t[b] = k1_sq[b] = t2

            return rest

        def v_part(n, lo, early=False):
            b, (p, m) = n % NKVB, divmod(n, NCH)
            tiles = range(4 * m + lo, min(4 * m + lo + 2, NKT))
            s, ps, fr = ring.take(1)
            for j, kt in enumerate(tiles):
                mw = 128 if kt < KT else 64
                a = 128 * (lo + j)
                for k, (i, j_) in enumerate(PARTS):
                    t = pe.mm(ps[0:mw, 256 * j:256 * j + 256], CP[b][j_][:, a:a + mw], WKV[i][:, 1024 + 128 * p:1280 + 128 * p], fr,
                              cp_t[n], kv_free["w"], start=k == 0, stop=k == 2, up="proj")
            cp_free[b] = t

            def rest():
                rows = slice(0, 128 if tiles[-1] < KT else 64)
                free = [kv_free.get(("v", b)), vs_free.get(m), w1_used]
                for dst, at in ((V1[b][:, 128 * lo:128 * (lo + len(tiles))].rearrange("p (i c) -> p i c", c=128), 0),
                                (Vs[:, tiles[0]:tiles[-1] + 1], 128)):
                    src = ps[:, 0:256 * len(tiles)].rearrange("p (i c) -> p i c", c=256)[:, :, at:at + 128]
                    if early and lo == 0:
                        r = ac.act(dst, src, ACT.Copy, t, free, up="v")
                    else:
                        r = dv.copy(dst[rows], src[rows], t, free, up="v")
                ring.free(s, r)
                v_ready.setdefault(n, []).append(r)

            return rest

        def k_norm(g):
            s, ps, fr = ring.take(1)
            ns = [n for n in range(NKVB * g, NKVB * g + NKVB) if n < 8 * NCH]
            ends = [n % NCH == NCH - 1 for n in ns]
            for b, end in enumerate(ends):
                n_ = 320 if end else 512
                t = pe.mm(ps[32 * b:32 * b + 32, 0:n_], sel2[:], sqk[b][:, 0:n_], sqk_t[b], fr, kv_free["c"], up="nk")
                sqk_free[b] = t
            n_ = 320 if any(ends) else 512
            r = slice(0, 32 * len(ns))
            t = dv.op(lambda e, r=r: e.tensor_reduce(mky[r, g:g + 1], ps[r, 0:n_], AX, ALU.max), t, up="mky")
            for b, end in enumerate(ends):
                if n_ < 512 and not end:
                    r, col = slice(32 * b, 32 * b + 32), 36 + ns[b] // NCH
                    t = dv.op(lambda e, r=r, col=col: e.tensor_reduce(mky[r, col:col + 1], ps[r, n_:512], AX, ALU.max),
                              up="mky")
            ring.free(s, t)


        def three(ps, k, w_t, w_, col, fr, src, src_t, rows=slice(0, 128)):
            (wh, wl), (sh, sl) = w_, src
            for n, (p, q) in enumerate(((wh, sh), (wh, sl), (wl, sh))):
                for a, b in chunks(T):
                    t = pe.mm(ps[:, a:b], p[:, col], q[:, a:b], fr, src_t[n == 1][a // 512], w_t, start=n == 0, stop=n == 2, up=k)
            return t

        def hidden(n):
            b = n % 2
            bias = first_weights(n)[1]
            for cc in range(4):
                s, ps, fr = ring.take()
                t = three(ps, "h", w_t[n], WS[b], slice(128 * cc, 128 * cc + 128), fr, (xh, xl), xs_t)
                r = ac.act(H[b][:, cc, :], ps, ACT.Relu, t, h_free[b], bias=bias[:, cc:cc + 1], up="hidden")
                ring.free(s, r)
                if cc == 1 and n < E:
                    split_weights(n + 1)
            ws_free[b] = t
            return r

        def experts_out(e, h_t):
            s, ps, fr = ring.take()
            y_t, before = [], x_t
            for i in range(NT):
                for cc in range(4):
                    t = pe.mm(ps[:, 128 * i:128 * i + 128], H[(e + 1) % 2][:, cc, 128 * i:128 * i + 128],
                              W2f[:, 512 * e + 128 * cc:512 * e + 128 * cc + 128], h_t, fr, w2_in, start=cc == 0,
                              stop=cc == 3, up="y")
                y_t.append(t)
            h_free[(e + 1) % 2] = t

            def add(h):
                dv.wait(y_t[4 * h + 3], g_t, xn_t, before)
                for i in range(4 * h, 4 * h + 4):
                    t = dv.stt(X[:, i, :], ps[:, 128 * i:128 * i + 128], G[:, i, e:e + 1], X[:, i, :], ALU.mult, ALU.add,
                               up="y")
                ring.free(s, t)
                return t

            return [add(0), (lambda: add(1)) if e == E - 1 else add(1)]

        w1_used = []
        h_t = hidden(0)
        nxt = hidden(1)
        s, ps, fr = ring.take()
        share = []
        for a, b in chunks(T):
            for cc in range(4):
                t = pe.mm(ps[32 * cc:32 * cc + 32, a:b], wf("rw2")[:, 32 * cc:32 * cc + 32], H[0][:, cc, a:b], h_t, fr,
                          up="sc")
            share.append(ac.act(xT[:, a:b], ps[:, a:b], ACT.Copy, t, xs_t, up="share"))
        h_free[0] = t
        ring.free(s, share[1])
        s, ps, fr = ring.take(1)
        for i in range(NT):
            t = pe.mm(ps[:, 8 * i:8 * i + 8], xT[:, 128 * i:128 * i + 128], c("sel8"), share[i // 4], fr, up="sc")
        r, g_t = gates(G, ps[:, 0:64], wf("rb2"), t, wf0_in, None, gb)
        ring.free(s, r)
        for e in range(E):
            h_t = nxt
            if e < E - 1:
                nxt = hidden(e + 2)
            if e == 2:
                split_kv_weights()
            if 3 <= e < 3 + NKVB:
                split_ctx(e - 3, dv)
            if e == E - 1:
                w1_used += [w_t[E]]
            if e == 1:
                gt_t = transposed_gates(G, GT, g_t, x0_end)
                s, ps, fr = ring.take()
                for i in range(NT):
                    t = pe.mm(ps[:, 128 * i:128 * i + 128], GT[:, 128 * i:128 * i + 128], wf("b2", 8), fr, gt_t, wf0_in,
                              up="b2")
                r = dv.tt(xf, xf, ps, ALU.add, t, x_t, up="res")
                x_t = [r, r]
                ring.free(s, r)
            x_t = experts_out(e, h_t)
        f0_pe = h_free[E % 2]
        idle.append(lambda: kv_chunk(0, True))

        b1 = Region(glob.at)
        lat = b1("lat", [33, T])
        QK = b1("QK", [128, NT, 32, 8])
        QR = b1("QR", [128, NT, 32, 8])
        Vt = b1("Vt", [128, NT, D])
        R1 = b1("R1", [128, NT, 32, 4])
        R2 = b1("R2", [128, NT, 32, 4])
        pr = [b1(f"pr{i}", [128, 2048]) for i in range(3)]
        att = b1("att", [128, NT, 16, 16])
        mx = b1("mx", [128, NT, 16])
        sm = b1("sm", [128, NT, 16])
        f0_end = [f0_pe, x_t, h_free]

        def wbs(a, rows=128):
            return WBs[0:rows, WB[a][0]:WB[a][1]]

        xn_t, xT_t = layernorm(x_t, None)
        lat1 = gp.op(lambda e: e.memset(lat[32:33, :], 1.0), f0_end)
        l_t, q_t, k_t = [], [], []
        for h in range(2):
            s, ps, fr = ring.take(1)
            a, b = 512 * h, 512 * h + 512
            t = pe.mm(ps[0:32, :], wbs("down"), xT[:, a:b], fr, xT_t[h], wb_in, up="proj")
            l_t.append(ac.act(lat[0:32, a:b], ps[0:32, :], ACT.Identity, t, f0_end, bias=wbs("bdown", 32), up="proj"))
            ring.free(s, l_t[h])
            s, ps, fr = ring.take(1)
            for i in range(4):
                o = ps[:, 128 * i:128 * i + 128]
                t = pe.mm(o, xT[:, 512 * h + 128 * i:512 * h + 128 * i + 128], wbs("q"), fr, xT_t[h], wb_in, up="proj")
            q_t.append(dv.tt(QK[:, 4 * h:4 * h + 4, 0:16, :].rearrange("p i h d -> p i (h d)"),
                             ps.rearrange("p (i c) -> p i c", i=4), wbs("bq").unsqueeze(1).to_broadcast([128, 4, 128]),
                             ALU.add, t, f0_end, up="proj"))
            ring.free(s, q_t[h])
            s, ps, fr = ring.take()
            for i in range(4):
                t = pe.mm(ps[:, 256 * i:256 * i + 256], lat[:, 512 * h + 128 * i:512 * h + 128 * i + 128], wbs("up", 33),
                          fr, l_t[h], lat1, up="proj")
            p3 = ps.rearrange("p (i c) -> p i c", i=4)
            k = ac.act(QK[:, 4 * h:4 * h + 4, 16:32, :].rearrange("p i h d -> p i (h d)"), p3[:, :, 0:128], ACT.Copy, t,
                       up="proj")
            k_t.append(ac.act(Vt[:, 4 * h:4 * h + 4, :], p3[:, :, 128:256], ACT.Copy, up="proj"))
            ring.free(s, k_t[h])


        def rope(lane, h, tiles):
            n = tiles.stop - tiles.start
            cs = {k: c(k).rearrange("p (i f) -> p i f", i=NT)[:, tiles].unsqueeze(2).to_broadcast([128, n, 32, 4])
                  for k in ("cos", "sin")}
            x1, x2 = QK[:, tiles, :, 0:4], QK[:, tiles, :, 4:8]
            t = None
            for d, (a, b, o) in enumerate((("cos", "sin", ALU.subtract), ("sin", "cos", ALU.add))):
                t1 = lane.tt(R1[:, tiles], x1, cs[a], ALU.mult, q_t[h], k_t[h], f0_end, c_in, t, up="rope")
                t2 = lane.tt(R2[:, tiles], x2, cs[b], ALU.mult, up="rope")
                t = lane.tt(QR[:, tiles, :, 4 * d:4 * d + 4], R1[:, tiles], R2[:, tiles], o, t1, t2, up="rope")
            return t

        r_t = {}
        ON_POOL1, ON_POOL2, ON_DVE1, ON_DVE2 = (1, 3, 5, 7), (2, 5, 7), (0,), (1, 3, 4, 6)
        ropes = {0: [(slice(0, 1), dv), (slice(1, 2), gp)], 1: [(slice(2, 4), dv)], 3: [(slice(4, 6), gp)],
                 5: [(slice(6, 8), dv)]}
        pr_free = [None, None, None]
        npr = [0]

        def product(lane, out4, a, b, *tok):
            k = npr[0] % 3
            npr[0] += 1
            t = lane.tt(out4(pr[k]), a, b, ALU.mult, pr_free[k], *tok, up="prod")
            return k, t

        def sums(k, t, on_dve, dst, view, n, slices):
            if on_dve:
                pr_free[k] = dv.op(lambda e: e.tensor_reduce(dst, view(pr[k]), AX, ALU.add), t, up="red")
                return dst, pr_free[k], None
            s, ps, fr = ring.take(1)
            m = view(pr[k])
            for j in range(slices):
                tt_ = pe.mm(ps[:, 0:n], ident, m[:, :, :, j], fr, t, start=j == 0, stop=j == slices - 1, up="red")
            pr_free[k] = tt_
            return ps[:, 0:n].rearrange("p (a b) -> p a b", a=16), tt_, s

        state = {}

        def scores(i):
            v = lambda p: p[:].rearrange("p (h g d) -> p h g d", h=16, g=16)
            k, t = product(gp if i in ON_POOL1 else dv, v, QR[:, i, 0:16, :].unsqueeze(2).to_broadcast([128, 16, 16, 8]),
                           QR[:, i, 16:32, :].unsqueeze(1).to_broadcast([128, 16, 16, 8]), r_t[i])
            state[i] = sums(k, t, i in ON_DVE1, att[:, i], v, 256, 8)

        def softmax(i):
            a, t, s = state[i]
            t = dv.op(lambda e: e.tensor_reduce(mx[:, i], a, AX, ALU.max), t, up="soft")
            t = dv.tt(att[:, i], a, mx[:, i].unsqueeze(2).to_broadcast([128, 16, 16]), ALU.subtract, t, up="soft")
            if s is not None:
                ring.free(s, t)
            state[i] = ac.act(att[:, i], att[:, i], ACT.Exp, t, scale=SC, up="att")

        def values(i):
            v = lambda p: p[:].rearrange("p (h d g) -> p h d g", h=16, d=8)
            k, t = product(gp if i in ON_POOL2 else dv, v, att[:, i].unsqueeze(2).to_broadcast([128, 16, 8, 16]),
                           Vt[:, i].rearrange("p (g d) -> p d g", d=8).unsqueeze(1).to_broadcast([128, 16, 8, 16]), state[i])
            t2 = dv.op(lambda e: e.tensor_reduce(sm[:, i], att[:, i], AX, ALU.add), state[i], up="soft")
            t2 = dv.op(lambda e: e.reciprocal(sm[:, i], sm[:, i]), t2, up="soft")
            state[i] = (t2,) + sums(k, t, i in ON_DVE2, mx8[:, i], v, 128, 16)

        def outs(i):
            t2, a, t, s = state[i]
            on_t[i // 4] = dv.tt(On[:, i].rearrange("p (h d) -> p h d", d=8), a,
                                 sm[:, i].unsqueeze(2).to_broadcast([128, 16, 8]), ALU.mult, t, t2, on_t[i // 4], up="on")
            if s is not None:
                ring.free(s, on_t[i // 4])

        mx8 = b1("mx8", [128, NT, 16, 8])
        for i in range(NT + 3):
            for tiles, lane in ropes.get(i, []):
                t = rope(lane, tiles.start // 4, tiles)
                for j in range(tiles.start, tiles.stop):
                    r_t[j] = t
            for k, f in enumerate((scores, softmax, values, outs)):
                if 0 <= i - k < NT:
                    f(i - k)
        bo_t = gp.tt(X[:], X[:], wbs("bout").unsqueeze(1).to_broadcast([128, NT, D]), ALU.add, xn_t, wb_in)
        x_t = out_proj(wbs("out"), wb_in, bo_t)
        b1_end = [x_t, osb_free]

        x1l = Region(glob.at)
        y_region = x1l.at
        Q1 = [x1l(f"Q1{i}", [128, 2, T], F32R) for i in range(2)]
        Q2 = [x1l(f"Q2{i}", [128, T], F32R) for i in range(2)]
        acc = [x1l(f"acc{i}", [128, T]) for i in range(4)]
        rsy = [x1l(f"rsy{i}", [128, 512]) for i in range(2)]
        sqq = x1l("sqq", [128, T], BF16)
        NPY = 6
        Py = [x1l(f"Py{i}", [128, T]) for i in range(NPY)]
        assert x1l.at <= KV_at, (x1l.at, KV_at)
        wr_in = {0: sp.dma(WR[0][:], f1w[0], b1_end, up="wr0")}
        sqq_free = [b1_end]
        q1_sq = [None, None]

        xn_t, xT_t = layernorm(x_t, None)
        x_t = gp.tt(X[:], X[:], wys("b", 0, 128).unsqueeze(1).to_broadcast([128, NT, D]), ALU.add, xn_t, wy_in)
        pf = [b1_end] * NPY
        acc_free = [b1_end, b1_end]
        q1_free = [b1_end, b1_end]
        osb1_free = [b1_end, b1_end]
        oy_free = [[b1_end, b1_end]]
        Y = On
        Yf = On[:].rearrange("p i d -> p (i d)")
        rsy_free = [b1_end, b1_end]
        y_t = [b1_end, b1_end]
        q_ready, norms = {}, {}

        def q_half(p, h):
            q1, q2 = Q1[p % 2], Q2[p % 2]
            c_ = slice(512 * h, 512 * h + 512)
            s, ps, fr = ring.take(1)
            t = pe.mm(ps, wys("q", 128 * p, 128), xT[:, c_], fr, xT_t[h], wy_in, up="proj")
            f = [q1_free[p % 2], q1_sq[p % 2]]
            h1 = ac.act(q1[A, 0, c_], ps[A, :], ACT.Copy, t, f, up="qh")
            h2 = ac.act(q1[B, 1, c_], ps[B, :], ACT.Copy, up="qh")
            dv.tt(q2[A, c_], ps[A, :], q1[A, 0, c_].bitcast(F32), ALU.subtract, h1, f)
            r = dv.tt(q2[B, c_], ps[B, :], q1[B, 1, c_].bitcast(F32), ALU.subtract, h2, up="q")
            ring.free(s, r)
            if p == 0:
                ac.act(q1[B, 0, c_], q1[A, 0, c_].bitcast(F32), ACT.Copy, h1)
                q_ready[p, h] = [r, ac.act(q1[A, 1, c_], q1[B, 1, c_].bitcast(F32), ACT.Copy, h2, up="qh")]
            else:
                dv.copy(q1[B, 0, c_], q1[A, 0, c_].bitcast(F32))
                q_ready[p, h] = dv.copy(q1[A, 1, c_], q1[B, 1, c_].bitcast(F32), up="q")
            for rows, hh in ((A, 0), (B, 1)):
                t = gp.tt(sqq[rows, c_], q1[rows, hh, c_].bitcast(F32), q1[rows, hh, c_].bitcast(F32), ALU.mult, h1, h2,
                          sqq_free[0])
            if h == 1:
                q1_sq[p % 2] = t

        def q_norm(p):
            s, ps, fr = ring.take(1)
            for a, b in chunks(T):
                r0 = 32 * (a // 512)
                t2 = pe.mm(ps[r0:r0 + 32, :], sel2[:], sqq[:, a:b], q1_sq[p % 2], fr, kv_free["c"], up="nq")
            sqq_free[0] = t2
            ring.free(s, dv.op(lambda e: e.tensor_reduce(mqy[:, p:p + 1], ps[0:64, :], AX, ALU.max), t2, up="mqy"))

        def norm_flag1():
            s, ps, fr = ring.take()
            t = dv.op(lambda e: e.tensor_reduce(mkp[:], mky[:], AX, ALU.max), dv.now("mky"), up="nm")
            pe.tr(ps[0:1, 0:128], mkp[:], ident, t, fr)
            t = dv.op(lambda e: e.tensor_reduce(mqp[:], mqy[:], AX, ALU.max), dv.now("mqy"), up="nm")
            t = pe.tr(ps[0:1, 128:192], mqp[:], ident[0:64, 0:64], t, up="nm")
            dv.op(lambda e: e.tensor_reduce(fl[:, 0:1], ps[0:1, 0:128], AX, ALU.max), t)
            t = dv.op(lambda e: e.tensor_reduce(fl[:, 1:2], ps[0:1, 128:192], AX, ALU.max), up="nm")
            t = dv.tt(fl[:, 0:1], fl[:, 0:1], fl[:, 1:2], ALU.mult, t, up="nm")
            fl_t[2] = compare(2, fl[:, 0:1], 0.125, True, t)
            ring.free(s, t)

        def finish_sums(p, h, acc_t, osb_t):
            c_ = slice(512 * h, 512 * h + 512)
            s, ps, fr = ring.take(1)
            for k, rows in enumerate((A, B)):
                t = pe.mm(ps[rows, :], c("one").to_broadcast([128, 64]), acc[2 * (p % 2) + k][:, c_], acc_t, fr, up="sum")
            if h == 1:
                acc_free[p % 2] = t
            t = ac.act(rsy[h][:], ps, ACT.Copy, t, rsy_free[h], up="rsy")
            ring.free(s, t)

            def invert(k):
                v = rsy[h][:, 256 * k:256 * k + 256]
                r = dv.op(lambda e: e.reciprocal(v, v), t, up="rsy")
                if k:
                    norms[p, h] = rsy_free[h] = gp.tt(Osb[:, c_], Osb[:, c_], rsy[h][:], ALU.mult, r, osb_t[h])

            invert(0)
            todo.insert(0, lambda: invert(1))

        def finish_proj(p, h):
            c_ = slice(512 * h, 512 * h + 512)
            s, ps, fr = ring.take(1)
            for i in range(4):
                t = pe.mm(ps[:, 128 * i:128 * i + 128], Osb[:, 512 * h + 128 * i:512 * h + 128 * i + 128],
                          wys("out", 128 * p, 128), norms[p, h], fr, up="yp")
            osb1_free[h] = t
            y_t[h] = dv.tt(Yf[:, c_], (Yf if p else xf)[:, c_], ps, ALU.add, t, y_t[h], x_t, up="y1")
            ring.free(s, y_t[h])

        def finish_last(acc_t, osb_t):
            s, ps, fr = ring.take(1)
            for h in range(2):
                for k in range(2):
                    r = 64 * h + 32 * k
                    t = pe.mm(ps[r:r + 32, :], c("one").to_broadcast([128, 32]), acc[2 + k][:, 512 * h:512 * h + 512],
                              acc_t, fr, up="sum")
            sum_t = ac.act(rsy[0][:], ps, ACT.Copy, t, rsy_free[0], up="rsy")
            ring.free(s, sum_t)
            ps_ = []
            for h in range(2):
                for k in range(2):
                    s, ps, fr = ring.take(1)
                    for i in range(4 * h, 4 * h + 4):
                        t = pe.mm(ps[:, 128 * (i % 4):128 * (i % 4) + 128], Osb[64 * k:64 * k + 64, 128 * i:128 * i + 128],
                                  wys("out", 128 * 7, 128, 64 * k, 64 * k + 64), osb_t[h], fr, up="yp")
                    ps_.append((s, ps, t))
                if h == 0:
                    s, ps, fr = ring.take(1)
                    for i in range(4):
                        t = pe.tr(ps[:, 128 * i:128 * i + 128], rsy[0][:, 128 * i:128 * i + 128], ident, sum_t, fr, up="sum")
                    v = ps.rearrange("p (i q c) -> p q i c", i=4, c=32)[:, :, :, 0]
                    r_t = dv.op(lambda e: e.reciprocal(rs[:, 0:16].rearrange("p (q i) -> p q i", i=4), v), t, up="rsy")
                    ring.free(s, r_t)
            for h in range(2):
                for k in range(2):
                    s, ps, t = ps_[2 * h + k]
                    dv.wait(t, r_t, y_t[h])
                    for i in range(4 * h, 4 * h + 4):
                        col = 4 * (2 * h + k) + i % 4
                        y_t[h] = dv.stt(Y[:, i, :], ps[:, 128 * (i % 4):128 * (i % 4) + 128], rs[:, col:col + 1], Y[:, i, :],
                                        ALU.mult, ALU.add, up="y1")
                    ring.free(s, y_t[h])

        todo = []
        pend = []
        un = 0
        q_half(0, 0)
        q_half(0, 1)
        for p in range(8):
            ac_t = [None, None]
            for kt in range(NKT):
                m, i = divmod(kt, 4)
                n = NCH * p + m
                b = n % NKVB
                k, kt_, vt_ = K1[b], k_ready[n], v_ready[n]
                q1, q2 = Q1[p % 2], Q2[p % 2]
                last = kt == KT
                sA, pA, fA = ring.take()
                if last:
                    for j, (lhs, q) in enumerate(((k[:, 0, 256:320], q1[:, 0]), (k[:, 1, 256:320], q1[:, 1]),
                                                  (k[:, 0, 320:384], q2[:]))):
                        for a, bb in chunks(T):
                            t = pe.mm(pA[0:64, a:bb], lhs, q[:, a:bb], fA, kt_, start=j == 0, stop=j == 2, up="sA")
                    kv_free["k", b] = q1_free[p % 2] = t
                    heads = [(sA, pA, t)]
                else:
                    sB, pB, fB = ring.take()
                    cols = slice(128 * i, 128 * i + 128)
                    for h, (ps, fr) in enumerate(((pA, fA), (pB, fB))):
                        for a, bb in chunks(T):
                            pe.mm(ps[:, a:bb], k[:, h, cols], q1[:, h, a:bb], fr, kt_, q_ready[p, a // 512], start=True,
                                  stop=False)
                    for a, bb in chunks(T):
                        tA = pe.mm(pA[:, a:bb], k[A, 0, cols], q2[A, a:bb], start=False, stop=True, up="sA")
                        tB = pe.mm(pB[:, a:bb], k[B, 1, cols], q2[B, a:bb], start=False, stop=True, up="sA")
                    kv_free["k", b] = q1_free[p % 2] = tB
                    heads = [(sA, pA, tA), (sB, pB, tB)]
                es = []
                for s, ps, t in heads:
                    pb = un % NPY
                    un += 1
                    r = slice(0, 64) if last else slice(0, 128)
                    t = ac.act(Py[pb][r, :], ps[r, :], ACT.Exp, t, pf[pb], scale=0.125, up="ey")
                    ring.free(s, t)
                    es.append([pb, t])
                if last:
                    es.append(list(es[0]))
                for h in range(2):
                    r = slice(32 * h, 32 * h + 4) if last else slice(0, 128)
                    ac_, py, t = acc[2 * (p % 2) + h], Py[es[h][0]], es[h][1]
                    if kt == 0:
                        ac_t[h] = dv.copy(ac_[:], py[:], t, acc_free[p % 2], up="acc")
                    else:
                        ac_t[h] = dv.tt(ac_[r, :], ac_[r, :], py[r, :], ALU.add, t, ac_t[h], up="acc")
                    es[h].append(ac_t[h])

                rows = [slice(32 * h, 32 * h + 4) if last else slice(0, 128) for h in range(2)]
                if p % 2 == 0:
                    vals = [V1[b][rows[h], 128 * i + 64 * h:128 * i + 64 * h + 64] for h in range(2)]
                else:
                    vals = [Vs[rows[h], kt, 64 * h:64 * h + 64] for h in range(2)]

                def pv(p=p, kt=kt, m=m, rows=rows, vals=vals, b=b, es=es, vt_=vt_):
                    last = []
                    for a, bb in chunks(T):
                        for h in range(2):
                            t = pe.mm(O[64 * h:64 * h + 64, a:bb], vals[h],
                                      Py[es[h][0]][rows[h], a:bb], es[h][1], vt_, oy_free[0][a // 512], start=kt == 0,
                                      stop=kt == NKT - 1, skip=True, up="pvy")
                        last.append(t)
                    if p % 2 == 0:
                        kv_free["v", b] = t
                    else:
                        vs_free[m] = t
                    for pb, _, t2 in es:
                        pf[pb] = [t, t2]
                    if kt == NKT - 1:
                        o = [ac.act(Osb[:, a:bb], O[:, a:bb], ACT.Copy, last[a // 512], osb1_free[a // 512], up="osb")
                             for a, bb in chunks(T)]
                        oy_free[0] = o
                        acc_t = [es[0][2], es[1][2]]
                        if p == 7:
                            finish_last(acc_t, o)
                            return
                        todo.extend([lambda: finish_sums(p, 0, acc_t, o), lambda: finish_sums(p, 1, acc_t, o),
                                     lambda: finish_proj(p, 0), lambda: finish_proj(p, 1)])

                pend.append(pv)
                if len(pend) > 1:
                    pend.pop(0)()
                new = len(k_ready)
                if new < 8 * NCH and (i == 0 and new < n + NKVB or i == 2 and new < n + NKVB - 1):
                    kv_chunk(new)()
                    if new // NCH % 2 == 0:
                        todo.insert(0, lambda n=new: v_part(n, 2)())
                    if new + 1 < 8 * NCH and new + 1 not in cp_t:
                        split_ctx(new + 1, gp)
                    if new % NKVB == NKVB - 1 or new == 8 * NCH - 1:
                        todo.insert(1 if new // NCH % 2 == 0 else 0, lambda g=new // NKVB: k_norm(g))
                elif todo:
                    todo.pop(0)()
                if kt == 0 and p == 0:
                    todo.append(lambda: q_norm(0))
                if kt == 46 and p == 7:
                    todo.append(norm_flag1)
                    todo.append(lambda: fl_r.update({2: load_flags(2)}))
                if kt == 36 and p < 7:
                    todo.append(lambda p=p: q_half(p + 1, 0))
                    todo.append(lambda p=p: q_half(p + 1, 1))
                    todo.append(lambda p=p: q_norm(p + 1))
        pend.pop(0)()
        general("gy", y_region, 64, ctxT, 97, S, gy, 321, 0.125, False, On[:], X[:], fl_r[2],
                flat(ring.freed, y_t, pf, acc_free, oy_free, osb1_free))
        x1_end = [pf, acc_free, osb1_free, y_t]

        f1 = Region(glob.at)
        WT = [[f1(f"wt{i}{k}", [128, 3, F], F32R) for k in range(2)] for i in range(2)]
        XE = [[f1(f"xe{i}{k}", [128, T], F32R) for k in range(2)] for i in range(2)]
        xg = f1("xg", [128, NT, D])
        th = [f1(f"th{i}", [128, T]) for i in range(2)]
        HF = [f1(f"hf{i}", [128, T]) for i in range(2)]
        HS = [[f1(f"hs{i}{k}", [128, T], F32R) for k in range(2)] for i in range(4)]
        G1 = f1("G1", [128, NT, 8])
        gb1 = gate_bufs(f1, 1)
        WR.append(f1("WR1", [128, 3, F]))
        assert f1.at <= WR_at, (f1.at, WR_at)
        wt_free, wt_t = [x1_end, x1_end], {}
        wr_in[1] = sp.dma(WR[1][:], f1w[1], x1_end, up="wr1")

        def weights(e, *which):
            b = e % 2
            for k in which:
                t = ac.act(WT[b][0][:, k], WR[b][:, k], ACT.Copy, wr_in[e], wt_free[b], up="wt")
                t2 = gp.tt(WT[b][1][:, k], WR[b][:, k], WT[b][0][:, k].bitcast(F32), ALU.subtract, t)
                wt_t[e, k] = [t, t2]
            if k == 2 and e + 2 < E:
                wr_in[e + 2] = sp.dma(WR[b][:], f1w[e + 2], t, t2, up=f"wr{b}")

        xn_t, xT_t = layernorm(y_t, None, Y)
        weights(0, 0, 1, 2)
        s, ps, fr = ring.take(1)
        for i in range(NT):
            t = pe.mm(ps[:, 8 * i:8 * i + 8], xT[:, 128 * i:128 * i + 128], WF1s[:, 0:8], fr, xT_t[i // 4], wf1_in, up="lg")
        r, g_t = gates(G1, ps[:, 0:64], WF1s[:, 8:16], t, wf1_in, x1_end, gb1)
        ring.free(s, r)
        x_t = gp.tt(X[:], Y[:], xn[:], ALU.add, xn_t, y_t)
        xe_free, xg_free = [x1_end, x1_end], x1_end
        xe_t, xg_t = {}, {}

        def gated(e):
            xg_t[e] = [dv.tt(xg[:, i:i + 4], xn[:, i:i + 4], G1[:, i:i + 4, e:e + 1].to_broadcast([128, 4, D]), ALU.mult, g_t,
                             xg_free, up="xe") for i in (0, 4)]

        def tokens_in(e):
            nonlocal xg_free
            xe_t[e] = [[], []]
            b = e % 2
            for h in range(2):
                c_ = slice(512 * h, 512 * h + 512)
                s, ps, fr = ring.take(1)
                for i in range(4):
                    t = pe.tr(ps[:, 128 * i:128 * i + 128], xg[:, 4 * h + i, :], ident, xg_t[e][h], fr, up="xT")
                hi = ac.act(XE[b][0][:, c_], ps, ACT.Copy, t, xe_free[b], up="xe")
                lo_ = dv.tt(XE[b][1][:, c_], ps, XE[b][0][:, c_].bitcast(F32), ALU.subtract, hi, up="xe")
                ring.free(s, lo_)
                xe_t[e][0].append(hi)
                xe_t[e][1].append(lo_)
            xg_free = t

        gated(0)
        tokens_in(0)
        th_free, hf_free, hs_free = [x1_end] * 2, [x1_end] * 2, [x1_end] * 4
        outs_ = []
        o1_free = flat(oy_free)

        def expert_out(e, cc, u, h_t):
            t = None
            hs = HS[u % 4]
            col = slice(128 * cc, 128 * cc + 128)
            for n, (p, q) in enumerate(((0, 0), (0, 1), (1, 0))):
                for a, b in chunks(T):
                    t = pe.mm(O[:, a:b], WT[e % 2][p][:, 2, col], hs[q][:, a:b], wt_t[e, 2], h_t[q], o1_free,
                              start=(u, n) == (0, 0), stop=(u, n) == (4 * E - 1, 2), skip=True, up="y")
            hs_free[u % 4] = t
            if cc == 3:
                wt_free[e % 2] = t
            return t

        def parts(e, cc, u, h):
            hs = HS[u % 4]
            hi = ac.act(hs[0][:], HF[u % 2][:], ACT.Copy, h, hs_free[u % 4], up="hs")
            lo_ = gp.tt(hs[1][:], HF[u % 2][:], hs[0][:].bitcast(F32), ALU.subtract, hi)
            hf_free[u % 2] = lo_
            outs_.append(lambda: expert_out(e, cc, u, [hi, lo_]))

        for u in range(4 * E):
            e, cc = divmod(u, 4)
            b = e % 2
            col = slice(128 * cc, 128 * cc + 128)
            part = []
            for k in range(2):
                s, ps, fr = ring.take()
                t = three(ps, "u", wt_t[e, k], (WT[b][0][:, k], WT[b][1][:, k]), col, fr, XE[b], xe_t[e])
                part.append((s, ps, t))
            (su, pu, tu), (sv, pv_, tv) = part
            k = u % 2
            t = ac.act(th[k][:], pu, ACT.Tanh, tu, th_free[k], scale=0.5, up="th")
            t = dv.stt(th[k][:], th[k][:], 1.0, pu, ALU.add, ALU.mult, t, up="hidden")
            ring.free(su, t)
            h = dv.stt(HF[k][:], th[k][:], 0.5, pv_, ALU.mult, ALU.mult, t, tv, hf_free[k], up="hidden")
            th_free[k] = h
            ring.free(sv, h)
            if u:
                parts(*was)
            was = (e, cc, u, h)
            if cc == 3:
                xe_free[b] = tv
            if cc == 0 and e + 1 < E:
                gated(e + 1)
            if cc == 2 and e + 1 < E:
                tokens_in(e + 1)
            if len(outs_) > 1:
                t = outs_.pop(0)()
            if cc and e + 1 < E:
                weights(e + 1, cc - 1)
        parts(*was)
        while outs_:
            t = outs_.pop(0)()
        xt_ = []
        for h in range(2):
            c_ = slice(512 * h, 512 * h + 512)
            o = ac.act(Osb[:, c_], O[:, c_], ACT.Copy, t, osb1_free[h], up="osb")
            s, ps, fr = ring.take(1)
            for i in range(4):
                t2 = pe.tr(ps[:, 128 * i:128 * i + 128], Osb[:, 512 * h + 128 * i:512 * h + 128 * i + 128], ident, o, fr,
                           up="otr")
            xt_.append(dv.tt(xf[:, c_], xf[:, c_], ps, ALU.add, t2, x_t, up="res"))
        x_t = xt_

        res_v = out.rearrange("a (i p) d -> p (a i) d", p=128)
        o_t = [sp.dma(res_v[:, 4 * h:4 * h + 4], X[:, 4 * h:4 * h + 4], x_t[h], up="out") for h in range(2)]
        sp.wait(o_t, *stores)

        with nc.Block() as block:
            @block.tensor
            def _(e):
                for f in pe.queue:
                    f(e)

            @block.scalar
            def _(e):
                for f in ac.queue:
                    f(e)

            @block.vector
            def _(e):
                for f in dv.queue:
                    f(e)

            @block.gpsimd
            def _(e):
                for f in gp.queue:
                    f(e)

            @block.sync
            def _(e):
                for f in sp.queue:
                    f(e)


def constants():
    c = np.zeros((128, NCST), np.float32)

    def put(name, v):
        c[:, CST[name][0]:CST[name][1]] = v

    q = np.arange(128)
    r = q % 32
    put("id", np.eye(128))
    low = (r >= 16) & (r < 24)
    put("qs", np.where(low, -1, 1)[:, None])
    put("qb", np.where(low, 1, 0)[:, None])
    low = (r >= 8) & (r < 16)
    put("ks", np.where(low, -1, 1)[:, None])
    put("kb", np.where(low, 1, 0)[:, None])
    put("mh", -0.5)
    inv = (1.0 / 10000.0 ** (np.arange(0, 8, 2, dtype=np.float32) / np.float32(8))).astype(np.float32)
    freq = np.arange(T, dtype=np.float32)[:, None] * inv[None]
    freq = freq.reshape(NT, 128, 4).transpose(1, 0, 2).reshape(128, NT * 4)
    put("cos", np.cos(freq))
    put("sin", np.sin(freq))
    put("iota", np.arange(8)[None])
    put("one", 1)
    put("selh", q[:, None] // 8 == np.arange(32)[None])
    put("sel2", q[:, None] // 64 == np.arange(32)[None])
    put("sel8", r[:, None] == np.arange(8)[None])
    g = np.zeros((128, T + NT), np.float32)
    g[:, :T] = np.arange(T)[None]
    g[:, T:] = q[:, None] + 128 * np.arange(NT)[None]
    return c, g


def layout(I):
    A = {"x": I["x"], "ctx_in": I["ctx_768"]}
    A["cst"], A["gc"] = constants()

    def z(*s):
        return np.zeros(s, np.float32)

    def rep(w):
        o = z(w.shape[0], 4, 32)
        v = w[:, 0:32].reshape(-1, 4, 8)
        for k in range(3):
            o[..., 8 * k:8 * k + 8] = v
        return o.reshape(w.shape[0], 128)

    def put(dst, table, name, v):
        dst[0:v.shape[0], table[name][0]:table[name][1]] = v

    w = A["wa"] = z(128, NWA)
    put(w, WA, "q0", rep(I["L0_attn_w_q"].T))
    put(w, WA, "k0", rep(I["L0_attn_w_k"].T))
    for n in "qkvo":
        put(w, WA, n, I["L0_attn_w_" + n].T)
    w = A["wx"] = z(128, NWX)
    put(w, WX, "q0", rep(I["L0_xattn_wq"]))
    put(w, WX, "q", I["L0_xattn_wq"])
    put(w, WX, "k", I["L0_xattn_wk"])
    w[96, WX["k"][0]:WX["k"][1]] = I["L0_xattn_bk"]
    v = z(97, 16, 9)
    v[:96, :, :8] = I["L0_xattn_wv"].reshape(96, 16, 8)
    v[96, :, :8] = I["L0_xattn_bv"].reshape(16, 8)
    v[96, :, 8] = 1
    put(w, WX, "v", v.reshape(97, 144))
    put(w, WX, "o", I["L0_xattn_wo"])
    put(w, WX, "bq0", rep(I["L0_xattn_bq"][None]).T)
    put(w, WX, "bq", I["L0_xattn_bq"][:, None])
    w[:, WX["bo"][0]:WX["bo"][1]] = I["L0_xattn_bo"][None]

    w = A["wf0"] = z(128, NWF0)
    put(w, WF0, "rw1", I["L0_ffn_rw1"])
    put(w, WF0, "rb1", I["L0_ffn_rb1"].reshape(4, 128).T)
    v = z(128, 4, 32)
    v[:, :, :8] = I["L0_ffn_rw2"].reshape(4, 128, 8).transpose(1, 0, 2)
    put(w, WF0, "rw2", v.reshape(128, 128))
    w[:, WF0["rb2"][0]:WF0["rb2"][1]] = I["L0_ffn_rb2"][None]
    put(w, WF0, "b1", I["L0_ffn_b1"].reshape(8, 4, 128).transpose(2, 0, 1).reshape(128, 32))
    put(w, WF0, "b2", I["L0_ffn_b2"])
    A["f0w1"] = I["L0_ffn_W1"].transpose(1, 0, 2).reshape(128, 4096)
    A["f0w2"] = I["L0_ffn_W2"].reshape(8, 4, 128, 128).transpose(2, 0, 1, 3).reshape(128, 4096)

    w = A["wb"] = z(128, NWB)
    h = np.arange(16)[:, None] * 16 + np.arange(8)[None]
    perm = np.concatenate([h, h + 8]).reshape(-1)
    put(w, WB, "q", I["L1_attn_Wq"])
    put(w, WB, "down", I["L1_attn_Wdown"])
    put(w, WB, "up", I["L1_attn_Wup"][:, perm])
    put(w, WB, "out", I["L1_attn_Wout"])
    w[:, WB["bq"][0]:WB["bq"][1]] = I["L1_attn_bq"][None]
    w[32, WB["up"][0]:WB["up"][1]] = I["L1_attn_bup"][perm]
    w[:, WB["bout"][0]:WB["bout"][1]] = I["L1_attn_bout"][None]
    put(w, WB, "bdown", I["L1_attn_bdown"][:, None])

    w = A["wy"] = z(128, NWY)
    put(w, WY, "q", I["L1_xattn_w_q"])
    put(w, WY, "kv", I["L1_xattn_w_kv"])
    put(w, WY, "out", I["L1_xattn_w_out"].reshape(8, 128, 128).transpose(1, 0, 2).reshape(128, 1024))
    w[:, WY["b"][0]:WY["b"][1]] = I["L1_xattn_b_out"][None]

    w = A["wf1"] = z(128, NWF1)
    put(w, WF1, "g", I["L1_ffn_Wg"])
    w[:, WF1["bg"][0]:WF1["bg"][1]] = I["L1_ffn_bg"][None]
    w = A["f1w"] = z(8, 128, 3, 512)
    w[:, :, 0] = I["L1_ffn_W1"]
    w[:, :, 1] = I["L1_ffn_W3"]
    w[:, :, 2] = I["L1_ffn_W2"].reshape(8, 4, 128, 128).transpose(0, 2, 1, 3).reshape(8, 128, 512)

    g = A["ga"] = z(16, 128, 25)
    for k, n in enumerate("qkv"):
        g[:, :, 8 * k:8 * k + 8] = I["L0_attn_w_" + n].reshape(16, 8, 128).transpose(0, 2, 1)
    g = A["gx"] = z(16, 128, 25)
    g[:, :, :8] = I["L0_xattn_wq"].reshape(128, 16, 8).transpose(1, 0, 2)
    for k, n in enumerate("kv"):
        g[:, :96, 8 + 8 * k:16 + 8 * k] = I["L0_xattn_w" + n].reshape(96, 16, 8).transpose(1, 0, 2)
        g[:, 96, 8 + 8 * k:16 + 8 * k] = I["L0_xattn_b" + n].reshape(16, 8)
    g[:, :8, 24] = I["L0_xattn_bq"].reshape(16, 8)
    g = A["gy"] = z(16, 128, 321)
    g[:, :, :64] = I["L1_xattn_w_q"].reshape(128, 16, 64).transpose(1, 0, 2)
    kv = I["L1_xattn_w_kv"].reshape(96, 2, 16, 64)
    for k in range(2):
        g[:, :96, 64 + 64 * k:128 + 64 * k] = kv[:, k].transpose(1, 0, 2)
    g[:, :64, 193:] = I["L1_xattn_w_out"].reshape(16, 64, 128)
    return A


_OUT = (1, 1024, 128)


def kernel(**inputs):
    import concourse.bacc as bacc
    from concourse.bass_utils import run_bass_kernel_spmd

    nc = bacc.Bacc("TRN2", target_bir_lowering=False, num_devices=1)
    arrays, args = {}, {}
    for name, a in layout({k: np.asarray(v) for k, v in inputs.items()}).items():
        a = np.ascontiguousarray(a)
        arrays["in_" + name] = a
        args[name] = nc.dram_tensor("in_" + name, a.shape, mybir.dt.from_np(a.dtype), kind="ExternalInput").ap()
    out = nc.dram_tensor("out_0", _OUT, F32, kind="ExternalOutput").ap()
    program(nc, out, **args)
    r = run_bass_kernel_spmd(nc, [arrays], core_ids=[0])
    return r.results[0]["out_0"]
```
